# Optimizing a Trainium2 kernel written in Bass

```python
import numpy as np
import jax
import jax.numpy as jnp

def _softmax(x, axis=-1):
    return jax.nn.softmax(x, axis=axis)

def _gelu(x):
    return jax.nn.gelu(x, approximate=True)

def _silu(x):
    return jax.nn.silu(x)

def _sigmoid(x):
    return jax.nn.sigmoid(x)

def _layernorm(x, axis=-1, eps=1e-05):
    m = jnp.mean(x, axis=axis, keepdims=True)
    v = jnp.var(x, axis=axis, keepdims=True)
    return (x - m) / jnp.sqrt(v + eps)

def _scatter_add(tgt, idx, src, axis=0):
    return tgt.at[idx].add(src)

def _segment_sum(src, seg, n):
    return jax.ops.segment_sum(src, seg, n)
kernel_name = 'mk_conv_seq_d4_conv_nchw512_r2_d8dd5d'

def setup_inputs(seed: int=0):
    np.random.seed(seed)
    _w = jnp.asarray

    def _rec_inputs():
        import jax
        import jax.numpy as jnp
        _gk = jax.random.key(seed)
        x = -0.000125 + 0.9999 * jax.random.normal(jax.random.fold_in(_gk, 1), (16, 256, 32, 32), jnp.float32)
        return x
    x = _rec_inputs()

    def _L0_conv_setup():
        import jax, jax.numpy as jnp
        import numpy as np
        EPS = 1e-05

        def _conv1x1(x, W, b):
            return jnp.einsum('bchw,oc->bohw', x, W) + b[None, :, None, None]
        key = jax.random.key(seed)
        ks = jax.random.split(key, 13)
        B, C, M, N = (16, 256, 32, 32)
        CR = C // 2
        s = 0.02
        return {'x': jax.random.normal(ks[0], (B, C, M, N), dtype=jnp.float32), 'Wq': jax.random.normal(ks[1], (CR, C), dtype=jnp.float32) * s, 'bq': jax.random.normal(ks[2], (CR,), dtype=jnp.float32) * s, 'Wk': jax.random.normal(ks[3], (CR, C), dtype=jnp.float32) * s, 'bk': jax.random.normal(ks[4], (CR,), dtype=jnp.float32) * s, 'Wv': jax.random.normal(ks[5], (CR, C), dtype=jnp.float32) * s, 'bv': jax.random.normal(ks[6], (CR,), dtype=jnp.float32) * s, 'Wr': jax.random.normal(ks[7], (C, CR), dtype=jnp.float32) * s, 'br': jax.random.normal(ks[8], (C,), dtype=jnp.float32) * s, 'gamma': jax.random.normal(ks[9], (C,), dtype=jnp.float32) * 0.1 + 1.0, 'beta': jax.random.normal(ks[10], (C,), dtype=jnp.float32) * 0.1, 'running_mean': jax.random.normal(ks[11], (C,), dtype=jnp.float32) * 0.1, 'running_var': jax.random.uniform(ks[12], (C,), dtype=jnp.float32, minval=0.5, maxval=1.5)}
    _L0_conv_all = _L0_conv_setup()
    _L0_conv_in = {k: v for k, v in _L0_conv_all.items() if k in ('Wq', 'bq', 'Wk', 'bk', 'Wv', 'bv', 'Wr', 'br', 'gamma', 'beta', 'running_mean', 'running_var')}
    del _L0_conv_all

    def _L1_conv_setup():
        import jax, jax.numpy as jnp
        import numpy as np
        NUM_HEADS = 8
        NUM_GROUPS = 32
        EPS = 1e-05

        def group_norm(x, scale, bias):
            b, c, t = x.shape
            xg = x.reshape(b, NUM_GROUPS, c // NUM_GROUPS, t)
            mean = xg.mean(axis=(2, 3), keepdims=True)
            var = xg.var(axis=(2, 3), keepdims=True)
            xn = ((xg - mean) * jax.lax.rsqrt(var + EPS)).reshape(b, c, t)
            return xn * scale[None, :, None] + bias[None, :, None]
        key = jax.random.key(seed)
        ks = jax.random.split(key, 3)
        b, c, h, w = (16, 256, 32, 32)
        x = jax.random.normal(ks[0], (b, c, h, w), dtype=jnp.float32)
        gn_scale = jnp.ones((c,), jnp.float32)
        gn_bias = jnp.zeros((c,), jnp.float32)
        w_qkv = jax.random.normal(ks[1], (3 * c, c), jnp.float32) * c ** (-0.5)
        b_qkv = jnp.zeros((3 * c,), jnp.float32)
        w_proj = jax.random.normal(ks[2], (c, c), jnp.float32) * c ** (-0.5)
        b_proj = jnp.zeros((c,), jnp.float32)
        return {'x': x, 'gn_scale': gn_scale, 'gn_bias': gn_bias, 'w_qkv': w_qkv, 'b_qkv': b_qkv, 'w_proj': w_proj, 'b_proj': b_proj}
    _L1_conv_all = _L1_conv_setup()
    _L1_conv_in = {k: v for k, v in _L1_conv_all.items() if k in ('gn_scale', 'gn_bias', 'w_qkv', 'b_qkv', 'w_proj', 'b_proj')}
    del _L1_conv_all

    def _L2_conv_setup():
        import jax, jax.numpy as jnp
        import numpy as np
        B, C, H, W = (16, 256, 32, 32)
        GROUPS = 16
        EPS = 1e-05

        def group_norm(x, w, b):
            Bx, Cx, Hx, Wx = x.shape
            xg = x.reshape(Bx, GROUPS, Cx // GROUPS, Hx, Wx)
            mu = jnp.mean(xg, axis=(2, 3, 4), keepdims=True)
            var = jnp.var(xg, axis=(2, 3, 4), keepdims=True)
            xg = (xg - mu) * jax.lax.rsqrt(var + EPS)
            x = xg.reshape(Bx, Cx, Hx, Wx)
            return x * w[None, :, None, None] + b[None, :, None, None]
        key = jax.random.key(seed)
        ks = jax.random.split(key, 6)
        x = jax.random.normal(ks[0], (B, C, H, W), dtype=jnp.float32)
        norm1_w = jnp.ones((C,), jnp.float32)
        norm1_b = jnp.zeros((C,), jnp.float32)
        kv_w = jax.random.normal(ks[1], (2 * C, C), dtype=jnp.float32) * (1.0 / np.sqrt(C))
        kv_b = jax.random.normal(ks[2], (2 * C,), dtype=jnp.float32) * 0.01
        norm2_w = jnp.ones((C,), jnp.float32)
        norm2_b = jnp.zeros((C,), jnp.float32)
        out_w = jax.random.normal(ks[3], (C, C), dtype=jnp.float32) * (1.0 / np.sqrt(C))
        out_b = jax.random.normal(ks[4], (C,), dtype=jnp.float32) * 0.01
        return {'x': x, 'norm1_w': norm1_w, 'norm1_b': norm1_b, 'kv_w': kv_w, 'kv_b': kv_b, 'norm2_w': norm2_w, 'norm2_b': norm2_b, 'out_w': out_w, 'out_b': out_b}
    _L2_conv_all = _L2_conv_setup()
    _L2_conv_in = {k: v for k, v in _L2_conv_all.items() if k in ('norm1_w', 'norm1_b', 'kv_w', 'kv_b', 'norm2_w', 'norm2_b', 'out_w', 'out_b')}
    del _L2_conv_all

    def _L3_conv_setup():
        import jax, jax.numpy as jnp
        import numpy as np
        UP = 2
        DOWN = 2
        NEG_SLOPE = 0.2
        MARGIN = 10
        FLRELU_SCALE = np.float32(2.0 ** 0.5)
        UP_PAD = ((10 + 1) // 2 + UP - 1, 10 // 2)
        DOWN_PAD = ((10 + 1) // 2, 10 // 2)
        _FILT = np.array([0.0, 0.00398, -0.01884, -0.05155, 0.12443, 0.44197, 0.44197, 0.12443, -0.05155, -0.01884, 0.00398, 0.0], dtype=np.float32)
        _FILT = _FILT / _FILT.sum()

        def _fir1d(x, k, up, down, pad0, pad1, axis):
            N, C, H, W = x.shape
            xr = x.reshape(N * C, 1, H, W)
            K = k.shape[0]
            kf = k[::-1].astype(x.dtype)
            if axis == 3:
                w = kf.reshape(1, 1, 1, K)
                lhs_dil = (1, up)
                strides = (1, down)
                padding = ((0, 0), (pad0, pad1 + up - 1))
            else:
                w = kf.reshape(1, 1, K, 1)
                lhs_dil = (up, 1)
                strides = (down, 1)
                padding = ((pad0, pad1 + up - 1), (0, 0))
            y = jax.lax.conv_general_dilated(xr, w, window_strides=strides, padding=padding, lhs_dilation=lhs_dil, dimension_numbers=('NCHW', 'OIHW', 'NCHW'))
            return y.reshape(N, C, y.shape[2], y.shape[3])

        def _sep_upfirdn(x, k, up, down, pad):
            x = _fir1d(x, k, up, down, pad[0], pad[1], axis=3)
            x = _fir1d(x, k, up, down, pad[0], pad[1], axis=2)
            return x
        key = jax.random.key(seed)
        k_in = jax.random.fold_in(key, 0)
        return {'input': jax.random.normal(k_in, (8, 256, 32, 32), dtype=jnp.float32), 'bias': jnp.zeros((256,), dtype=jnp.float32), 'up_filter': jnp.asarray(_FILT), 'down_filter': jnp.asarray(_FILT)}
    _L3_conv_all = _L3_conv_setup()
    _L3_conv_in = {k: v for k, v in _L3_conv_all.items() if k in ('bias', 'up_filter', 'down_filter')}
    del _L3_conv_all
    return {'x': x, 'L0_conv_Wq': _L0_conv_in['Wq'], 'L0_conv_bq': _L0_conv_in['bq'], 'L0_conv_Wk': _L0_conv_in['Wk'], 'L0_conv_bk': _L0_conv_in['bk'], 'L0_conv_Wv': _L0_conv_in['Wv'], 'L0_conv_bv': _L0_conv_in['bv'], 'L0_conv_Wr': _L0_conv_in['Wr'], 'L0_conv_br': _L0_conv_in['br'], 'L0_conv_gamma': _L0_conv_in['gamma'], 'L0_conv_beta': _L0_conv_in['beta'], 'L0_conv_running_mean': _L0_conv_in['running_mean'], 'L0_conv_running_var': _L0_conv_in['running_var'], 'L1_conv_gn_scale': _L1_conv_in['gn_scale'], 'L1_conv_gn_bias': _L1_conv_in['gn_bias'], 'L1_conv_w_qkv': _L1_conv_in['w_qkv'], 'L1_conv_b_qkv': _L1_conv_in['b_qkv'], 'L1_conv_w_proj': _L1_conv_in['w_proj'], 'L1_conv_b_proj': _L1_conv_in['b_proj'], 'L2_conv_norm1_w': _L2_conv_in['norm1_w'], 'L2_conv_norm1_b': _L2_conv_in['norm1_b'], 'L2_conv_kv_w': _L2_conv_in['kv_w'], 'L2_conv_kv_b': _L2_conv_in['kv_b'], 'L2_conv_norm2_w': _L2_conv_in['norm2_w'], 'L2_conv_norm2_b': _L2_conv_in['norm2_b'], 'L2_conv_out_w': _L2_conv_in['out_w'], 'L2_conv_out_b': _L2_conv_in['out_b'], 'L3_conv_bias': _L3_conv_in['bias'], 'L3_conv_up_filter': _L3_conv_in['up_filter'], 'L3_conv_down_filter': _L3_conv_in['down_filter']}

def reference(x, L0_conv_Wq, L0_conv_bq, L0_conv_Wk, L0_conv_bk, L0_conv_Wv, L0_conv_bv, L0_conv_Wr, L0_conv_br, L0_conv_gamma, L0_conv_beta, L0_conv_running_mean, L0_conv_running_var, L1_conv_gn_scale, L1_conv_gn_bias, L1_conv_w_qkv, L1_conv_b_qkv, L1_conv_w_proj, L1_conv_b_proj, L2_conv_norm1_w, L2_conv_norm1_b, L2_conv_kv_w, L2_conv_kv_b, L2_conv_norm2_w, L2_conv_norm2_b, L2_conv_out_w, L2_conv_out_b, L3_conv_bias, L3_conv_up_filter, L3_conv_down_filter):
    import jax
    import jax.numpy as jnp

    def _L0_conv_ref(x, Wq, bq, Wk, bk, Wv, bv, Wr, br, gamma, beta, running_mean, running_var):
        import jax, jax.numpy as jnp
        import numpy as np
        EPS = 1e-05

        def _conv1x1(x, W, b):
            return jnp.einsum('bchw,oc->bohw', x, W) + b[None, :, None, None]
        b, c, m, n = x.shape
        cr = Wq.shape[0]
        Q = _conv1x1(x, Wq, bq).reshape(b * cr, m, n)
        K = _conv1x1(x, Wk, bk).reshape(b * cr, m, n)
        V = _conv1x1(x, Wv, bv).reshape(b * cr, m, n)
        corr = jnp.einsum('gik,gjk->gij', Q, K)
        attn = jax.nn.softmax(corr, axis=-1)
        y = jnp.einsum('gij,gjn->gin', attn, V).reshape(b, cr, m, n)
        y = _conv1x1(y, Wr, br)
        inv = gamma / jnp.sqrt(running_var + EPS)
        y = y * inv[None, :, None, None] + (beta - running_mean * inv)[None, :, None, None]
        return y + x

    def _L1_conv_ref(x, gn_scale, gn_bias, w_qkv, b_qkv, w_proj, b_proj):
        import jax, jax.numpy as jnp
        import numpy as np
        NUM_HEADS = 8
        NUM_GROUPS = 32
        EPS = 1e-05

        def group_norm(x, scale, bias):
            b, c, t = x.shape
            xg = x.reshape(b, NUM_GROUPS, c // NUM_GROUPS, t)
            mean = xg.mean(axis=(2, 3), keepdims=True)
            var = xg.var(axis=(2, 3), keepdims=True)
            xn = ((xg - mean) * jax.lax.rsqrt(var + EPS)).reshape(b, c, t)
            return xn * scale[None, :, None] + bias[None, :, None]
        b, c, h, w = x.shape
        t = h * w
        xf = x.reshape(b, c, t)
        xn = group_norm(xf, gn_scale, gn_bias)
        qkv = jnp.einsum('oc,bct->bot', w_qkv, xn) + b_qkv[None, :, None]
        dh = c // NUM_HEADS
        qkv = qkv.reshape(b * NUM_HEADS, 3 * dh, t)
        q, k, v = jnp.split(qkv, 3, axis=1)
        scale = dh ** (-0.25)
        logits = jnp.einsum('bct,bcs->bts', q * scale, k * scale)
        weight = jax.nn.softmax(logits.astype(jnp.float32), axis=-1).astype(logits.dtype)
        attn = jnp.einsum('bts,bcs->bct', weight, v)
        attn = attn.reshape(b, c, t)
        out = jnp.einsum('oc,bct->bot', w_proj, attn) + b_proj[None, :, None]
        return (xf + out).reshape(b, c, h, w)

    def _L2_conv_ref(x, norm1_w, norm1_b, kv_w, kv_b, norm2_w, norm2_b, out_w, out_b):
        import jax, jax.numpy as jnp
        import numpy as np
        B, C, H, W = (16, 256, 32, 32)
        GROUPS = 16
        EPS = 1e-05

        def group_norm(x, w, b):
            Bx, Cx, Hx, Wx = x.shape
            xg = x.reshape(Bx, GROUPS, Cx // GROUPS, Hx, Wx)
            mu = jnp.mean(xg, axis=(2, 3, 4), keepdims=True)
            var = jnp.var(xg, axis=(2, 3, 4), keepdims=True)
            xg = (xg - mu) * jax.lax.rsqrt(var + EPS)
            x = xg.reshape(Bx, Cx, Hx, Wx)
            return x * w[None, :, None, None] + b[None, :, None, None]
        Bx, Cx, Hx, Wx = x.shape
        n = Hx * Wx
        xn = group_norm(x, norm1_w, norm1_b)
        q_scale = Cx ** (-0.5)
        kv = jnp.einsum('bchw,oc->bohw', xn, kv_w) + kv_b[None, :, None, None]
        k4, v4 = jnp.split(kv, 2, axis=1)
        k = k4.reshape(Bx, Cx, n)
        v = v4.reshape(Bx, Cx, n)
        q = jax.nn.softmax(k, axis=1) * q_scale
        k = jax.nn.softmax(k, axis=2)
        context = jnp.einsum('bdn,ben->bde', k, v)
        out = jnp.einsum('bde,bdn->ben', context, q)
        out = out.reshape(Bx, Cx, Hx, Wx)
        out = group_norm(out, norm2_w, norm2_b)
        out = jax.nn.gelu(out, approximate=False)
        out = jnp.einsum('bchw,oc->bohw', out, out_w) + out_b[None, :, None, None]
        return xn + out

    def _L3_conv_ref(input, bias, up_filter, down_filter):
        import jax, jax.numpy as jnp
        import numpy as np
        UP = 2
        DOWN = 2
        NEG_SLOPE = 0.2
        MARGIN = 10
        FLRELU_SCALE = np.float32(2.0 ** 0.5)
        UP_PAD = ((10 + 1) // 2 + UP - 1, 10 // 2)
        DOWN_PAD = ((10 + 1) // 2, 10 // 2)
        _FILT = np.array([0.0, 0.00398, -0.01884, -0.05155, 0.12443, 0.44197, 0.44197, 0.12443, -0.05155, -0.01884, 0.00398, 0.0], dtype=np.float32)
        _FILT = _FILT / _FILT.sum()

        def _fir1d(x, k, up, down, pad0, pad1, axis):
            N, C, H, W = x.shape
            xr = x.reshape(N * C, 1, H, W)
            K = k.shape[0]
            kf = k[::-1].astype(x.dtype)
            if axis == 3:
                w = kf.reshape(1, 1, 1, K)
                lhs_dil = (1, up)
                strides = (1, down)
                padding = ((0, 0), (pad0, pad1 + up - 1))
            else:
                w = kf.reshape(1, 1, K, 1)
                lhs_dil = (up, 1)
                strides = (down, 1)
                padding = ((pad0, pad1 + up - 1), (0, 0))
            y = jax.lax.conv_general_dilated(xr, w, window_strides=strides, padding=padding, lhs_dilation=lhs_dil, dimension_numbers=('NCHW', 'OIHW', 'NCHW'))
            return y.reshape(N, C, y.shape[2], y.shape[3])

        def _sep_upfirdn(x, k, up, down, pad):
            x = _fir1d(x, k, up, down, pad[0], pad[1], axis=3)
            x = _fir1d(x, k, up, down, pad[0], pad[1], axis=2)
            return x
        out = input + bias[None, :, None, None]
        upf = up_filter * UP
        out = _sep_upfirdn(out, upf, UP, 1, UP_PAD)
        out = jax.nn.leaky_relu(out, NEG_SLOPE) * FLRELU_SCALE
        out = _sep_upfirdn(out, down_filter, 1, DOWN, DOWN_PAD)
        m = (MARGIN * UP - MARGIN * DOWN) // 2
        if m > 0:
            out = out[:, :, m:-m, m:-m]
        return out

    def _gn(v, G=32, eps=1e-05):
        B_, C_, H_, W_ = v.shape
        g = v.reshape(B_, G, C_ // G, H_, W_)
        m = jnp.mean(g, axis=(2, 3, 4), keepdims=True)
        s = jnp.var(g, axis=(2, 3, 4), keepdims=True)
        return ((g - m) / jnp.sqrt(s + eps)).reshape(v.shape)

    def _ln_c(v, eps=1e-06):
        m = jnp.mean(v, axis=1, keepdims=True)
        s = jnp.var(v, axis=1, keepdims=True)
        return (v - m) / jnp.sqrt(s + eps)

    def _ln_t(v, eps=1e-05):
        m = jnp.mean(v, axis=-1, keepdims=True)
        s = jnp.var(v, axis=-1, keepdims=True)
        return (v - m) / jnp.sqrt(s + eps)

    def _to_tokens(v):
        B_, C_, H_, W_ = v.shape
        return v.reshape(B_, C_, H_ * W_).transpose(0, 2, 1)

    def _from_tokens(t, like):
        B_, C_, H_, W_ = like.shape
        return t.transpose(0, 2, 1).reshape(B_, C_, H_, W_)
    x = _L0_conv_ref(x, L0_conv_Wq, L0_conv_bq, L0_conv_Wk, L0_conv_bk, L0_conv_Wv, L0_conv_bv, L0_conv_Wr, L0_conv_br, L0_conv_gamma, L0_conv_beta, L0_conv_running_mean, L0_conv_running_var)
    x = _L1_conv_ref(x, L1_conv_gn_scale, L1_conv_gn_bias, L1_conv_w_qkv, L1_conv_b_qkv, L1_conv_w_proj, L1_conv_b_proj)
    x = _L2_conv_ref(x, L2_conv_norm1_w, L2_conv_norm1_b, L2_conv_kv_w, L2_conv_kv_b, L2_conv_norm2_w, L2_conv_norm2_b, L2_conv_out_w, L2_conv_out_b)
    x = _L3_conv_ref(x, L3_conv_bias, L3_conv_up_filter, L3_conv_down_filter)
    return x

_drawn_inputs = setup_inputs


def setup_inputs(seed=0):
    import zlib

    import numpy as np

    out = dict(_drawn_inputs(seed))
    spreads = {'L1_conv_gn_scale': (1.0, 0.2),
     'L1_conv_gn_bias': (0.0, 0.1),
     'L1_conv_b_qkv': (0.0, 0.1),
     'L1_conv_b_proj': (0.0, 0.1),
     'L2_conv_norm1_w': (1.0, 0.2),
     'L2_conv_norm1_b': (0.0, 0.1),
     'L2_conv_norm2_w': (1.0, 0.2),
     'L2_conv_norm2_b': (0.0, 0.1),
     'L3_conv_bias': (0.0, 0.1)}
    factors = {'L0_conv_Wq': 8.0,
     'L0_conv_bq': 8.0,
     'L0_conv_Wk': 8.0,
     'L0_conv_bk': 8.0,
     'L0_conv_Wv': 4.078,
     'L0_conv_bv': 3.453,
     'L2_conv_out_b': 6.242}
    for name, (base, spread) in spreads.items():
        noise = np.random.default_rng([zlib.crc32(name.encode()), seed]).standard_normal(out[name].shape)
        drawn = base * np.exp(spread * noise) if base else spread * noise
        out[name] = jnp.asarray(drawn.astype(out[name].dtype))
    for name, factor in factors.items():
        out[name] = (out[name] * factor).astype(out[name].dtype)
    return out
```

```python
from contextlib import ExitStack

import concourse.bass as bass
from concourse import mybir

ALU = mybir.AluOpType
ACT = mybir.ActivationFunctionType
AX_X = mybir.AxisListType.X
F32 = mybir.dt.float32
F32R = mybir.dt.float32r

B, C, H, W = 16, 256, 32, 32
P = 128
CT = C // P
N = H * W
HALF = N // 2
NT = N // P
CR = C // 2
Q4 = 4
HEADS, DH = 8, 32
GROUPS4 = HEADS // Q4
UNITS = GROUPS4 * 2
STACK = 3 * DH
EPS = 1e-5
UPH = 2 * H
UPT = UPH // 2
TAPS = 12
REACH = 3
WIN = 2 * REACH + 1
ROOT2 = float(2.0 ** 0.5)
SLOPE = 0.2

VEC = {}
for _name, _n in (("bq", 1), ("bk", 1), ("bv", 1), ("br", CT), ("gamma", CT), ("beta", CT), ("mean", CT), ("var", CT),
                  ("gn1_scale", CT), ("gn1_bias", CT), ("b_qk", 2 * GROUPS4), ("b_proj", CT),
                  ("gn2_scale", CT), ("gn2_bias", CT), ("gn3_scale", CT), ("gn3_bias", CT)):
    VEC[_name] = (sum(n for _, n in VEC.values()), _n)
NVEC = sum(n for _, n in VEC.values())


START = 1


class Signal:

    def __init__(self, sem, per_image, size=1):
        self.sem, self.per_image, self.size = sem, per_image, size

    def __call__(self, b, k):
        return b * (self.per_image * self.size) + (k * self.size + START)


def chain_kernel(nc, x, weights, vectors, rows, filters, consts, out):
    with ExitStack() as ctx:
        def sb(name, shape, dt=F32, over=None):
            return (over or ctx).enter_context(nc.sbuf_tensor(name, shape, dt))

        looped = []

        def signal(name, per_image, size=1):
            made = Signal(ctx.enter_context(nc.semaphore(name)), per_image, size)
            if per_image:
                looped.append(made)
            return made

        ps = ctx.enter_context(nc.psum_tensor("ps", [P, 8, HALF], F32))

        wq0 = sb("wq0", [P, CT, 3 * CR])
        wr0 = sb("wr0", [P, C])
        wqk1 = sb("wqk1", [P, CT, 4 * P])
        wv1 = sb("wv1", [P, CT, C])
        wp1 = sb("wp1", [P, CT, C])
        wkv2 = sb("wkv2", [P, CT, 2 * C])
        wo2 = sb("wo2", [P, CT, C])
        vec = sb("vec", [P, NVEC])
        rowc = sb("rowc", [P, 5 * C])
        ident = sb("ident", [P, P])
        avg8 = sb("avg8", [P, P])
        avg16 = sb("avg16", [P, P])
        up_h = sb("up_h", [P, 4 * 3 * 2])
        up_w = sb("up_w", [P, UPH])
        dn_h = sb("dn_h", [P, WIN])
        dn_w = sb("dn_w", [P, W])
        up_m = sb("up_m", [P, 4 * 3, P])
        dn_m = sb("dn_m", [P, WIN * W])
        inv0 = sb("inv0", [P, CT])
        add0 = sb("add0", [P, CT])
        minus_half = sb("minus_half", [P, CT])
        b_z = sb("b_z", [P, C])

        x0 = sb("x0", [P, CT, N])
        x1 = sb("x1", [P, CT, N])
        x2 = sb("x2", [P, CT, N])
        xn2 = sb("xn2", [P, CT, N])
        ks = sb("ks", [P, HEADS, N], F32R)
        vo = sb("vo", [P, NT, HEADS, 2 * DH])
        spare = sb("spare", [P, 1])
        st6 = sb("st6", [P, CT, 2, 6])
        mv = sb("mv", [P, CT, 2])
        sq = sb("sq", [P, CT])
        gm = sb("gm", [P, CT, 2])
        gsq = sb("gsq", [P, CT])
        gve = sb("gve", [P, CT])
        rstd = sb("rstd", [P, CT])
        ga = sb("ga", [P, CT])
        gma = sb("gma", [P, CT])
        gb = sb("gb", [P, CT])
        with ExitStack() as own:
            qkv0 = sb("qkv0", [P, 3, N], over=own)
            qT0 = sb("qT0", [P, H, 32], over=own)
            kT0 = sb("kT0", [P, H, 32], over=own)
            vT0 = sb("vT0", [P, W, 32], over=own)
            e0 = sb("e0", [P, 32, 32], over=own)
            pT0 = sb("pT0", [P, 32, 32], over=own)
            y0 = sb("y0", [P, 32, 32], over=own)
            yc0 = sb("yc0", [P, H, W], over=own)
            mx0 = sb("mx0", [P, 32], over=own)
            sum0 = sb("sum0", [P, 32], over=own)
        with ExitStack() as own:
            xn1 = sb("xn1", [P, CT, N], over=own)
            hi1 = sb("hi1", [P, 4, N], F32R, over=own)
            lo1 = sb("lo1", [P, 4, N], F32R, over=own)
            qs = sb("qs", [P, HEADS, N], F32R, over=own)
            mxp = sb("mxp", [P, Q4, 4, 2], over=own)
            mxr = sb("mxr", [P, Q4, 4], over=own)
            prob = sb("prob", [P, 2, Q4, HALF], over=own)
            rec1 = sb("rec1", [DH, 2, HALF], over=own)
        with ExitStack() as own:
            kv = sb("kv", [P, NT, 2 * C + 1], over=own)
            rmx = sb("rmx", [P, NT], over=own)
            qe = sb("qe", [P, NT, C], over=own)
            qsum = sb("qsum", [P, NT], over=own)
            qrec = sb("qrec", [P, NT], over=own)
            cmx = sb("cmx", [P, C], over=own)
            cmc = sb("cmc", [P, CT], over=own)
            cmb = sb("cmb", [P, C], over=own)
            ke = sb("ke", [P, NT, C], over=own)
            qc = sb("qc", [P, CT, N], over=own)
            crec = sb("crec", [P, CT], over=own)
            ctx2 = sb("ctx2", [P, CT, C], over=own)
            o2 = sb("o2", [P, CT, N], over=own)
            g2 = o2
            z3 = x1[:, :, :].rearrange("p c n -> p (c n)").rearrange("p (t c) -> p t c", c=C)
            rl3 = sb("rl3", [P, 2, 2 * C], over=own)
            up3 = sb("up3", [P, UPT, C], over=own)
            o3 = o2
        att1 = xn2
        r0 = x2

        def v(name, i=0):
            at = VEC[name][0]
            return vec[:, at + i:at + i + 1]

        def vv(name):
            at, n = VEC[name]
            return vec[:, at:at + n]

        consts_in = signal("consts_in", 0)
        prep_v = signal("prep_v", 0)
        prep_p = signal("prep_p", 0)
        x_in = signal("x_in", 2, 16)
        qkv0_mm = signal("qkv0_mm", 3)
        qkv0_sb = signal("qkv0_sb", 3)
        tr0 = signal("tr0", 3)
        corr0 = signal("corr0", 1)
        dve0 = signal("dve0", 6)
        exp0 = signal("exp0", 1)
        pT0_ok = signal("pT0_ok", 1)
        av0 = signal("av0", 1)
        wr_mm = signal("wr_mm", 2)
        r0_ok = signal("r0_ok", 2)
        x1_ok = signal("x1_ok", 2)
        gn_v = signal("gn_v", 3 * 11)
        gn_mm = signal("gn_mm", 3)
        gn_p = signal("gn_p", 3)
        xn1_ok = signal("xn1_ok", 2)
        qk1_mm = signal("qk1_mm", 4)
        hi1_ok = signal("hi1_ok", 4)
        lo1_ok = signal("lo1_ok", 4)
        stack_ok = [signal(f"stack_ok{g}", 6 * Q4, 16) for g in range(GROUPS4)]
        v1_mm = signal("v1_mm", 4)
        v1_ok = signal("v1_ok", 4)
        max_mm = signal("max_mm", UNITS * 32)
        max_ok = signal("max_ok", UNITS * 32)
        mxr_ok = signal("mxr_ok", UNITS)
        row_mm = signal("row_mm", UNITS * Q4)
        row_ok = signal("row_ok", UNITS * Q4)
        s_mm = signal("s_mm", UNITS * NT * 2)
        p_ok = signal("p_ok", UNITS * NT * 2)
        av_mm = signal("av_mm", UNITS * NT)
        rec_ok = signal("rec_ok", UNITS * Q4)
        att_ok = signal("att_ok", UNITS * Q4)
        proj_mm = signal("proj_mm", 2)
        x2_ok = signal("x2_ok", 2)
        xn2_ok = signal("xn2_ok", 2)
        kv_mm = signal("kv_mm", NT)
        kv_ok = signal("kv_ok", NT)
        rmx_ok = signal("rmx_ok", 1)
        qe_ok = signal("qe_ok", NT)
        qrec_ok = signal("qrec_ok", 1)
        qn_ok = signal("qn_ok", NT)
        cmx_ok = signal("cmx_ok", 1)
        cmt_mm = signal("cmt_mm", 1)
        cmc_ok = signal("cmc_ok", 1)
        cmb_mm = signal("cmb_mm", 1)
        cmb_ok = signal("cmb_ok", 1)
        ks_ok = signal("ks_ok", 1)
        ke_ok = signal("ke_ok", 1)
        qt_mm = signal("qt_mm", 4)
        qc_ok = signal("qc_ok", 4)
        ctx_mm = signal("ctx_mm", CT)
        crec_ok = signal("crec_ok", CT)
        ctx_ok = signal("ctx_ok", CT)
        o2_mm = signal("o2_mm", 2)
        o2_ok = signal("o2_ok", 2)
        g2_ok = signal("g2_ok", 2)
        z_mm = signal("z_mm", 4)
        z_ok = signal("z_ok", 4)
        up_mm = signal("up_mm", UPT // 2)
        relu_ok = signal("relu_ok", UPT // 2)
        up_ok = signal("up_ok", UPT // 2)
        dn_mm = signal("dn_mm", 2)
        o3_ok = signal("o3_ok", 2)
        stored = signal("stored", 2, 16)

        def gn_ps(n):
            return ps[:, (6, 4, 4)[n], 0:2 * CT].rearrange("p (c s) -> p c s", s=2)

        loads = [(wq0, weights["wq0"]), (wr0, weights["wr0"]), (wqk1, weights["wqk1"]), (wv1, weights["wv1"]),
                 (wp1, weights["wp1"]), (wkv2, weights["wkv2"]), (wo2, weights["wo2"]), (vec, vectors),
                 (rowc, rows), (ident, consts["ident"]), (avg8, consts["avg8"]), (avg16, consts["avg16"]),
                 (up_h, filters["up_h"]), (up_w, filters["up_w"]), (dn_h, filters["dn_h"]), (dn_w, filters["dn_w"])]
        PREP_V = 27
        PREP_P = 5

        block = ctx.enter_context(nc.Block())

        @block.sync
        def _(sp):
            for made in looped:
                sp.sem_inc(made.sem, START)
            for dst, src in loads:
                sp.dma_start(dst[tuple(slice(None) for _ in dst.shape)], src).then_inc(consts_in.sem, 16)
            with sp.Fori(0, B) as b:
                sp.wait_ge(x1_ok.sem, x1_ok(b, 0))
                for ct in range(CT):
                    sp.dma_start(x0[:, ct, :], x[b, ct * P:(ct + 1) * P, :]).then_inc(x_in.sem, 16)
                for g in range(GROUPS4):
                    if g == 0:
                        sp.wait_ge(s_mm.sem, s_mm(b, 0))
                    sp.wait_ge(hi1_ok.sem, hi1_ok(b, 2 * g + 2))
                    sp.wait_ge(lo1_ok.sem, lo1_ok(b, 2 * g + 2))
                    for h in range(Q4):
                        src = slice(DH * h, DH * h + DH)
                        for stack, part, roles in ((qs, 2 * g, (hi1, lo1, hi1)), (ks, 2 * g + 1, (hi1, hi1, lo1))):
                            for r, of in enumerate(roles):
                                sp.dma_start(stack[DH * r:DH * r + DH, g * Q4 + h, :].bitcast(F32),
                                             of[src, part, :].bitcast(F32)).then_inc(stack_ok[g].sem, 16)
                for ct in range(CT):
                    sp.wait_ge(o3_ok.sem, o3_ok(b, ct + 1))
                    sp.dma_start(out[b, ct * P:(ct + 1) * P, :], o3[:, ct, :]).then_inc(stored.sem, 16)
            sp.wait_ge(stored.sem, stored(B, 0))

        @block.gpsimd
        def _(pool):
            pool.memset(minus_half[:, :], -0.5).then_inc(prep_p.sem, 1)
            pool.wait_ge(prep_p.sem, 1)
            pool.memset(vo[:, :, :, :], 1.0).then_inc(prep_p.sem, 1)
            pool.wait_ge(prep_p.sem, 2)
            pool.memset(ks[STACK:STACK + 1, :, :].bitcast(F32), -1.0).then_inc(prep_p.sem, 1)
            pool.wait_ge(prep_p.sem, 3)
            pool.wait_ge(consts_in.sem, 16 * len(loads))
            pool.tensor_scalar(inv0[:, :], vv("var"), EPS, None, ALU.add).then_inc(prep_p.sem, 1)
            pool.wait_ge(prep_p.sem, 4)
            pool.tensor_tensor(inv0[:, :], inv0[:, :], minus_half[:, :], ALU.pow).then_inc(prep_p.sem, 1)
            with pool.Fori(0, B) as b:
                for n in range(3):
                    pool.wait_ge(gn_v.sem, gn_v(b, 11 * n + 8))
                    pool.tensor_tensor(rstd[:, :], gve[:, :], minus_half[:, :], ALU.pow).then_inc(gn_p.sem, 1)

        @block.vector
        def _(dve):
            dve.wait_ge(consts_in.sem, 16 * len(loads))
            dve.wait_ge(prep_p.sem, PREP_P)
            done = 0

            def prepared(ins):
                nonlocal done
                done += 1
                ins.then_inc(prep_v.sem, 1)

            for m in range(4 * 3):
                for e in range(2):
                    prepared(dve.tensor_scalar(up_m[:, m, e * UPH:(e + 1) * UPH], up_w[:, :],
                                               up_h[:, 2 * m + e:2 * m + e + 1], 4.0, ALU.mult, ALU.mult))
            for r in range(WIN):
                ins = dve.tensor_scalar(dn_m[:, r * W:(r + 1) * W], dn_w[:, :], dn_h[:, r:r + 1], None, ALU.mult)
            prepared(ins)
            dve.tensor_tensor(b_z[:, :], rowc[:, 3 * C:4 * C], rowc[:, 4 * C:5 * C], ALU.add)
            dve.tensor_scalar(wqk1[:, :, :], wqk1[:, :, :], float(DH) ** -0.25, None, ALU.mult)
            dve.tensor_scalar(vv("b_qk"), vv("b_qk"), float(DH) ** -0.25, None, ALU.mult)
            dve.tensor_tensor(inv0[:, :], inv0[:, :], vv("gamma"), ALU.mult)
            prepared(dve.tensor_tensor(add0[:, :], vv("br"), vv("mean"), ALU.subtract))
            dve.wait_ge(prep_v.sem, done)
            prepared(dve.tensor_tensor(add0[:, :], add0[:, :], inv0[:, :], ALU.mult))
            dve.wait_ge(prep_v.sem, done)
            dve.tensor_tensor(add0[:, :], add0[:, :], vv("beta"), ALU.add).then_inc(prep_v.sem, 1)
            assert done + 1 == PREP_V + 1, done
            dve.wait_ge(prep_v.sem, done + 1)

            def group_norm(b, n, src, scale, bias):
                k = 11 * n

                def step(ins):
                    nonlocal k
                    k += 1
                    ins.then_inc(gn_v.sem, 1)
                    return k

                def last():
                    dve.wait_ge(gn_v.sem, gn_v(b, k))

                for ct in range(CT):
                    for half in range(2):
                        ins = dve.bn_stats(st6[:, ct, half, :], src[:, ct, half * HALF:(half + 1) * HALF])
                step(ins)
                last()
                dve.memset(spare[:, :], 0.0)
                for ct in range(CT):
                    ins = dve.bn_aggr(mv[:, ct, :], st6[:, ct, :, :])
                step(ins)
                last()
                step(dve.tensor_tensor(sq[:, :], mv[:, :, 0], mv[:, :, 0], ALU.mult))
                last()
                step(dve.tensor_tensor(mv[:, :, 1], mv[:, :, 1], sq[:, :], ALU.add))
                dve.wait_ge(gn_mm.sem, gn_mm(b, n + 1))
                step(dve.tensor_copy(gm[:, :, :], gn_ps(n)))
                last()
                step(dve.tensor_tensor(gsq[:, :], gm[:, :, 0], gm[:, :, 0], ALU.mult))
                step(dve.tensor_scalar(gve[:, :], gm[:, :, 1], EPS, None, ALU.add))
                last()
                step(dve.tensor_tensor(gve[:, :], gve[:, :], gsq[:, :], ALU.subtract))
                dve.wait_ge(gn_p.sem, gn_p(b, n + 1))
                step(dve.tensor_tensor(ga[:, :], rstd[:, :], vv(scale), ALU.mult))
                last()
                step(dve.tensor_tensor(gma[:, :], gm[:, :, 0], ga[:, :], ALU.mult))
                last()
                step(dve.tensor_tensor(gb[:, :], vv(bias), gma[:, :], ALU.subtract))
                last()

            with dve.Fori(0, B) as b:
                for i, (dst, pattern) in enumerate(((qT0, None), (kT0, None), (vT0, "p (h w) -> p w h"))):
                    dve.wait_ge(qkv0_sb.sem, qkv0_sb(b, i + 1))
                    if i == 0:
                        dve.wait_ge(av0.sem, av0(b, 0))
                    src = qkv0[:, i, :].rearrange(pattern or "p (h w) -> p h w", h=H)
                    dve.transpose(dst[:, :, :], src).then_inc(tr0.sem, 1)
                scores = ps[:, 6:8, :].rearrange("p a (c j) -> p (a c) j", j=32)
                dve.wait_ge(corr0.sem, corr0(b, 1))
                dve.tensor_reduce(mx0[:, :], scores, AX_X, ALU.max).then_inc(dve0.sem, 1)
                dve.wait_ge(dve0.sem, dve0(b, 1))
                dve.tensor_tensor(e0[:, :, :], scores, mx0[:, :].unsqueeze(2).to_broadcast([P, 32, 32]),
                                  ALU.subtract).then_inc(dve0.sem, 1)
                dve.wait_ge(exp0.sem, exp0(b, 1))
                dve.transpose(pT0[:, :, :], e0[:, :, :]).then_inc(pT0_ok.sem, 1)
                dve.tensor_reduce(sum0[:, :], e0[:, :, :], AX_X, ALU.add).then_inc(dve0.sem, 1)
                dve.wait_ge(dve0.sem, dve0(b, 3))
                dve.reciprocal(sum0[:, :], sum0[:, :]).then_inc(dve0.sem, 1)
                dve.wait_ge(dve0.sem, dve0(b, 4))
                dve.wait_ge(av0.sem, av0(b, 1))
                dve.tensor_tensor(y0[:, :, :], ps[:, 0:2, :].rearrange("p a (c n) -> p (a c) n", n=32),
                                  sum0[:, :].unsqueeze(2).to_broadcast([P, 32, 32]), ALU.mult).then_inc(dve0.sem, 1)
                dve.wait_ge(dve0.sem, dve0(b, 5))
                dve.transpose(yc0[:, :, :].rearrange("p h w -> p w h"),
                              y0[:, :, :].rearrange("p c w -> p w c")).then_inc(dve0.sem, 1)
                for ct in range(CT):
                    dve.wait_ge(r0_ok.sem, r0_ok(b, ct + 1))
                    dve.tensor_tensor(x1[:, ct, :], r0[:, ct, :], x0[:, ct, :], ALU.add).then_inc(x1_ok.sem, 1)
                dve.wait_ge(x1_ok.sem, x1_ok(b, 2))

                group_norm(b, 0, x1, "gn1_scale", "gn1_bias")
                dve.wait_ge(stored.sem, stored(b, 0))
                for ct in range(CT):
                    dve.tensor_scalar(xn1[:, ct, :], x1[:, ct, :], ga[:, ct:ct + 1], gb[:, ct:ct + 1],
                                      ALU.mult, ALU.add).then_inc(xn1_ok.sem, 1)
                for i in range(4):
                    dve.wait_ge(hi1_ok.sem, hi1_ok(b, i + 1))
                    dve.scalar_tensor_tensor(out=lo1[:, i, :], in0=ps[:, 2 * i:2 * i + 2, :].rearrange("p a n -> p (a n)"),
                                             scalar=v("b_qk", i), in1=hi1[:, i, :].bitcast(F32),
                                             op0=ALU.add, op1=ALU.subtract).then_inc(lo1_ok.sem, 1)
                for j in range(4):
                    dve.wait_ge(v1_mm.sem, v1_mm(b, j + 1))
                    dve.tensor_tensor(vo[:, 2 * j:2 * j + 2, :, 0:DH],
                                      ps[:, j, :].rearrange("p (s h d) -> p s h d", s=2, d=DH),
                                      rowc[:, 0:C].rearrange("p (s h d) -> p s h d", s=1, d=DH)
                                      .to_broadcast([P, 2, HEADS, DH]), ALU.add).then_inc(v1_ok.sem, 1)

                def max_steps(u, i):
                    if i == 0:
                        dve.wait_ge(mxr_ok.sem, mxr_ok(b, u))
                    for m in range(4):
                        k = u * 32 + 4 * i + m
                        dve.wait_ge(max_mm.sem, max_mm(b, k + 1))
                        dve.tensor_reduce(mxp[:, 2 * (i % 2) + m // 2, i // 2, m % 2:m % 2 + 1],
                                          ps[:, 2 + m % 2, :], AX_X, ALU.max).then_inc(max_ok.sem, 1)

                def max_join(u):
                    dve.wait_ge(max_ok.sem, max_ok(b, 32 * (u + 1)))
                    dve.tensor_tensor(mxr[:, :, :], mxp[:, :, :, 0], mxp[:, :, :, 1], ALU.max).then_inc(mxr_ok.sem, 1)

                def normalise(u):
                    g, th = u // 2, u % 2
                    dve.wait_ge(av_mm.sem, av_mm(b, (u + 1) * NT))
                    for bank in range(2):
                        for m in range(2):
                            at = 2 * DH * m
                            dve.wait_ge(att_ok.sem, att_ok(b, max(Q4 * u + 2 * bank + m - 1, 0)))
                            dve.reciprocal(rec1[:, m, :], ps[at + DH:at + 2 * DH, 4 + bank, :]).then_inc(rec_ok.sem, 1)
                        for m in range(2):
                            at, h = 2 * DH * m, 2 * bank + m
                            dve.wait_ge(rec_ok.sem, rec_ok(b, Q4 * u + h + 1))
                            dve.tensor_tensor(att1[DH * h:DH * h + DH, g, th * HALF:(th + 1) * HALF],
                                              ps[at:at + DH, 4 + bank, :], rec1[:, m, :],
                                              ALU.mult).then_inc(att_ok.sem, 1)

                for i in range(NT):
                    max_steps(0, i)
                max_join(0)
                for u in range(UNITS):
                    for i in range(NT):
                        if i == 0 and u > 0:
                            normalise(u - 1)
                        if u + 1 < UNITS:
                            max_steps(u + 1, i)
                    if u + 1 < UNITS:
                        max_join(u + 1)
                normalise(UNITS - 1)
                for ct in range(CT):
                    dve.wait_ge(proj_mm.sem, proj_mm(b, ct + 1))
                    dve.scalar_tensor_tensor(out=x2[:, ct, :], in0=ps[:, 2 * ct:2 * ct + 2, :].rearrange("p a n -> p (a n)"),
                                             scalar=v("b_proj", ct), in1=x1[:, ct, :],
                                             op0=ALU.add, op1=ALU.add).then_inc(x2_ok.sem, 1)
                dve.wait_ge(x2_ok.sem, x2_ok(b, 2))

                group_norm(b, 1, x2, "gn2_scale", "gn2_bias")
                for ct in range(CT):
                    dve.tensor_scalar(xn2[:, ct, :], x2[:, ct, :], ga[:, ct:ct + 1], gb[:, ct:ct + 1],
                                      ALU.mult, ALU.add).then_inc(xn2_ok.sem, 1)
                dve.memset(kv[:, :, 2 * C:2 * C + 1], 1.0)
                for t in range(NT):
                    dve.wait_ge(kv_mm.sem, kv_mm(b, t + 1))
                    dve.tensor_tensor(kv[:, t, 0:2 * C], ps[:, t % 4, :], rowc[:, C:3 * C], ALU.add).then_inc(kv_ok.sem, 1)
                dve.wait_ge(kv_ok.sem, kv_ok(b, NT))
                dve.tensor_reduce(rmx[:, :], kv[:, :, 0:C], AX_X, ALU.max, negate=True).then_inc(rmx_ok.sem, 1)
                dve.tensor_reduce(cmx[:, :], kv[:, :, 0:C].rearrange("p t d -> p d t"), AX_X, ALU.max).then_inc(cmx_ok.sem, 1)
                dve.wait_ge(cmt_mm.sem, cmt_mm(b, 1))
                dve.tensor_reduce(cmc[:, :], ps[:, 4, 0:C].rearrange("p (a n) -> p a n", a=CT), AX_X, ALU.max).then_inc(cmc_ok.sem, 1)
                dve.wait_ge(qe_ok.sem, qe_ok(b, NT))
                dve.reciprocal(qrec[:, :], qsum[:, :]).then_inc(qrec_ok.sem, 1)
                dve.wait_ge(qrec_ok.sem, qrec_ok(b, 1))
                for t in range(NT):
                    dve.tensor_scalar(qe[:, t, :], qe[:, t, :], qrec[:, t:t + 1], float(C) ** -0.5,
                                      ALU.mult, ALU.mult).then_inc(qn_ok.sem, 1)
                dve.wait_ge(cmb_mm.sem, cmb_mm(b, 1))
                dve.tensor_copy(cmb[:, :], ps[:, 5, 0:C]).then_inc(cmb_ok.sem, 1)
                dve.wait_ge(cmb_ok.sem, cmb_ok(b, 1))
                dve.tensor_tensor(ke[:, :, :], kv[:, :, 0:C], cmb[:, :].unsqueeze(1).to_broadcast([P, NT, C]),
                                  ALU.subtract).then_inc(ks_ok.sem, 1)
                for j in range(4):
                    ct, half = j // 2, j % 2
                    dve.wait_ge(qt_mm.sem, qt_mm(b, j + 1))
                    dve.tensor_copy(qc[:, ct, half * HALF:(half + 1) * HALF], ps[:, j, :]).then_inc(qc_ok.sem, 1)
                for ct in range(CT):
                    dve.wait_ge(ctx_mm.sem, ctx_mm(b, ct + 1))
                    dve.reciprocal(crec[:, ct:ct + 1], ps[:, 6 + ct, C:C + 1]).then_inc(crec_ok.sem, 1)
                    dve.wait_ge(crec_ok.sem, crec_ok(b, ct + 1))
                    dve.tensor_scalar(ctx2[:, ct, :], ps[:, 6 + ct, 0:C], crec[:, ct:ct + 1], None, ALU.mult).then_inc(ctx_ok.sem, 1)
                dve.wait_ge(o2_ok.sem, o2_ok(b, 2))
                group_norm(b, 2, o2, "gn3_scale", "gn3_bias")
                for j in range(4):
                    dve.wait_ge(z_mm.sem, z_mm(b, j + 1))
                    dve.tensor_tensor(z3[:, 2 * j:2 * j + 2, :], ps[:, j, :].rearrange("p (s c) -> p s c", s=2),
                                      b_z[:, :].unsqueeze(1).to_broadcast([P, 2, C]), ALU.add).then_inc(z_ok.sem, 1)

                for j in range(UPT // 2):
                    dve.wait_ge(relu_ok.sem, relu_ok(b, j + 1))
                    dve.scalar_tensor_tensor(out=up3[:, 2 * j:2 * j + 2, :].rearrange("p s c -> p (s c)"),
                                             in0=ps[:, 4 + j % 4, :], scalar=SLOPE * ROOT2, in1=rl3[:, j % 2, :],
                                             op0=ALU.mult, op1=ALU.add).then_inc(up_ok.sem, 1)

        @block.scalar
        def _(act):
            act.wait_ge(consts_in.sem, 16 * len(loads))
            act.wait_ge(prep_v.sem, PREP_V + 1)

            def two_banks(at):
                return ps[:, at:at + 2, :].rearrange("p a n -> p (a n)")

            with act.Fori(0, B) as b:
                for i, name in enumerate(("bq", "bk", "bv")):
                    act.wait_ge(qkv0_mm.sem, qkv0_mm(b, i + 1))
                    act.wait_ge(tr0.sem, tr0(b, 0))
                    act.activation(qkv0[:, i, :], two_banks(2 * i), ACT.Identity, bias=v(name)).then_inc(qkv0_sb.sem, 1)
                act.wait_ge(dve0.sem, dve0(b, 2))
                act.activation(e0[:, :, :], e0[:, :, :], ACT.Exp).then_inc(exp0.sem, 1)
                for ct in range(CT):
                    act.wait_ge(wr_mm.sem, wr_mm(b, ct + 1))
                    act.activation(r0[:, ct, :], two_banks(2 + 2 * ct), ACT.Identity, bias=add0[:, ct:ct + 1],
                                   scale=inv0[:, ct:ct + 1]).then_inc(r0_ok.sem, 1)

                for i in range(4):
                    act.wait_ge(qk1_mm.sem, qk1_mm(b, i + 1))
                    act.activation(hi1[:, i, :], two_banks(2 * i), ACT.Identity, bias=v("b_qk", i)).then_inc(hi1_ok.sem, 1)

                def row_copies(u):
                    g, th = u // 2, u % 2
                    for h in range(Q4):
                        act.wait_ge(row_mm.sem, row_mm(b, Q4 * u + h + 1))
                        act.activation(qs[STACK:STACK + 1, g * Q4 + h, th * HALF:(th + 1) * HALF],
                                       ps[STACK:STACK + 1, 2 + h % 2, :], ACT.Copy).then_inc(row_ok.sem, 1)

                row_copies(0)
                for u in range(UNITS):
                    for s in range(NT):
                        n = u * NT + s
                        act.wait_ge(av_mm.sem, av_mm(b, max(n - 1, 0)))
                        for pair in range(2):
                            k = 2 * n + pair
                            act.wait_ge(s_mm.sem, s_mm(b, k + 1))
                            act.activation(prob[:, n % 2, 2 * pair:2 * pair + 2, :].rearrange("p a n -> p (a n)"),
                                           two_banks(6 * pair), ACT.Exp).then_inc(p_ok.sem, 1)
                    if u + 1 < UNITS:
                        row_copies(u + 1)

                act.wait_ge(rmx_ok.sem, rmx_ok(b, 1))
                for t in range(NT):
                    act.activation(qe[:, t, :], kv[:, t, 0:C], ACT.Exp, bias=rmx[:, t:t + 1],
                                   accum_out=qsum[:, t:t + 1]).then_inc(qe_ok.sem, 1)
                act.wait_ge(ks_ok.sem, ks_ok(b, 1))
                act.activation(ke[:, :, :], ke[:, :, :], ACT.Exp).then_inc(ke_ok.sem, 1)
                for ct in range(CT):
                    act.wait_ge(o2_mm.sem, o2_mm(b, ct + 1))
                    act.activation(o2[:, ct, :], two_banks(2 * ct), ACT.Copy).then_inc(o2_ok.sem, 1)
                act.wait_ge(gn_v.sem, gn_v(b, 33))
                for ct in range(CT):
                    act.activation(g2[:, ct, :], o2[:, ct, :], ACT.Gelu, bias=gb[:, ct:ct + 1],
                                   scale=ga[:, ct:ct + 1]).then_inc(g2_ok.sem, 1)

                for j in range(UPT // 2):
                    act.wait_ge(up_mm.sem, up_mm(b, j + 1))
                    if j >= 2:
                        act.wait_ge(up_ok.sem, up_ok(b, j - 1))
                    act.activation(rl3[:, j % 2, :], ps[:, 4 + j % 4, :], ACT.Relu,
                                   scale=(1.0 - SLOPE) * ROOT2).then_inc(relu_ok.sem, 1)
                for ct in range(CT):
                    act.wait_ge(dn_mm.sem, dn_mm(b, ct + 1))
                    act.wait_ge(stored.sem, stored(b, 0))
                    act.activation(o3[:, ct, :], two_banks(2 * ct), ACT.Copy).then_inc(o3_ok.sem, 1)

        @block.tensor
        def _(pe):
            pe.wait_ge(consts_in.sem, 16 * len(loads))
            pe.wait_ge(prep_p.sem, PREP_P)
            pe.wait_ge(prep_v.sem, PREP_V + 1)

            def product(dst, pairs):
                for n, (lhsT, rhs) in enumerate(pairs):
                    ins = pe.matmul(dst, lhsT, rhs, start=(n == 0), stop=(n == len(pairs) - 1))
                return ins

            def half(t, ct, i):
                return t[:, ct, i * HALF:(i + 1) * HALF]

            def average(b, n, matrix):
                pe.wait_ge(gn_v.sem, gn_v(b, 11 * n + 4))
                pe.matmul(gn_ps(n), matrix[:, :], mv[:, :, :], start=True, stop=True).then_inc(gn_mm.sem, 1)

            with pe.Fori(0, B) as b:
                pe.wait_ge(x_in.sem, x_in(b, 2))
                pe.wait_ge(o3_ok.sem, o3_ok(b, 0))
                pe.wait_ge(up_ok.sem, up_ok(b, 0))
                for i in range(3):
                    for hf in range(2):
                        ins = product(ps[:, 2 * i + hf, :],
                                      [(wq0[:, kt, i * CR:(i + 1) * CR], half(x0, kt, hf)) for kt in range(CT)])
                    ins.then_inc(qkv0_mm.sem, 1)
                pe.wait_ge(tr0.sem, tr0(b, 2))
                pe.matmul(ps[:, 6, 0:1], ident[:, :], ident[:, 0:1], start=True, stop=True)
                for q in range(Q4):
                    at = slice(32 * q, 32 * q + 32)
                    for c in range(32):
                        ins = pe.matmul(ps[at, 6 + c // 16, 32 * (c % 16):32 * (c % 16) + 32],
                                        qT0[at, :, c], kT0[at, :, c], start=True, stop=True)
                ins.then_inc(corr0.sem, 1)
                pe.wait_ge(pT0_ok.sem, pT0_ok(b, 1))
                pe.wait_ge(tr0.sem, tr0(b, 3))
                pe.matmul(ps[:, 0, 0:1], ident[:, :], ident[:, 0:1], start=True, stop=True)
                for q in range(Q4):
                    at = slice(32 * q, 32 * q + 32)
                    for c in range(32):
                        ins = pe.matmul(ps[at, c // 16, 32 * (c % 16):32 * (c % 16) + 32],
                                        pT0[at, c, :], vT0[at, :, c], start=True, stop=True)
                ins.then_inc(av0.sem, 1)
                pe.wait_ge(dve0.sem, dve0(b, 6))
                yc = yc0[:, :, :].rearrange("p h w -> p (h w)")
                for ct in range(CT):
                    for hf in range(2):
                        ins = product(ps[:, 2 + 2 * ct + hf, :],
                                      [(wr0[:, ct * P:(ct + 1) * P], yc[:, hf * HALF:(hf + 1) * HALF])])
                    ins.then_inc(wr_mm.sem, 1)

                average(b, 0, avg8)
                pe.wait_ge(xn1_ok.sem, xn1_ok(b, 2))
                for i in range(4):
                    for hf in range(2):
                        ins = product(ps[:, 2 * i + hf, :],
                                      [(wqk1[:, kt, i * P:(i + 1) * P], half(xn1, kt, hf)) for kt in range(CT)])
                    ins.then_inc(qk1_mm.sem, 1)
                for j in range(4):
                    pe.wait_ge(lo1_ok.sem, lo1_ok(b, 1 + j // 2))
                    for s in range(2):
                        t = 2 * j + s
                        ins = product(ps[:, j, s * C:(s + 1) * C],
                                      [(xn1[:, kt, t * P:(t + 1) * P], wv1[:, kt, :]) for kt in range(CT)])
                    ins.then_inc(v1_mm.sem, 1)

                def max_products(u, i):
                    g, th = u // 2, u % 2
                    for m in range(4):
                        k = u * 32 + 4 * i + m
                        head = g * Q4 + 2 * (i % 2) + m // 2
                        t0 = th * HALF + (i // 2) * P
                        if k >= 2:
                            pe.wait_ge(max_ok.sem, max_ok(b, k - 1))
                        if i == 0 and m < 2:
                            if u == 0:
                                pe.wait_ge(v1_ok.sem, v1_ok(b, 4))
                            else:
                                pe.wait_ge(row_ok.sem, row_ok(b, Q4 * u))
                        pe.matmul(ps[:, 2 + m % 2, :], qs[0:STACK, head, t0:t0 + P],
                                  ks[0:STACK, head, (m % 2) * HALF:(m % 2 + 1) * HALF],
                                  start=True, stop=True).then_inc(max_mm.sem, 1)

                def row_products(u):
                    pe.wait_ge(mxr_ok.sem, mxr_ok(b, u + 1))
                    for h in range(Q4):
                        if h >= 2:
                            pe.wait_ge(row_ok.sem, row_ok(b, Q4 * u + h - 1))
                        for tt in range(4):
                            ins = pe.matmul(ps[STACK:STACK + 1, 2 + h % 2, tt * P:(tt + 1) * P],
                                            mxr[:, h, tt:tt + 1], ident[:, :], start=True, stop=True)
                        ins.then_inc(row_mm.sem, 1)

                def logits(u, s):
                    g, th = u // 2, u % 2
                    for pair in range(2):
                        k = 2 * (u * NT + s) + pair
                        if k >= 2:
                            pe.wait_ge(p_ok.sem, p_ok(b, k - 1))
                        for m in range(2):
                            h = 2 * pair + m
                            if s == 0:
                                pe.wait_ge(row_ok.sem, row_ok(b, Q4 * u + h + 1))
                            ins = pe.matmul(ps[:, 6 * pair + m, :], ks[0:STACK + 1, g * Q4 + h, s * P:(s + 1) * P],
                                            qs[0:STACK + 1, g * Q4 + h, th * HALF:(th + 1) * HALF],
                                            start=True, stop=True)
                        ins.then_inc(s_mm.sem, 1)

                def values(u, s):
                    n = u * NT + s
                    pe.wait_ge(p_ok.sem, p_ok(b, 2 * n + 2))
                    if s == 0 and u > 0:
                        pe.wait_ge(att_ok.sem, att_ok(b, Q4 * u))
                    for h in range(Q4):
                        at = 2 * DH * (h % 2)
                        ins = pe.matmul(ps[at:at + 2 * DH, 4 + h // 2, :], vo[:, s, (u // 2) * Q4 + h, :],
                                        prob[:, n % 2, h, :], start=(s == 0), stop=(s == NT - 1))
                    ins.then_inc(av_mm.sem, 1)

                pe.wait_ge(stack_ok[0].sem, stack_ok[0](b, 24))
                pe.wait_ge(lo1_ok.sem, lo1_ok(b, 4))
                for i in range(NT):
                    max_products(0, i)
                row_products(0)
                for u in range(UNITS):
                    if u == 1:
                        pe.wait_ge(stack_ok[1].sem, stack_ok[1](b, 24))
                    for s in range(NT):
                        logits(u, s)
                        if u + 1 < UNITS:
                            max_products(u + 1, s)
                        if s > 0:
                            values(u, s - 1)
                    values(u, NT - 1)
                    if u + 1 < UNITS:
                        row_products(u + 1)
                pe.wait_ge(att_ok.sem, att_ok(b, UNITS * Q4))
                for ct in range(CT):
                    for hf in range(2):
                        ins = product(ps[:, 2 * ct + hf, :],
                                      [(wp1[:, kt, ct * P:(ct + 1) * P], half(att1, kt, hf)) for kt in range(CT)])
                    ins.then_inc(proj_mm.sem, 1)

                average(b, 1, avg16)
                pe.wait_ge(xn2_ok.sem, xn2_ok(b, 2))
                for t in range(NT):
                    if t >= 4:
                        pe.wait_ge(kv_ok.sem, kv_ok(b, t - 3))
                    product(ps[:, t % 4, :],
                            [(xn2[:, kt, t * P:(t + 1) * P], wkv2[:, kt, :]) for kt in range(CT)]).then_inc(kv_mm.sem, 1)
                pe.wait_ge(cmx_ok.sem, cmx_ok(b, 1))
                for ct in range(CT):
                    ins = pe.transpose(ps[:, 4, ct * P:(ct + 1) * P], cmx[:, ct * P:(ct + 1) * P], ident[:, :])
                ins.then_inc(cmt_mm.sem, 1)
                pe.wait_ge(cmc_ok.sem, cmc_ok(b, 1))
                for ct in range(CT):
                    ins = pe.matmul(ps[:, 5, ct * P:(ct + 1) * P], cmc[:, ct:ct + 1].to_broadcast([P, P]),
                                    ident[:, :], start=True, stop=True)
                ins.then_inc(cmb_mm.sem, 1)
                for j in range(4):
                    ct, hf = j // 2, j % 2
                    pe.wait_ge(qn_ok.sem, qn_ok(b, 4 * hf + 4))
                    if j == 0:
                        pe.wait_ge(kv_ok.sem, kv_ok(b, NT))
                    for t in range(4):
                        ins = pe.transpose(ps[:, j, t * P:(t + 1) * P], qe[:, 4 * hf + t, ct * P:(ct + 1) * P], ident[:, :])
                    ins.then_inc(qt_mm.sem, 1)
                pe.wait_ge(ke_ok.sem, ke_ok(b, 1))
                for ct in range(CT):
                    product(ps[:, 6 + ct, 0:C + 1],
                            [(ke[:, t, ct * P:(ct + 1) * P], kv[:, t, C:2 * C + 1]) for t in range(NT)])\
                        .then_inc(ctx_mm.sem, 1)
                pe.wait_ge(ctx_ok.sem, ctx_ok(b, CT))
                pe.wait_ge(qc_ok.sem, qc_ok(b, 4))
                for ct in range(CT):
                    for hf in range(2):
                        ins = product(ps[:, 2 * ct + hf, :],
                                      [(ctx2[:, kt, ct * P:(ct + 1) * P], half(qc, kt, hf)) for kt in range(CT)])
                    ins.then_inc(o2_mm.sem, 1)
                average(b, 2, avg16)
                pe.wait_ge(g2_ok.sem, g2_ok(b, 2))
                for j in range(4):
                    for s in range(2):
                        t = 2 * j + s
                        at = slice(t * P, (t + 1) * P)
                        for kt in range(CT):
                            pe.matmul(ps[:, j, s * C:(s + 1) * C], g2[:, kt, at], wo2[:, kt, :],
                                      start=(kt == 0 and s == 0), stop=False, skip_group_check=True)
                        for kt in range(CT):
                            ins = pe.matmul(ps[:, j, s * C + kt * P:s * C + (kt + 1) * P], xn2[:, kt, at], ident[:, :],
                                            start=False, stop=True, skip_group_check=True)
                    ins.then_inc(z_mm.sem, 1)

                for j in range(UPT):
                    if j % 2 == 0 and j >= 8:
                        pe.wait_ge(up_ok.sem, up_ok(b, j // 2 - 3))
                    tiles = [(j // 4 + d, 3 * (j % 4) + d + 1) for d in (-1, 0, 1)
                             if 0 <= j // 4 + d < NT and j - REACH < 4 * (j // 4 + d) + 4 and j + REACH >= 4 * (j // 4 + d)]
                    pe.wait_ge(z_ok.sem, z_ok(b, max(t for t, _ in tiles) // 2 + 1))
                    ins = product(ps[:, 4 + (j // 2) % 4, (j % 2) * C:(j % 2 + 1) * C],
                                  [(up_m[:, m, :], z3[:, t, :]) for t, m in tiles])
                    if j % 2 == 1:
                        ins.then_inc(up_mm.sem, 1)
                for ct in range(CT):
                    begun = set()
                    for j in range(UPT):
                        pe.wait_ge(up_ok.sem, up_ok(b, j // 2 + 1))
                        lo, hi = max(j - REACH, 0), min(j + REACH + 1, H)
                        for bank in range(2):
                            r0_, r1_ = max(lo, bank * 16), min(hi, bank * 16 + 16)
                            if r0_ >= r1_:
                                continue
                            m0 = (r0_ - (j - REACH)) * W
                            ins = pe.matmul(ps[:, 2 * ct + bank, (r0_ - bank * 16) * W:(r1_ - bank * 16) * W],
                                            up3[:, j, ct * P:(ct + 1) * P], dn_m[:, m0:m0 + (r1_ - r0_) * W],
                                            start=(bank not in begun), stop=(j == UPT - 1 or r1_ == 16 and j == 18),
                                            skip_group_check=True)
                            begun.add(bank)
                    ins.then_inc(dn_mm.sem, 1)


def kernel(x, **w):
    import numpy as np
    import concourse.bacc as bacc
    from concourse.bass_utils import run_bass_kernel_spmd

    def tiles(a):
        a = np.asarray(a)
        return np.ascontiguousarray(a.reshape(-1, P, a.shape[-1]).transpose(1, 0, 2))

    def toeplitz(taps, index):
        padded = np.concatenate([np.asarray(taps)[::-1], np.zeros(1, np.float32)])
        return padded[np.where((index >= 0) & (index < TAPS), index, TAPS)]

    a = {k: np.asarray(v) for k, v in w.items()}
    x = np.asarray(x)
    L0, L1, L2, L3 = "L0_conv_", "L1_conv_", "L2_conv_", "L3_conv_"
    arrays = {"x": np.ascontiguousarray(x.reshape(B, C, N))}
    arrays["wq0"] = tiles(np.concatenate([a[L0 + "Wq"], a[L0 + "Wk"], a[L0 + "Wv"]]).T)
    arrays["wr0"] = np.ascontiguousarray(a[L0 + "Wr"].T)
    qkv = a[L1 + "w_qkv"].reshape(GROUPS4, Q4, 3, DH, C)
    arrays["wqk1"] = tiles(qkv[:, :, 0:2].transpose(0, 2, 1, 3, 4).reshape(4 * P, C).T)
    arrays["wv1"] = tiles(qkv[:, :, 2].reshape(C, C).T)
    arrays["wp1"] = tiles(a[L1 + "w_proj"].T)
    arrays["wkv2"] = tiles(a[L2 + "kv_w"].T)
    arrays["wo2"] = tiles(a[L2 + "out_w"].T)
    b_qkv = a[L1 + "b_qkv"].reshape(GROUPS4, Q4, 3, DH)
    vectors = {"bq": a[L0 + "bq"], "bk": a[L0 + "bk"], "bv": a[L0 + "bv"], "br": a[L0 + "br"],
               "gamma": a[L0 + "gamma"], "beta": a[L0 + "beta"], "mean": a[L0 + "running_mean"],
               "var": a[L0 + "running_var"], "gn1_scale": a[L1 + "gn_scale"], "gn1_bias": a[L1 + "gn_bias"],
               "b_qk": b_qkv[:, :, 0:2].transpose(0, 2, 1, 3).reshape(-1), "b_proj": a[L1 + "b_proj"],
               "gn2_scale": a[L2 + "norm1_w"], "gn2_bias": a[L2 + "norm1_b"],
               "gn3_scale": a[L2 + "norm2_w"], "gn3_bias": a[L2 + "norm2_b"]}
    arrays["vectors"] = np.ascontiguousarray(np.concatenate([vectors[k].reshape(-1, P) for k in VEC]).T)
    row = np.concatenate([b_qkv[:, :, 2].reshape(-1), a[L2 + "kv_b"], a[L2 + "out_b"], a[L3 + "bias"]])
    arrays["rows"] = np.ascontiguousarray(np.broadcast_to(row, (P, row.size)))

    lane = np.arange(P)
    h4, w4 = lane // W, lane % W
    r, d, e = (i.reshape(-1) for i in np.meshgrid(np.arange(4), np.arange(-1, 2), np.arange(2), indexing="ij"))
    up = a[L3 + "up_filter"]
    arrays["up_h"] = toeplitz(up, 2 * (4 * d[None] + h4[:, None]) - (2 * r + e)[None] + 6)
    arrays["up_w"] = toeplitz(up, 2 * w4[:, None] - np.arange(UPH)[None] + 6)
    down = a[L3 + "down_filter"]
    e2, w2 = lane // UPH, lane % UPH
    arrays["dn_h"] = toeplitz(down, e2[:, None] - 2 * np.arange(WIN)[None] + 11)
    arrays["dn_w"] = toeplitz(down, w2[:, None] - 2 * np.arange(W)[None] + 5)

    arrays["ident"] = np.eye(P, dtype=np.float32)
    for name, size in (("avg8", 8), ("avg16", 16)):
        arrays[name] = np.kron(np.eye(P // size), np.full((size, size), 1.0 / size)).astype(np.float32)

    nc = bacc.Bacc("TRN2", target_bir_lowering=False, num_devices=1)
    ap = {k: nc.dram_tensor("in_" + k, t.shape, mybir.dt.from_np(t.dtype), kind="ExternalInput").ap()
          for k, t in arrays.items()}
    out = nc.dram_tensor("out", (B, C, N), F32, kind="ExternalOutput").ap()
    chain_kernel(nc, ap["x"], ap, ap["vectors"], ap["rows"], ap, ap, out)
    got = run_bass_kernel_spmd(nc, [{"in_" + k: t for k, t in arrays.items()}], core_ids=[0])
    return got.results[0]["out"].reshape(B, C, H, W)
```

```python
from contextlib import ExitStack

import concourse.bass as bass
from concourse import mybir

ALU = mybir.AluOpType
ACT = mybir.ActivationFunctionType
AX_X = mybir.AxisListType.X
F32 = mybir.dt.float32
F32R = mybir.dt.float32r

B, C, H, W = 16, 256, 32, 32
P = 128
CT = C // P
N = H * W
HALF = N // 2
NT = N // P
CR = C // 2
Q4 = 4
HEADS, DH = 8, 32
GROUPS4 = HEADS // Q4
UNITS = GROUPS4 * 2
STACK = 3 * DH
EPS = 1e-5
UPH = 2 * H
UPT = UPH // 2
TAPS = 12
REACH = 3
WIN = 2 * REACH + 1
ROOT2 = float(2.0 ** 0.5)
SLOPE = 0.2

VEC = {}
for _name, _n in (("bq", 1), ("bk", 1), ("bv", 1), ("br", CT), ("gamma", CT), ("beta", CT), ("mean", CT), ("var", CT),
                  ("gn1_scale", CT), ("gn1_bias", CT), ("b_qk", 2 * GROUPS4), ("b_proj", CT),
                  ("gn2_scale", CT), ("gn2_bias", CT), ("gn3_scale", CT), ("gn3_bias", CT)):
    VEC[_name] = (sum(n for _, n in VEC.values()), _n)
NVEC = sum(n for _, n in VEC.values())


LEAD = 2
STEPS = UNITS * NT

SIDE = {
    0: ["q1"], 1: ["k1", "v1"], 2: ["proj0"], 3: ["proj1", "stats2"], 4: ["norm2", "copy_x"], 5: ["kv0", "kv1"],
    6: ["kv2", "kv3"], 7: ["kmax", "kmaxT"], 8: ["ke", "l0q"], 9: ["l0k", "l0v"], 10: ["corr0", "corr1"],
    11: ["corr2", "corr3", "soft0"], 12: ["context"], 13: ["av0", "av1"], 14: ["av2", "av3"], 15: ["qT0", "qT1"],
    16: ["wr0", "wr1", "stats1"], 17: ["o20"], 18: ["norm1", "o21"], 19: ["stats3", "q0"], 20: ["norm3", "k0", "v0"],
    21: ["z0", "z1"], 22: ["z2", "z3"], 23: ["up00"], 24: ["up01"], 25: ["dn00", "dn01"], 26: ["dn02", "dn03"],
    27: ["up10"], 28: ["up11"], 29: ["dn10", "dn11"], 30: ["dn12", "dn13"], 31: [],
}
OF_B, OF_J = ("q1", "k1", "v1"), ("l0", "corr", "soft0", "av", "wr", "stats1", "norm1", "q0", "k0", "v0")
FIRST = [name for n in range(STEPS) for name in SIDE[n] if name.startswith(OF_J)]


def beside(n, i, j):
    for name in SIDE[n]:
        if name == "copy_x" or name.startswith(OF_B) or (i is not None and not name.startswith(OF_J)) \
                or (j is not None and name.startswith(OF_J)):
            yield name


START = 1


class Signal:

    def __init__(self, sem, per_image, size=1):
        self.sem, self.per_image, self.size = sem, per_image, size

    def __call__(self, image, k):
        image, away = image if isinstance(image, tuple) else (image, 0)
        return image * (self.per_image * self.size) + ((away * self.per_image + k) * self.size + START)


def number(image):
    return image[0] + image[1] if isinstance(image, tuple) else image


def chain_kernel(nc, x, weights, vectors, rows, filters, consts, out):
    with ExitStack() as ctx:
        def sb(name, shape, dt=F32, over=None):
            return (over or ctx).enter_context(nc.sbuf_tensor(name, shape, dt))

        looped = []

        def signal(name, per_image, size=1):
            made = Signal(ctx.enter_context(nc.semaphore(name)), per_image, size)
            if per_image:
                looped.append(made)
            return made

        ps = ctx.enter_context(nc.psum_tensor("ps", [P, 8, HALF], F32))

        wq0 = sb("wq0", [P, CT, 3 * CR])
        wr0 = sb("wr0", [P, C])
        wqk1 = sb("wqk1", [P, CT, 4 * P])
        wv1 = sb("wv1", [P, CT, C])
        wp1 = sb("wp1", [P, CT, C])
        wkv2 = sb("wkv2", [P, CT, 2 * C])
        wo2 = sb("wo2", [P, CT, C])
        vec = sb("vec", [P, NVEC])
        rowc = sb("rowc", [P, 5 * C])
        ident = sb("ident", [P, P])
        avg8 = sb("avg8", [P, P])
        avg16 = sb("avg16", [P, P])
        up_m = sb("up_m", [P, 4 * 3, P])
        dn_m = sb("dn_m", [P, WIN * W])
        inv0 = sb("inv0", [P, CT])
        add0 = sb("add0", [P, CT])
        minus_half = sb("minus_half", [P, CT])
        b_z = sb("b_z", [P, C])

        xb = sb("xb", [P, CT, N])
        xa = sb("xa", [P, CT, N])
        st6 = sb("st6", [P, 3, CT, 2, 6])
        mv = sb("mv", [P, 3, CT, 2])
        sq = sb("sq", [P, 3, CT])
        gm = sb("gm", [P, 3, CT, 2])
        gsq = sb("gsq", [P, 3, CT])
        gve = sb("gve", [P, 3, CT])
        rstd = sb("rstd", [P, 3, CT])
        ga = sb("ga", [P, 3, CT])
        gma = sb("gma", [P, 3, CT])
        gb = sb("gb", [P, 3, CT])
        spare = sb("spare", [P, 1])
        xn1 = sb("xn1", [P, CT, N])
        ks = sb("ks", [P, HEADS, N], F32R)
        qs = sb("qs", [P, UNITS, Q4, HALF], F32R)
        vo = sb("vo", [P, NT, HEADS, 2 * DH])
        mxp = sb("mxp", [P, Q4, 4, 2])
        mxr = sb("mxr", [P, Q4, 4])
        mrow = sb("mrow", [4 * Q4, P], F32R)
        prob = sb("prob", [P, Q4, HALF])
        av_o = sb("av_o", [P, HALF])
        av_s = sb("av_s", [P, HALF])
        att1 = sb("att1", [P, GROUPS4, N])
        with ExitStack() as own:
            hi1 = sb("hi1", [P, 2, N], F32R, over=own)
            lo1 = sb("lo1", [P, 2, N], F32R, over=own)
        qT0 = sb("qT0", [P, H, 32])
        kT0 = sb("kT0", [P, H, 32])
        vT0 = sb("vT0", [P, W, 32])
        mx0 = sb("mx0", [P, 32])
        sum0 = sb("sum0", [P, 32])
        cmx = sb("cmx", [P, C])
        ctx2 = sb("ctx2", [P, CT, C])
        up_h = sb("up_h", [P, 4 * 3 * 2])
        up_w = sb("up_w", [P, UPH])
        dn_h = sb("dn_h", [P, WIN + 1])
        dn_w = sb("dn_w", [P, W])
        sb("region_end", [P, 64])
        slots0 = xn1
        e0, pT0 = (slots0[:, m, :].rearrange("p (c n) -> p c n", n=32) for m in range(2))
        y0 = e0
        yc0 = qT0
        xn2 = sb("xn2", [P, CT, N])
        o3 = xn2
        rmx = sb("rmx", [P, NT])
        qsum = sb("qsum", [P, NT])
        qrec = sb("qrec", [P, NT])
        cmc = sb("cmc", [P, CT])
        crec = sb("crec", [P, CT])
        with ExitStack() as own:
            up3 = sb("up3", [P, UPT, P], over=own)
        k2 = sb("k2", [P, NT, C])
        qe = sb("qe", [P, NT, C])
        v2 = sb("v2", [P, NT, C + 1])
        qc = k2[:, :, :].rearrange("p t c -> p (t c)").rearrange("p (a n) -> p a n", a=CT)
        o2 = qe[:, :, :].rearrange("p t c -> p (t c)").rearrange("p (a n) -> p a n", a=CT)
        z3 = v2[:, :, 0:C]

        def v(name, i=0):
            at = VEC[name][0]
            return vec[:, at + i:at + i + 1]

        def vv(name):
            at, n = VEC[name]
            return vec[:, at:at + n]

        def both(at=6):
            return ps[:, at:at + 2, :].rearrange("p a n -> p (a n)")

        def gn_ps(n):
            return ps[:, 7 if n == 2 else 6, 0:2 * CT].rearrange("p (c s) -> p c s", s=2)

        consts_in = signal("consts_in", 0)
        prep_v = signal("prep_v", 0)
        prep_p = signal("prep_p", 0)
        x_in = signal("x_in", 2, 16)
        xa_in = signal("xa_in", 1, 16)
        l0_mm = signal("l0_mm", 3)
        l0_sb = signal("l0_sb", 3)
        tr0 = signal("tr0", 3)
        corr0 = signal("corr0", 1)
        mx0_ok = signal("mx0_ok", 1)
        sub0 = signal("sub0", 1)
        exp0 = signal("exp0", 1)
        pT0_ok = signal("pT0_ok", 1)
        sum0_ok = signal("sum0_ok", 2)
        av0 = signal("av0", 1)
        y0_ok = signal("y0_ok", 1)
        yc0_ok = signal("yc0_ok", 1)
        wr_mm = signal("wr_mm", 2)
        res0 = signal("res0", 2)
        x1_ok = signal("x1_ok", 2)
        gn_v = [signal(f"gn_v{n}", 11) for n in range(3)]
        gn_mm = [signal(f"gn_mm{n}", 1) for n in range(3)]
        gn_p = [signal(f"gn_p{n}", 1) for n in range(3)]
        xn1_ok = signal("xn1_ok", 2)
        qk1_mm = signal("qk1_mm", 4)
        hi1_ok = signal("hi1_ok", 4)
        lo1_ok = signal("lo1_ok", 4)
        stack_ok = [signal(f"stack_ok{g}", 6 * Q4, 16) for g in range(GROUPS4)]
        v1_mm = signal("v1_mm", 2)
        v1_ok = signal("v1_ok", 4)
        max_mm = signal("max_mm", STEPS * Q4)
        max_ok = signal("max_ok", STEPS * Q4)
        mxr_ok = signal("mxr_ok", UNITS)
        row_mm = signal("row_mm", UNITS)
        row_ok = signal("row_ok", UNITS)
        row_in = signal("row_in", UNITS, 16)
        s_mm = signal("s_mm", STEPS * Q4)
        p_ok = signal("p_ok", STEPS * Q4)
        av_mm = signal("av_mm", STEPS * 2)
        av_o_ok = signal("av_o_ok", UNITS * Q4)
        av_s_ok = signal("av_s_ok", UNITS * Q4)
        rec_ok = signal("rec_ok", UNITS)
        att_ok = signal("att_ok", UNITS)
        proj_mm = signal("proj_mm", 2)
        x2_ok = signal("x2_ok", 2)
        xn2_ok = signal("xn2_ok", 2)
        ones2 = signal("ones2", 1)
        kv_mm = signal("kv_mm", NT)
        kv_ok = signal("kv_ok", NT * 2)
        rmx_ok = signal("rmx_ok", 1)
        qe_ok = signal("qe_ok", NT)
        qrec_ok = signal("qrec_ok", 1)
        qn_ok = signal("qn_ok", NT)
        cmx_ok = signal("cmx_ok", 1)
        cmt_mm = signal("cmt_mm", 1)
        cmc_ok = signal("cmc_ok", 1)
        cmb_mm = signal("cmb_mm", 1)
        ksub = signal("ksub", 1)
        ke_ok = signal("ke_ok", 1)
        qt_mm = signal("qt_mm", 4)
        qc_ok = signal("qc_ok", 4)
        ctx_mm = signal("ctx_mm", CT)
        crec_ok = signal("crec_ok", CT)
        ctx_ok = signal("ctx_ok", CT)
        o2_mm = signal("o2_mm", 2)
        o2_ok = signal("o2_ok", 2)
        g2_ok = signal("g2_ok", 2)
        z_mm = signal("z_mm", 4)
        z_ok = signal("z_ok", 4)
        up_mm = signal("up_mm", UPT // 2)
        relu_ok = signal("relu_ok", UPT // 2)
        up_ok = signal("up_ok", UPT // 2)
        dn_mm = signal("dn_mm", 2)
        o3_ok = signal("o3_ok", 2)
        stored = signal("stored", 2, 16)

        loads = [(wq0, weights["wq0"]), (wr0, weights["wr0"]), (wqk1, weights["wqk1"]), (wv1, weights["wv1"]),
                 (wp1, weights["wp1"]), (wkv2, weights["wkv2"]), (wo2, weights["wo2"]), (vec, vectors),
                 (rowc, rows), (ident, consts["ident"]), (avg8, consts["avg8"]), (avg16, consts["avg16"]),
                 (up_h, filters["up_h"]), (up_w, filters["up_w"]), (dn_h, filters["dn_h"]), (dn_w, filters["dn_w"])]
        PREP_V = 27
        PREP_P = 5

        def periods(eng, first, period, last):
            first()
            period(0, None, 1)
            with eng.Fori(1, B - 1) as b:
                period((b, 0), (b, -1), (b, 1))
            period(B - 1, B - 2, None)
            last(B - 1)

        def copied(eng, n, *images):
            if n % 4 or not isinstance(images[0], tuple):
                return images
            register = eng.alloc_register(f"image_at_step{n}")
            eng.reg_mov(register, images[0][0])
            copy = eng.snap(register, min_val=1, max_val=B - 2)
            return [(copy, away) for _, away in images]

        def row_step(n, j):
            if n % NT != NT - 1 - LEAD:
                return None
            u = n // NT + 1
            return u if u < UNITS else (0 if j is not None else None)

        block = ctx.enter_context(nc.Block())

        @block.sync
        def _(sp):
            for made in looped:
                sp.sem_inc(made.sem, START)
            for dst, src in loads:
                sp.dma_start(dst[:, 0:WIN] if dst is dn_h else dst[tuple(slice(None) for _ in dst.shape)], src).then_inc(consts_in.sem, 16)

            def load(j):
                for ct in range(CT):
                    sp.dma_start(xb[:, ct, :], x[number(j), ct * P:(ct + 1) * P, :]).then_inc(x_in.sem, 16)

            def copy_x(b, i, j):
                if i is not None:
                    sp.wait_ge(xn2_ok.sem, xn2_ok(i, 2))
                sp.dma_start(xa[:, :, :], xb[:, :, :]).then_inc(xa_in.sem, 16)
                if j is not None:
                    sp.wait_ge(xa_in.sem, xa_in(b, 1))
                    load(j)

            def stack(b, before, g, part):
                sp.wait_ge(hi1_ok.sem, hi1_ok(b, 2 * g + part + 1))
                sp.wait_ge(lo1_ok.sem, lo1_ok(b, 2 * g + part + 1))
                if before is not None:
                    sp.wait_ge(s_mm.sem, s_mm(before, STEPS * Q4 // 2 * (g + 1)))
                for h in range(Q4):
                    for r, of in enumerate(((hi1, lo1, hi1), (hi1, hi1, lo1))[part]):
                        at = slice(DH * r, DH * r + DH)
                        src = of[DH * h:DH * h + DH, part, :]
                        if part:
                            sp.dma_start(ks[at, g * Q4 + h, :].bitcast(F32), src.bitcast(F32))\
                              .then_inc(stack_ok[g].sem, 16)
                        else:
                            sp.dma_start(qs[at, 2 * g:2 * g + 2, h, :].bitcast(F32),
                                         src.bitcast(F32).rearrange("p (a n) -> p a n", a=2))\
                              .then_inc(stack_ok[g].sem, 16)

            def rows_in(b, u):
                sp.wait_ge(row_ok.sem, row_ok(b, u + 1))
                sp.dma_start(qs[STACK:STACK + 1, u, :, :].bitcast(F32), mrow[:, :].bitcast(F32))\
                    .then_inc(row_in.sem, 16)

            def store(i, ct):
                sp.wait_ge(o3_ok.sem, o3_ok(i, ct + 1))
                sp.dma_start(out[number(i), ct * P:(ct + 1) * P, :], o3[:, ct, :]).then_inc(stored.sem, 16)

            def side(name, b, i, j):
                if name == "copy_x":
                    copy_x(b, i, j)
                elif name in ("q1", "k1"):
                    stack(b, i, 1, int(name == "k1"))
                elif name in ("q0", "k0"):
                    stack(j, b, 0, int(name == "k0"))
                elif name in ("dn03", "dn13"):
                    store(i, int(name[2]))

            def first():
                load(0)
                for name in FIRST:
                    side(name, None, None, 0)
                rows_in(0, 0)

            def period(b, i, j):
                for n in range(STEPS):
                    b, i, j = copied(sp, n, b, i, j)
                    if n and row_step(n - 1, j) is not None:
                        u = row_step(n - 1, j)
                        rows_in(b if u else j, u)
                    for name in beside(n, i, j):
                        side(name, b, i, j)

            def last(i):
                for n in range(STEPS):
                    for name in SIDE[n]:
                        if not name.startswith(OF_B + OF_J) and name != "copy_x":
                            side(name, None, i, None)

            periods(sp, first, period, last)
            sp.wait_ge(stored.sem, stored(B, 0))

        @block.gpsimd
        def _(pool):
            pool.memset(minus_half[:, :], -0.5).then_inc(prep_p.sem, 1)
            pool.wait_ge(prep_p.sem, 1)
            pool.memset(vo[:, :, :, :], 1.0).then_inc(prep_p.sem, 1)
            pool.wait_ge(prep_p.sem, 2)
            pool.memset(ks[STACK:STACK + 1, :, :].bitcast(F32), -1.0).then_inc(prep_p.sem, 1)
            pool.wait_ge(prep_p.sem, 3)
            pool.wait_ge(consts_in.sem, 16 * len(loads))
            pool.tensor_scalar(inv0[:, :], vv("var"), EPS, None, ALU.add).then_inc(prep_p.sem, 1)
            pool.wait_ge(prep_p.sem, 4)
            pool.tensor_tensor(inv0[:, :], inv0[:, :], minus_half[:, :], ALU.pow).then_inc(prep_p.sem, 1)

            def side(name, b, i, j):
                if name.startswith("norm"):
                    n = int(name[4]) - 1
                    pool.wait_ge(gn_v[n].sem, gn_v[n](j if n == 0 else i, 8))
                    pool.tensor_tensor(rstd[:, n, :], gve[:, n, :], minus_half[:, :], ALU.pow).then_inc(gn_p[n].sem, 1)

            def first():
                for name in FIRST:
                    side(name, None, None, 0)

            def period(b, i, j):
                for n in range(STEPS):
                    b, i, j = copied(pool, n, b, i, j)
                    for name in beside(n, i, j):
                        side(name, b, i, j)

            def last(i):
                for n in range(STEPS):
                    for name in SIDE[n]:
                        if not name.startswith(OF_B + OF_J):
                            side(name, None, i, None)

            periods(pool, first, period, last)

        @block.vector
        def _(dve):
            dve.wait_ge(consts_in.sem, 16 * len(loads))
            dve.wait_ge(prep_p.sem, PREP_P)
            done = 0

            def prepared(ins):
                nonlocal done
                done += 1
                ins.then_inc(prep_v.sem, 1)

            for m in range(4 * 3):
                for e in range(2):
                    prepared(dve.tensor_scalar(up_m[:, m, e * UPH:(e + 1) * UPH], up_w[:, :],
                                               up_h[:, 2 * m + e:2 * m + e + 1], 4.0, ALU.mult, ALU.mult))
            for r in range(WIN):
                ins = dve.tensor_scalar(dn_m[:, r * W:(r + 1) * W], dn_w[:, :], dn_h[:, r:r + 1], None, ALU.mult)
            prepared(ins)
            dve.tensor_tensor(b_z[:, :], rowc[:, 3 * C:4 * C], rowc[:, 4 * C:5 * C], ALU.add)
            dve.tensor_scalar(wqk1[:, :, :], wqk1[:, :, :], float(DH) ** -0.25, None, ALU.mult)
            dve.tensor_scalar(vv("b_qk"), vv("b_qk"), float(DH) ** -0.25, None, ALU.mult)
            dve.tensor_tensor(inv0[:, :], inv0[:, :], vv("gamma"), ALU.mult)
            prepared(dve.tensor_tensor(add0[:, :], vv("br"), vv("mean"), ALU.subtract))
            dve.wait_ge(prep_v.sem, done)
            prepared(dve.tensor_tensor(add0[:, :], add0[:, :], inv0[:, :], ALU.mult))
            dve.wait_ge(prep_v.sem, done)
            dve.tensor_tensor(add0[:, :], add0[:, :], vv("beta"), ALU.add).then_inc(prep_v.sem, 1)
            assert done + 1 == PREP_V + 1, done
            dve.wait_ge(prep_v.sem, done + 1)

            def stepper(n, i, k):
                def step(ins):
                    nonlocal k
                    k += 1
                    ins.then_inc(gn_v[n].sem, 1)

                def last():
                    dve.wait_ge(gn_v[n].sem, gn_v[n](i, k))
                return step, last

            def stats(n, i, src):
                step, last = stepper(n, i, 0)
                for ct in range(CT):
                    for half in range(2):
                        ins = dve.bn_stats(st6[:, n, ct, half, :], src[:, ct, half * HALF:(half + 1) * HALF])
                step(ins)
                last()
                dve.memset(spare[:, :], 0.0)
                for ct in range(CT):
                    ins = dve.bn_aggr(mv[:, n, ct, :], st6[:, n, ct, :, :])
                step(ins)
                last()
                step(dve.tensor_tensor(sq[:, n, :], mv[:, n, :, 0], mv[:, n, :, 0], ALU.mult))
                last()
                step(dve.tensor_tensor(mv[:, n, :, 1], mv[:, n, :, 1], sq[:, n, :], ALU.add))

            def factors(n, i, scale, bias):
                step, last = stepper(n, i, 4)
                dve.wait_ge(gn_mm[n].sem, gn_mm[n](i, 1))
                step(dve.tensor_copy(gm[:, n, :, :], gn_ps(n)))
                last()
                step(dve.tensor_tensor(gsq[:, n, :], gm[:, n, :, 0], gm[:, n, :, 0], ALU.mult))
                step(dve.tensor_scalar(gve[:, n, :], gm[:, n, :, 1], EPS, None, ALU.add))
                last()
                step(dve.tensor_tensor(gve[:, n, :], gve[:, n, :], gsq[:, n, :], ALU.subtract))
                dve.wait_ge(gn_p[n].sem, gn_p[n](i, 1))
                step(dve.tensor_tensor(ga[:, n, :], rstd[:, n, :], vv(scale), ALU.mult))
                last()
                step(dve.tensor_tensor(gma[:, n, :], gm[:, n, :, 0], ga[:, n, :], ALU.mult))
                last()
                step(dve.tensor_tensor(gb[:, n, :], vv(bias), gma[:, n, :], ALU.subtract))
                last()

            def apply_norm(n, dst, src, ok):
                for ct in range(CT):
                    dve.tensor_scalar(dst[:, ct, :], src[:, ct, :], ga[:, n, ct:ct + 1], gb[:, n, ct:ct + 1],
                                      ALU.mult, ALU.add).then_inc(ok.sem, 1)

            def turn(j, m):
                dst, pattern = ((qT0, "p (h w) -> p h w"), (kT0, "p (h w) -> p h w"), (vT0, "p (h w) -> p w h"))[m]
                dve.wait_ge(l0_sb.sem, l0_sb(j, m + 1))
                dve.transpose(dst[:, :, :], slots0[:, m % 2, :].rearrange(pattern, h=H)).then_inc(tr0.sem, 1)

            def less_max(j):
                scores = ps[:, 6:8, :].rearrange("p a (c j) -> p (a c) j", j=32)
                dve.wait_ge(corr0.sem, corr0(j, 1))
                dve.tensor_reduce(mx0[:, :], scores, AX_X, ALU.max).then_inc(mx0_ok.sem, 1)
                dve.wait_ge(mx0_ok.sem, mx0_ok(j, 1))
                dve.wait_ge(tr0.sem, tr0(j, 3))
                dve.tensor_tensor(e0, scores, mx0[:, :].unsqueeze(2).to_broadcast([P, 32, 32]),
                                  ALU.subtract).then_inc(sub0.sem, 1)

            def weights0(j):
                dve.wait_ge(exp0.sem, exp0(j, 1))
                dve.transpose(pT0, e0).then_inc(pT0_ok.sem, 1)
                dve.tensor_reduce(sum0[:, :], e0, AX_X, ALU.add).then_inc(sum0_ok.sem, 1)
                dve.wait_ge(sum0_ok.sem, sum0_ok(j, 1))
                dve.reciprocal(sum0[:, :], sum0[:, :]).then_inc(sum0_ok.sem, 1)

            def result0(j):
                dve.wait_ge(sum0_ok.sem, sum0_ok(j, 2))
                dve.wait_ge(av0.sem, av0(j, 1))
                dve.tensor_tensor(y0, ps[:, 6:8, :].rearrange("p a (c n) -> p (a c) n", n=32),
                                  sum0[:, :].unsqueeze(2).to_broadcast([P, 32, 32]), ALU.mult).then_inc(y0_ok.sem, 1)
                dve.wait_ge(y0_ok.sem, y0_ok(j, 1))
                dve.transpose(yc0[:, :, :].rearrange("p h w -> p w h"),
                              y0.rearrange("p c w -> p w c")).then_inc(yc0_ok.sem, 1)

            def residual0(j, ct):
                dve.wait_ge(wr_mm.sem, wr_mm(j, ct + 1))
                dve.scalar_tensor_tensor(out=xb[:, ct, :], in0=both(), scalar=inv0[:, ct:ct + 1], in1=xb[:, ct, :],
                                         op0=ALU.mult, op1=ALU.add).then_inc(res0.sem, 1)
                dve.wait_ge(res0.sem, res0(j, ct + 1))
                dve.tensor_scalar(xb[:, ct, :], xb[:, ct, :], add0[:, ct:ct + 1], None, ALU.add).then_inc(x1_ok.sem, 1)

            def low(b, g, part):
                k = 2 * g + part
                dve.wait_ge(hi1_ok.sem, hi1_ok(b, k + 1))
                dve.scalar_tensor_tensor(out=lo1[:, part, :], in0=both(), scalar=v("b_qk", k),
                                         in1=hi1[:, part, :].bitcast(F32), op0=ALU.add, op1=ALU.subtract)\
                    .then_inc(lo1_ok.sem, 1)

            def values_in(b, g):
                dve.wait_ge(v1_mm.sem, v1_mm(b, g + 1))
                for m in range(2):
                    dve.tensor_tensor(vo[:, 4 * m:4 * m + 4, g * Q4:(g + 1) * Q4, 0:DH],
                                      ps[:, 6 + m, :].rearrange("p (s h d) -> p s h d", s=4, d=DH),
                                      rowc[:, g * P:(g + 1) * P].rearrange("p (s h d) -> p s h d", s=1, d=DH)
                                      .to_broadcast([P, 4, Q4, DH]), ALU.add).then_inc(v1_ok.sem, 1)

            def max_steps(b, m):
                u, s = m // NT, m % NT
                if s == 0:
                    dve.wait_ge(mxr_ok.sem, mxr_ok(b, u))
                for e in range(Q4):
                    dve.wait_ge(max_mm.sem, max_mm(b, Q4 * m + e + 1))
                    dve.tensor_reduce(mxp[:, 2 * (s % 2) + e // 2, s // 2, e % 2:e % 2 + 1],
                                      ps[:, 2 + e % 2, :], AX_X, ALU.max).then_inc(max_ok.sem, 1)

            def max_join(b, u):
                dve.wait_ge(max_ok.sem, max_ok(b, Q4 * NT * (u + 1)))
                dve.tensor_tensor(mxr[:, :, :], mxp[:, :, :, 0], mxp[:, :, :, 1], ALU.max).then_inc(mxr_ok.sem, 1)

            def row_turned(b, u):
                dve.wait_ge(row_mm.sem, row_mm(b, u + 1))
                dve.wait_ge(row_in.sem, row_in(b, u))
                dve.tensor_copy(mrow[:, :], ps[0:4 * Q4, 2, 0:P]).then_inc(row_ok.sem, 1)

            def copy_values(b, u):
                dve.wait_ge(att_ok.sem, att_ok(b, u))
                for h in range(Q4):
                    if h % 2 == 0:
                        dve.wait_ge(av_mm.sem, av_mm(b, 2 * (u + 1) * NT - 1 + h // 2))
                    at = 2 * DH * (h % 2)
                    dve.tensor_copy(av_o[DH * h:DH * h + DH, :], ps[at:at + DH, 4 + h // 2, :]).then_inc(av_o_ok.sem, 1)

            def normalise(b, u):
                g, th = u // 2, u % 2
                dve.wait_ge(av_s_ok.sem, av_s_ok(b, (u + 1) * Q4))
                dve.reciprocal(av_s[:, :], av_s[:, :]).then_inc(rec_ok.sem, 1)
                dve.wait_ge(rec_ok.sem, rec_ok(b, u + 1))
                dve.wait_ge(av_o_ok.sem, av_o_ok(b, (u + 1) * Q4))
                dve.tensor_tensor(att1[:, g, th * HALF:(th + 1) * HALF], av_o[:, :], av_s[:, :],
                                  ALU.mult).then_inc(att_ok.sem, 1)

            def residual1(i, ct):
                dve.wait_ge(proj_mm.sem, proj_mm(i, ct + 1))
                dve.wait_ge(xa_in.sem, xa_in(i, 1))
                dve.scalar_tensor_tensor(out=xa[:, ct, :], in0=both(), scalar=v("b_proj", ct), in1=xa[:, ct, :],
                                         op0=ALU.add, op1=ALU.add).then_inc(x2_ok.sem, 1)

            def kv_in(i, m):
                if m == 0:
                    dve.memset(v2[:, :, C:C + 1], 1.0).then_inc(ones2.sem, 1)
                for t in (2 * m, 2 * m + 1):
                    dve.wait_ge(kv_mm.sem, kv_mm(i, t + 1))
                    dve.tensor_tensor(k2[:, t, :], ps[:, 6 + t % 2, 0:C], rowc[:, C:2 * C], ALU.add).then_inc(kv_ok.sem, 1)
                    dve.tensor_tensor(v2[:, t, 0:C], ps[:, 6 + t % 2, C:2 * C], rowc[:, 2 * C:3 * C],
                                      ALU.add).then_inc(kv_ok.sem, 1)

            def k_maxima(i, b):
                dve.wait_ge(kv_ok.sem, kv_ok(i, 2 * NT))
                if b is not None:
                    dve.wait_ge(stack_ok[1].sem, stack_ok[1](b, 6 * Q4))
                dve.tensor_reduce(cmx[:, :], k2[:, :, :].rearrange("p t d -> p d t"), AX_X, ALU.max).then_inc(cmx_ok.sem, 1)
                dve.tensor_reduce(rmx[:, :], k2[:, :, :], AX_X, ALU.max, negate=True).then_inc(rmx_ok.sem, 1)

            def k_maxima_joined(i):
                dve.wait_ge(cmt_mm.sem, cmt_mm(i, 1))
                dve.tensor_reduce(cmc[:, :], ps[:, 6, 0:C].rearrange("p (a n) -> p a n", a=CT), AX_X, ALU.max)\
                    .then_inc(cmc_ok.sem, 1)

            def k_less_max(i):
                dve.wait_ge(cmb_mm.sem, cmb_mm(i, 1))
                dve.wait_ge(qe_ok.sem, qe_ok(i, NT))
                dve.tensor_tensor(k2[:, :, :], k2[:, :, :], ps[:, 7, 0:C].unsqueeze(1).to_broadcast([P, NT, C]),
                                  ALU.subtract).then_inc(ksub.sem, 1)
                dve.reciprocal(qrec[:, :], qsum[:, :]).then_inc(qrec_ok.sem, 1)

            def q_normalise(i):
                dve.wait_ge(qrec_ok.sem, qrec_ok(i, 1))
                for t in range(NT):
                    dve.tensor_scalar(qe[:, t, :], qe[:, t, :], qrec[:, t:t + 1], float(C) ** -0.5,
                                      ALU.mult, ALU.mult).then_inc(qn_ok.sem, 1)

            def context_in(i):
                for ct in range(CT):
                    dve.wait_ge(ctx_mm.sem, ctx_mm(i, ct + 1))
                    dve.reciprocal(crec[:, ct:ct + 1], ps[:, 6 + ct, C:C + 1]).then_inc(crec_ok.sem, 1)
                    dve.wait_ge(crec_ok.sem, crec_ok(i, ct + 1))
                    dve.tensor_scalar(ctx2[:, ct, :], ps[:, 6 + ct, 0:C], crec[:, ct:ct + 1], None,
                                      ALU.mult).then_inc(ctx_ok.sem, 1)

            def q_turned(i, m):
                for hf in range(2):
                    dve.wait_ge(qt_mm.sem, qt_mm(i, 2 * m + hf + 1))
                    dve.tensor_copy(qc[:, m, hf * HALF:(hf + 1) * HALF], ps[:, 6 + hf, :]).then_inc(qc_ok.sem, 1)

            def z_in(i, m):
                dve.wait_ge(z_mm.sem, z_mm(i, m + 1))
                dve.tensor_tensor(z3[:, 2 * m:2 * m + 2, :], ps[:, 6 + m % 2, :].rearrange("p (s c) -> p s c", s=2),
                                  b_z[:, :].unsqueeze(1).to_broadcast([P, 2, C]), ALU.add).then_inc(z_ok.sem, 1)

            def leaky(i, f):
                dve.wait_ge(relu_ok.sem, relu_ok(i, f + 1))
                tile = up3[:, 4 * (f % 8):4 * (f % 8) + 4, :].rearrange("p s c -> p (s c)")
                dve.scalar_tensor_tensor(out=tile, in0=ps[:, 6 + f % 2, :], scalar=SLOPE * ROOT2, in1=tile,
                                         op0=ALU.mult, op1=ALU.add).then_inc(up_ok.sem, 1)

            def side(name, b, i, j):
                digit = int(name[-1]) if name[-1].isdigit() else None
                if name in ("l0q", "l0k", "l0v"):
                    turn(j, "qkv".index(name[2]))
                elif name == "soft0":
                    less_max(j)
                    weights0(j)
                elif name == "av3":
                    result0(j)
                elif name in ("wr0", "wr1"):
                    residual0(j, digit)
                elif name == "stats1":
                    dve.wait_ge(x1_ok.sem, x1_ok(j, 2))
                    stats(0, j, xb)
                elif name == "norm1":
                    factors(0, j, "gn1_scale", "gn1_bias")
                    if b is not None:
                        dve.wait_ge(v1_mm.sem, v1_mm(b, 2))
                    apply_norm(0, xn1, xb, xn1_ok)
                elif name in ("q0", "k0"):
                    low(j, 0, int(name == "k0"))
                elif name in ("q1", "k1"):
                    low(b, 1, int(name == "k1"))
                elif name == "v0":
                    values_in(j, 0)
                elif name == "v1":
                    values_in(b, 1)
                elif name in ("proj0", "proj1"):
                    residual1(i, digit)
                elif name == "stats2":
                    dve.wait_ge(x2_ok.sem, x2_ok(i, 2))
                    stats(1, i, xa)
                elif name == "norm2":
                    factors(1, i, "gn2_scale", "gn2_bias")
                    dve.wait_ge(stored.sem, stored(i, 0))
                    apply_norm(1, xn2, xa, xn2_ok)
                elif name.startswith("kv"):
                    kv_in(i, digit)
                elif name == "kmax":
                    k_maxima(i, b)
                elif name == "kmaxT":
                    k_maxima_joined(i)
                elif name == "ke":
                    k_less_max(i)
                    q_normalise(i)
                elif name == "context":
                    context_in(i)
                elif name in ("qT0", "qT1"):
                    q_turned(i, digit)
                elif name == "stats3":
                    dve.wait_ge(o2_ok.sem, o2_ok(i, 2))
                    stats(2, i, o2)
                elif name == "norm3":
                    factors(2, i, "gn3_scale", "gn3_bias")
                elif name.startswith("z"):
                    z_in(i, digit)
                elif name.startswith("up"):
                    for f in range(4):
                        leaky(i, 8 * int(name[2]) + 4 * digit + f)

            def first():
                for name in FIRST:
                    side(name, None, None, 0)
                for m in range(NT):
                    max_steps(0, m)
                max_join(0, 0)
                row_turned(0, 0)
                for m in range(NT, NT + LEAD):
                    max_steps(0, m)

            def period(b, i, j):
                for n in range(STEPS):
                    b, i, j = copied(dve, n, b, i, j)
                    if n and row_step(n - 1, j) is not None:
                        u = row_step(n - 1, j)
                        row_turned(b if u else j, u)
                    if n == 0 and i is not None:
                        copy_values(i, UNITS - 1)
                        normalise(i, UNITS - 1)
                    elif n and n % NT == 0:
                        copy_values(b, n // NT - 1)
                        normalise(b, n // NT - 1)
                    m = n + NT + LEAD
                    if m < STEPS:
                        max_steps(b, m)
                    elif j is not None:
                        max_steps(j, m - STEPS)
                    u = row_step(n, j)
                    if u is not None:
                        max_join(b if u else j, u)
                    for name in beside(n, i, j):
                        side(name, b, i, j)

            def last(i):
                copy_values(i, UNITS - 1)
                normalise(i, UNITS - 1)
                for n in range(STEPS):
                    for name in SIDE[n]:
                        if not name.startswith(OF_B + OF_J):
                            side(name, None, i, None)

            periods(dve, first, period, last)

        @block.scalar
        def _(act):
            act.wait_ge(consts_in.sem, 16 * len(loads))
            act.wait_ge(prep_v.sem, PREP_V + 1)

            def exponentials(b, i, n):
                for h in range(Q4):
                    k = Q4 * n + h
                    if h % 2 == 0:
                        if n > 0:
                            act.wait_ge(av_mm.sem, av_mm(b, 2 * (n - 1) + h // 2 + 1))
                        elif i is not None:
                            act.wait_ge(av_mm.sem, av_mm(i, 2 * (STEPS - 1) + h // 2 + 1))
                    act.wait_ge(s_mm.sem, s_mm(b, k + 1))
                    act.activation(prob[:, h, :], ps[:, k % 2, :], ACT.Exp).then_inc(p_ok.sem, 1)

            def copy_sums(b, u):
                act.wait_ge(att_ok.sem, att_ok(b, u))
                for h in range(Q4):
                    if h % 2 == 0:
                        act.wait_ge(av_mm.sem, av_mm(b, 2 * (u + 1) * NT - 1 + h // 2))
                    at = 2 * DH * (h % 2) + DH
                    act.activation(av_s[DH * h:DH * h + DH, :], ps[at:at + DH, 4 + h // 2, :], ACT.Copy)\
                        .then_inc(av_s_ok.sem, 1)

            def qkv0(j, b, m):
                act.wait_ge(l0_mm.sem, l0_mm(j, m + 1))
                if m == 0 and b is not None:
                    act.wait_ge(stack_ok[1].sem, stack_ok[1](b, 6 * Q4))
                if m == 2:
                    act.wait_ge(tr0.sem, tr0(j, 1))
                act.activation(slots0[:, m % 2, :], both(), ACT.Identity, bias=v(("bq", "bk", "bv")[m]))\
                    .then_inc(l0_sb.sem, 1)

            def high(b, g, part):
                k = 2 * g + part
                act.wait_ge(qk1_mm.sem, qk1_mm(b, k + 1))
                if g == 1:
                    act.wait_ge(stack_ok[0].sem, stack_ok[0](b, 6 * Q4))
                act.activation(hi1[:, part, :], both(), ACT.Identity, bias=v("b_qk", k)).then_inc(hi1_ok.sem, 1)

            def side(name, b, i, j):
                digit = int(name[-1]) if name[-1].isdigit() else None
                if name in ("l0q", "l0k", "l0v"):
                    qkv0(j, b, "qkv".index(name[2]))
                elif name == "soft0":
                    act.wait_ge(sub0.sem, sub0(j, 1))
                    act.activation(e0, e0, ACT.Exp).then_inc(exp0.sem, 1)
                elif name in ("q0", "k0"):
                    high(j, 0, int(name == "k0"))
                elif name in ("q1", "k1"):
                    high(b, 1, int(name == "k1"))
                elif name == "kmax":
                    act.wait_ge(rmx_ok.sem, rmx_ok(i, 1))
                    for t in range(NT):
                        act.activation(qe[:, t, :], k2[:, t, :], ACT.Exp, bias=rmx[:, t:t + 1],
                                       accum_out=qsum[:, t:t + 1]).then_inc(qe_ok.sem, 1)
                elif name == "ke":
                    act.wait_ge(ksub.sem, ksub(i, 1))
                    act.activation(k2[:, :, :], k2[:, :, :], ACT.Exp).then_inc(ke_ok.sem, 1)
                elif name in ("o20", "o21"):
                    act.wait_ge(o2_mm.sem, o2_mm(i, digit + 1))
                    act.activation(o2[:, digit, :], both(), ACT.Copy).then_inc(o2_ok.sem, 1)
                elif name == "norm3":
                    act.wait_ge(gn_v[2].sem, gn_v[2](i, 11))
                    for ct in range(CT):
                        act.activation(o2[:, ct, :], o2[:, ct, :], ACT.Gelu, bias=gb[:, 2, ct:ct + 1],
                                       scale=ga[:, 2, ct:ct + 1]).then_inc(g2_ok.sem, 1)
                elif name.startswith("up"):
                    for f in range(8 * int(name[2]) + 4 * digit, 8 * int(name[2]) + 4 * digit + 4):
                        act.wait_ge(up_mm.sem, up_mm(i, f + 1))
                        act.activation(up3[:, 4 * (f % 8):4 * (f % 8) + 4, :].rearrange("p s c -> p (s c)"),
                                       ps[:, 6 + f % 2, :], ACT.Relu, scale=(1.0 - SLOPE) * ROOT2)\
                            .then_inc(relu_ok.sem, 1)
                elif name in ("dn03", "dn13"):
                    ct = int(name[2])
                    act.wait_ge(dn_mm.sem, dn_mm(i, ct + 1))
                    act.activation(o3[:, ct, :], both(), ACT.Copy).then_inc(o3_ok.sem, 1)

            def first():
                for name in FIRST:
                    side(name, None, None, 0)

            def period(b, i, j):
                for n in range(STEPS):
                    b, i, j = copied(act, n, b, i, j)
                    if n == 0 and i is not None:
                        copy_sums(i, UNITS - 1)
                    elif n and n % NT == 0:
                        copy_sums(b, n // NT - 1)
                    exponentials(b, i, n)
                    for name in beside(n, i, j):
                        side(name, b, i, j)

            def last(i):
                copy_sums(i, UNITS - 1)
                for n in range(STEPS):
                    for name in SIDE[n]:
                        if not name.startswith(OF_B + OF_J):
                            side(name, None, i, None)

            periods(act, first, period, last)

        @block.tensor
        def _(pe):
            pe.wait_ge(consts_in.sem, 16 * len(loads))
            pe.wait_ge(prep_p.sem, PREP_P)
            pe.wait_ge(prep_v.sem, PREP_V + 1)

            def product(dst, pairs):
                for n, (lhsT, rhs) in enumerate(pairs):
                    ins = pe.matmul(dst, lhsT, rhs, start=(n == 0), stop=(n == len(pairs) - 1))
                return ins

            def both_halves(weights, src, signal):
                for hf in range(2):
                    ins = product(ps[:, 6 + hf, :], [(w, s[:, hf * HALF:(hf + 1) * HALF]) for w, s in zip(weights, src)])
                ins.then_inc(signal.sem, 1)

            def channel_tiles(t):
                return [t[:, ct, :] for ct in range(CT)]

            def average(n, i, matrix):
                pe.wait_ge(gn_v[n].sem, gn_v[n](i, 4))
                pe.matmul(gn_ps(n), matrix[:, :], mv[:, n, :, :], start=True, stop=True).then_inc(gn_mm[n].sem, 1)

            def logits(b, n, pair, i):
                u, s = n // NT, n % NT
                for h in (2 * pair, 2 * pair + 1):
                    k = Q4 * n + h
                    if k >= 2:
                        pe.wait_ge(p_ok.sem, p_ok(b, k - 1))
                    elif i is not None:
                        pe.wait_ge(p_ok.sem, p_ok(i, STEPS * Q4 + k - 1))
                    if s == 0 and h == 0:
                        pe.wait_ge(row_in.sem, row_in(b, u + 1))
                    pe.matmul(ps[:, k % 2, :], ks[0:STACK + 1, (u // 2) * Q4 + h, s * P:(s + 1) * P],
                              qs[0:STACK + 1, u, h, :], start=True, stop=True).then_inc(s_mm.sem, 1)

            def max_products(b, m, pair, i=None):
                u, s = m // NT, m % NT
                if m in (0, STEPS // 2) and pair == 0:
                    pe.wait_ge(stack_ok[u // 2].sem, stack_ok[u // 2](b, 6 * Q4))
                for e in (2 * pair, 2 * pair + 1):
                    k = Q4 * m + e
                    if k >= 2:
                        pe.wait_ge(max_ok.sem, max_ok(b, k - 1))
                    elif i is not None:
                        pe.wait_ge(max_ok.sem, max_ok(i, STEPS * Q4 + k - 1))
                    head = 2 * (s % 2) + e // 2
                    pe.matmul(ps[:, 2 + e % 2, :], qs[0:STACK, u, head, (s // 2) * P:(s // 2 + 1) * P],
                              ks[0:STACK, (u // 2) * Q4 + head, (e % 2) * HALF:(e % 2 + 1) * HALF],
                              start=True, stop=True).then_inc(max_mm.sem, 1)

            def rows(b, u):
                pe.wait_ge(mxr_ok.sem, mxr_ok(b, u + 1))
                pe.transpose(ps[0:4 * Q4, 2, 0:P], mxr[:, :, :].rearrange("p h t -> p (h t)"), ident[:, :])\
                  .then_inc(row_mm.sem, 1)

            def rows_gone(b, u):
                pe.wait_ge(row_ok.sem, row_ok(b, u + 1))

            def values(b, n, pair, i=None):
                u, s = n // NT, n % NT
                pe.wait_ge(p_ok.sem, p_ok(b, Q4 * n + 2 * pair + 2))
                if s == 0 and n > 0:
                    pe.wait_ge(av_o_ok.sem, av_o_ok(b, Q4 * (u - 1) + 2 * pair + 2))
                    pe.wait_ge(av_s_ok.sem, av_s_ok(b, Q4 * (u - 1) + 2 * pair + 2))
                elif n == 0 and i is not None:
                    pe.wait_ge(av_o_ok.sem, av_o_ok(i, Q4 * (UNITS - 1) + 2 * pair + 2))
                    pe.wait_ge(av_s_ok.sem, av_s_ok(i, Q4 * (UNITS - 1) + 2 * pair + 2))
                for e in range(2):
                    ins = pe.matmul(ps[2 * DH * e:2 * DH * (e + 1), 4 + pair, :], vo[:, s, (u // 2) * Q4 + 2 * pair + e, :],
                                    prob[:, 2 * pair + e, :], start=(s == 0), stop=(s == NT - 1))
                ins.then_inc(av_mm.sem, 1)

            def qkv0(b, i, j, m):
                if m == 0:
                    pe.wait_ge(x_in.sem, x_in(j, 2))
                    if i is not None:
                        pe.wait_ge(ksub.sem, ksub(i, 1))
                    elif b is not None:
                        pe.wait_ge(v1_ok.sem, v1_ok(b, 4))
                else:
                    pe.wait_ge(l0_sb.sem, l0_sb(j, m))
                both_halves([wq0[:, kt, m * CR:(m + 1) * CR] for kt in range(CT)], channel_tiles(xb), l0_mm)

            def one_column(bank):
                pe.matmul(ps[:, bank, 0:1], ident[:, :], ident[:, 0:1], start=True, stop=True)

            def scores0(j, q):
                if q == 0:
                    pe.wait_ge(l0_sb.sem, l0_sb(j, 3))
                    pe.wait_ge(tr0.sem, tr0(j, 2))
                    one_column(6)
                at = slice(32 * q, 32 * q + 32)
                for c in range(32):
                    ins = pe.matmul(ps[at, 6 + c // 16, 32 * (c % 16):32 * (c % 16) + 32],
                                    qT0[at, :, c], kT0[at, :, c], start=True, stop=True)
                if q == Q4 - 1:
                    ins.then_inc(corr0.sem, 1)

            def values0(i, j, q):
                if q == 0:
                    pe.wait_ge(tr0.sem, tr0(j, 3))
                    if i is not None:
                        pe.wait_ge(ctx_ok.sem, ctx_ok(i, CT))
                    pe.wait_ge(pT0_ok.sem, pT0_ok(j, 1))
                    one_column(6)
                at = slice(32 * q, 32 * q + 32)
                for c in range(32):
                    ins = pe.matmul(ps[at, 6 + c // 16, 32 * (c % 16):32 * (c % 16) + 32],
                                    pT0[at, c, :], vT0[at, :, c], start=True, stop=True)
                if q == Q4 - 1:
                    ins.then_inc(av0.sem, 1)

            def wr(i, j, ct):
                if ct == 0:
                    pe.wait_ge(yc0_ok.sem, yc0_ok(j, 1))
                    if i is not None:
                        pe.wait_ge(qc_ok.sem, qc_ok(i, 4))
                else:
                    pe.wait_ge(res0.sem, res0(j, 1))
                both_halves([wr0[:, ct * P:(ct + 1) * P]], [yc0[:, :, :].rearrange("p h w -> p (h w)")], wr_mm)

            def qk1(b, i, g, part):
                k = 2 * g + part
                if part == 1:
                    pe.wait_ge(lo1_ok.sem, lo1_ok(b, k))
                    if g == 0 and i is not None:
                        pe.wait_ge(gn_v[2].sem, gn_v[2](i, 5))
                elif g == 0:
                    pe.wait_ge(xn1_ok.sem, xn1_ok(b, 2))
                    if i is not None:
                        pe.wait_ge(o2_ok.sem, o2_ok(i, 2))
                else:
                    pe.wait_ge(v1_ok.sem, v1_ok(b, 2))
                    if i is not None:
                        pe.wait_ge(o3_ok.sem, o3_ok(i, 0))
                both_halves([wqk1[:, kt, k * P:(k + 1) * P] for kt in range(CT)], channel_tiles(xn1), qk1_mm)

            def v1(b, g):
                pe.wait_ge(lo1_ok.sem, lo1_ok(b, 2 * g + 2))
                for t in range(NT):
                    ins = product(ps[:, 6 + t // 4, (t % 4) * P:(t % 4 + 1) * P],
                                  [(xn1[:, kt, t * P:(t + 1) * P], wv1[:, kt, g * P:(g + 1) * P]) for kt in range(CT)])
                ins.then_inc(v1_mm.sem, 1)

            def proj(b, i, ct):
                if ct == 0:
                    if b is not None:
                        pe.wait_ge(v1_ok.sem, v1_ok(b, 4))
                    else:
                        pe.wait_ge(o3_ok.sem, o3_ok(i, 0))
                    pe.wait_ge(att_ok.sem, att_ok(i, UNITS))
                else:
                    pe.wait_ge(x2_ok.sem, x2_ok(i, 1))
                both_halves([wp1[:, kt, ct * P:(ct + 1) * P] for kt in range(CT)], channel_tiles(att1), proj_mm)

            def kv(i, m):
                if m == 0:
                    pe.wait_ge(xn2_ok.sem, xn2_ok(i, 2))
                for t in (2 * m, 2 * m + 1):
                    if t >= 2:
                        pe.wait_ge(kv_ok.sem, kv_ok(i, 2 * (t - 1)))
                    product(ps[:, 6 + t % 2, :],
                            [(xn2[:, kt, t * P:(t + 1) * P], wkv2[:, kt, :]) for kt in range(CT)]).then_inc(kv_mm.sem, 1)

            def maxima_turned(i):
                pe.wait_ge(cmx_ok.sem, cmx_ok(i, 1))
                for ct in range(CT):
                    ins = pe.transpose(ps[:, 6, ct * P:(ct + 1) * P], cmx[:, ct * P:(ct + 1) * P], ident[:, :])
                ins.then_inc(cmt_mm.sem, 1)

            def maxima_spread(i):
                pe.wait_ge(cmc_ok.sem, cmc_ok(i, 1))
                for ct in range(CT):
                    ins = pe.matmul(ps[:, 7, ct * P:(ct + 1) * P], cmc[:, ct:ct + 1].to_broadcast([P, P]),
                                    ident[:, :], start=True, stop=True)
                ins.then_inc(cmb_mm.sem, 1)

            def context(i, j):
                pe.wait_ge(ke_ok.sem, ke_ok(i, 1))
                if j is not None:
                    pe.wait_ge(sub0.sem, sub0(j, 1))
                for ct in range(CT):
                    product(ps[:, 6 + ct, 0:C + 1],
                            [(k2[:, t, ct * P:(ct + 1) * P], v2[:, t, :]) for t in range(NT)]).then_inc(ctx_mm.sem, 1)

            def q_turned(i, j, m):
                if m == 0:
                    pe.wait_ge(qn_ok.sem, qn_ok(i, NT))
                    if j is not None:
                        pe.wait_ge(y0_ok.sem, y0_ok(j, 1))
                    else:
                        pe.wait_ge(ctx_ok.sem, ctx_ok(i, CT))
                for hf in range(2):
                    if m == 1:
                        pe.wait_ge(qc_ok.sem, qc_ok(i, 1 + hf))
                    for t in range(4):
                        ins = pe.transpose(ps[:, 6 + hf, t * P:(t + 1) * P], qe[:, 4 * hf + t, m * P:(m + 1) * P],
                                           ident[:, :])
                    ins.then_inc(qt_mm.sem, 1)

            def o2_product(i, j, ct):
                if ct == 0:
                    pe.wait_ge(qc_ok.sem, qc_ok(i, 4))
                    if j is not None:
                        pe.wait_ge(res0.sem, res0(j, 2))
                else:
                    pe.wait_ge(o2_ok.sem, o2_ok(i, 1))
                    if j is not None:
                        pe.wait_ge(gn_v[0].sem, gn_v[0](j, 5))
                both_halves([ctx2[:, kt, ct * P:(ct + 1) * P] for kt in range(CT)], channel_tiles(qc), o2_mm)

            def z_product(i, j, m):
                if m == 0:
                    pe.wait_ge(g2_ok.sem, g2_ok(i, 2))
                    if j is not None:
                        pe.wait_ge(v1_ok.sem, v1_ok(j, 2))
                if m >= 2:
                    pe.wait_ge(z_ok.sem, z_ok(i, m - 1))
                for s in range(2):
                    at = slice((2 * m + s) * P, (2 * m + s + 1) * P)
                    for kt in range(CT):
                        pe.matmul(ps[:, 6 + m % 2, s * C:(s + 1) * C], o2[:, kt, at], wo2[:, kt, :],
                                  start=(kt == 0 and s == 0), stop=False, skip_group_check=True)
                    for kt in range(CT):
                        ins = pe.matmul(ps[:, 6 + m % 2, s * C + kt * P:s * C + (kt + 1) * P], xn2[:, kt, at],
                                        ident[:, :], start=False, stop=True, skip_group_check=True)
                ins.then_inc(z_mm.sem, 1)

            def up(i, f):
                ct = f // 8
                if f == 0:
                    pe.wait_ge(z_ok.sem, z_ok(i, 4))
                elif f == 8:
                    pe.wait_ge(o3_ok.sem, o3_ok(i, 1))
                elif f != 1 and f != 9:
                    pe.wait_ge(up_ok.sem, up_ok(i, f - 1))
                for m in range(4):
                    t = 4 * (f % 8) + m
                    tiles = [(t // 4 + d, 3 * (t % 4) + d + 1) for d in (-1, 0, 1)
                             if 0 <= t // 4 + d < NT and t - REACH < 4 * (t // 4 + d) + 4 and t + REACH >= 4 * (t // 4 + d)]
                    ins = product(ps[:, 6 + f % 2, m * P:(m + 1) * P],
                                  [(up_m[:, k, :], z3[:, s, ct * P:(ct + 1) * P]) for s, k in tiles])
                ins.then_inc(up_mm.sem, 1)

            def down(i, ct, part):
                if part == 0:
                    pe.wait_ge(up_ok.sem, up_ok(i, 8 * ct + 8))
                for t in range(8 * part, 8 * part + 8):
                    lo, hi = max(t - REACH, 0), min(t + REACH + 1, H)
                    for bank in range(2):
                        r, e = max(lo, 16 * bank), min(hi, 16 * bank + 16)
                        if r >= e:
                            continue
                        at = (r - (t - REACH)) * W
                        ins = pe.matmul(ps[:, 6 + bank, (r - 16 * bank) * W:(e - 16 * bank) * W],
                                        up3[:, t, :], dn_m[:, at:at + (e - r) * W],
                                        start=(t == (0, 16 - REACH)[bank]), stop=(t == (15 + REACH, UPT - 1)[bank]),
                                        skip_group_check=True)
                if part == 3:
                    ins.then_inc(dn_mm.sem, 1)

            def side(name, b, i, j):
                digit = int(name[-1]) if name[-1].isdigit() else None
                if name in ("l0q", "l0k", "l0v"):
                    qkv0(b, i, j, "qkv".index(name[2]))
                elif name.startswith("corr"):
                    scores0(j, digit)
                elif name.startswith("av"):
                    values0(i, j, digit)
                elif name in ("wr0", "wr1"):
                    wr(i, j, digit)
                elif name == "norm1":
                    if i is not None:
                        pe.wait_ge(o2_ok.sem, o2_ok(i, 1))
                    average(0, j, avg8)
                elif name in ("q0", "k0"):
                    qk1(j, i, 0, int(name == "k0"))
                elif name in ("q1", "k1"):
                    qk1(b, i, 1, int(name == "k1"))
                elif name == "v0":
                    v1(j, 0)
                elif name == "v1":
                    v1(b, 1)
                elif name in ("proj0", "proj1"):
                    proj(b, i, digit)
                elif name == "norm2":
                    average(1, i, avg16)
                elif name == "norm3":
                    if j is not None:
                        pe.wait_ge(lo1_ok.sem, lo1_ok(j, 1))
                    average(2, i, avg16)
                elif name.startswith("kv"):
                    kv(i, digit)
                elif name == "kmaxT":
                    maxima_turned(i)
                elif name == "ke":
                    maxima_spread(i)
                elif name == "context":
                    context(i, j)
                elif name in ("qT0", "qT1"):
                    q_turned(i, j, digit)
                elif name in ("o20", "o21"):
                    o2_product(i, j, digit)
                elif name.startswith("z"):
                    z_product(i, j, digit)
                elif name.startswith("up"):
                    for f in range(8 * int(name[2]) + 4 * digit, 8 * int(name[2]) + 4 * digit + 4):
                        up(i, f)
                elif name.startswith("dn"):
                    down(i, int(name[2]), digit)

            def first():
                for name in FIRST:
                    side(name, None, None, 0)
                for m in range(NT):
                    max_products(0, m, 0)
                    max_products(0, m, 1)
                pe.wait_ge(max_ok.sem, max_ok(0, Q4 * NT))
                rows(0, 0)
                rows_gone(0, 0)
                for m in range(NT, NT + LEAD):
                    max_products(0, m, 0)
                    max_products(0, m, 1)

            def period(b, i, j):
                for n in range(STEPS):
                    b, i, j = copied(pe, n, b, i, j)
                    for pair in range(2):
                        logits(b, n, pair, i)
                        if pair == 0 and n and row_step(n - 1, j) is not None:
                            u = row_step(n - 1, j)
                            rows(b if u else j, u)
                            rows_gone(b if u else j, u)
                        m = n + NT + LEAD
                        if m < STEPS:
                            max_products(b, m, pair)
                        elif j is not None:
                            max_products(j, m - STEPS, pair, b)
                        if pair == 1:
                            values(b, n, 0, i)
                        elif n > 0:
                            values(b, n - 1, 1, i)
                        elif i is not None:
                            values(i, STEPS - 1, 1)
                    for name in beside(n, i, j):
                        side(name, b, i, j)

            def last(i):
                values(i, STEPS - 1, 1)
                for n in range(STEPS):
                    for name in SIDE[n]:
                        if not name.startswith(OF_B + OF_J):
                            side(name, None, i, None)

            periods(pe, first, period, last)


def kernel(x, **w):
    import numpy as np
    import concourse.bacc as bacc
    from concourse.bass_utils import run_bass_kernel_spmd

    def tiles(a):
        a = np.asarray(a)
        return np.ascontiguousarray(a.reshape(-1, P, a.shape[-1]).transpose(1, 0, 2))

    def toeplitz(taps, index):
        padded = np.concatenate([np.asarray(taps)[::-1], np.zeros(1, np.float32)])
        return padded[np.where((index >= 0) & (index < TAPS), index, TAPS)]

    a = {k: np.asarray(v) for k, v in w.items()}
    x = np.asarray(x)
    L0, L1, L2, L3 = "L0_conv_", "L1_conv_", "L2_conv_", "L3_conv_"
    arrays = {"x": np.ascontiguousarray(x.reshape(B, C, N))}
    arrays["wq0"] = tiles(np.concatenate([a[L0 + "Wq"], a[L0 + "Wk"], a[L0 + "Wv"]]).T)
    arrays["wr0"] = np.ascontiguousarray(a[L0 + "Wr"].T)
    qkv = a[L1 + "w_qkv"].reshape(GROUPS4, Q4, 3, DH, C)
    arrays["wqk1"] = tiles(qkv[:, :, 0:2].transpose(0, 2, 1, 3, 4).reshape(4 * P, C).T)
    arrays["wv1"] = tiles(qkv[:, :, 2].reshape(C, C).T)
    arrays["wp1"] = tiles(a[L1 + "w_proj"].T)
    arrays["wkv2"] = tiles(a[L2 + "kv_w"].T)
    arrays["wo2"] = tiles(a[L2 + "out_w"].T)
    b_qkv = a[L1 + "b_qkv"].reshape(GROUPS4, Q4, 3, DH)
    vectors = {"bq": a[L0 + "bq"], "bk": a[L0 + "bk"], "bv": a[L0 + "bv"], "br": a[L0 + "br"],
               "gamma": a[L0 + "gamma"], "beta": a[L0 + "beta"], "mean": a[L0 + "running_mean"],
               "var": a[L0 + "running_var"], "gn1_scale": a[L1 + "gn_scale"], "gn1_bias": a[L1 + "gn_bias"],
               "b_qk": b_qkv[:, :, 0:2].transpose(0, 2, 1, 3).reshape(-1), "b_proj": a[L1 + "b_proj"],
               "gn2_scale": a[L2 + "norm1_w"], "gn2_bias": a[L2 + "norm1_b"],
               "gn3_scale": a[L2 + "norm2_w"], "gn3_bias": a[L2 + "norm2_b"]}
    arrays["vectors"] = np.ascontiguousarray(np.concatenate([vectors[k].reshape(-1, P) for k in VEC]).T)
    row = np.concatenate([b_qkv[:, :, 2].reshape(-1), a[L2 + "kv_b"], a[L2 + "out_b"], a[L3 + "bias"]])
    arrays["rows"] = np.ascontiguousarray(np.broadcast_to(row, (P, row.size)))

    lane = np.arange(P)
    h4, w4 = lane // W, lane % W
    r, d, e = (i.reshape(-1) for i in np.meshgrid(np.arange(4), np.arange(-1, 2), np.arange(2), indexing="ij"))
    up = a[L3 + "up_filter"]
    arrays["up_h"] = toeplitz(up, 2 * (4 * d[None] + h4[:, None]) - (2 * r + e)[None] + 6)
    arrays["up_w"] = toeplitz(up, 2 * w4[:, None] - np.arange(UPH)[None] + 6)
    down = a[L3 + "down_filter"]
    e2, w2 = lane // UPH, lane % UPH
    arrays["dn_h"] = toeplitz(down, e2[:, None] - 2 * np.arange(WIN)[None] + 11)
    arrays["dn_w"] = toeplitz(down, w2[:, None] - 2 * np.arange(W)[None] + 5)

    arrays["ident"] = np.eye(P, dtype=np.float32)
    for name, size in (("avg8", 8), ("avg16", 16)):
        arrays[name] = np.kron(np.eye(P // size), np.full((size, size), 1.0 / size)).astype(np.float32)

    nc = bacc.Bacc("TRN2", target_bir_lowering=False, num_devices=1)
    ap = {k: nc.dram_tensor("in_" + k, t.shape, mybir.dt.from_np(t.dtype), kind="ExternalInput").ap()
          for k, t in arrays.items()}
    out = nc.dram_tensor("out", (B, C, N), F32, kind="ExternalOutput").ap()
    chain_kernel(nc, ap["x"], ap, ap["vectors"], ap["rows"], ap, ap, out)
    got = run_bass_kernel_spmd(nc, [{"in_" + k: t for k, t in arrays.items()}], core_ids=[0])
    return got.results[0]["out"].reshape(B, C, H, W)
```

```python
from contextlib import ExitStack

import concourse.bass as bass
from concourse import mybir

ALU = mybir.AluOpType
ACT = mybir.ActivationFunctionType
AX_X = mybir.AxisListType.X
F32 = mybir.dt.float32
F32R = mybir.dt.float32r

B, C, H, W = 16, 256, 32, 32
P = 128
CT = C // P
N = H * W
HALF = N // 2
NT = N // P
CR = C // 2
Q4 = 4
HEADS, DH = 8, 32
GROUPS4 = HEADS // Q4
UNITS = GROUPS4 * 2
STACK = 3 * DH
EPS = 1e-5
UPH = 2 * H
UPT = UPH // 2
TAPS = 12
REACH = 3
WIN = 2 * REACH + 1
ROOT2 = float(2.0 ** 0.5)
SLOPE = 0.2

VEC = {}
for _name, _n in (("bq", 1), ("bk", 1), ("bv", 1), ("br", CT), ("gamma", CT), ("beta", CT), ("mean", CT), ("var", CT),
                  ("gn1_scale", CT), ("gn1_bias", CT), ("b_qk", 2 * GROUPS4), ("b_proj", CT),
                  ("gn2_scale", CT), ("gn2_bias", CT), ("gn3_scale", CT), ("gn3_bias", CT)):
    VEC[_name] = (sum(n for _, n in VEC.values()), _n)
NVEC = sum(n for _, n in VEC.values())


LEAD = 2
STEPS = UNITS * NT

SIDE = {
    0: ["q1"], 1: ["k1"], 3: ["proj0"], 4: ["proj1"], 5: ["stats2a"], 6: ["stats2b", "v1"], 7: ["norm2a"],
    8: ["norm2b", "copy_x"], 9: ["kv0"], 10: ["kv1"], 11: ["kv2"], 12: ["kv3"], 13: ["kmax0"], 14: ["kmax1"],
    15: ["kmaxT", "rmax0"], 16: ["spread", "rmax1"], 17: ["l0q", "qe0"], 18: ["l0k", "qe1"], 19: ["l0v", "ksub0"],
    20: ["corr0", "kexp0", "ksub1"], 21: ["corr1", "kexp1"], 22: ["corr2", "corr3", "qn"], 23: ["soft0"],
    24: ["soft1"], 25: ["context0"], 26: ["soft2", "context1"], 27: ["av0"], 28: ["av1"], 29: ["av2", "av3"],
    31: ["qT0"], 32: ["qT1"], 33: ["wr0"], 34: ["wr1"], 35: ["o20", "stats1a"], 36: ["o21", "stats1b"],
    37: ["norm1a", "stats3a"], 38: ["norm1b", "stats3b"], 39: ["q0"], 40: ["norm3a", "k0"], 41: ["norm3b"],
    42: ["v0", "gelu"], 44: ["z0"], 45: ["z1"], 46: ["z2"], 47: ["z3"],
    48: ["up0", "up1"], 49: ["up2", "up3"], 50: ["up4", "up5"], 51: ["up6", "up7"],
    52: ["dn00"], 53: ["dn01"], 54: ["dn02"], 55: ["dn03"],
    56: ["up8", "up9"], 57: ["up10", "up11"], 58: ["up12", "up13"], 59: ["up14", "up15"],
    60: ["dn10"], 61: ["dn11"], 62: ["dn12"], 63: ["dn13"],
}
OF_B, OF_J = ("q1", "k1", "v1"), ("l0", "corr", "soft", "av", "wr", "stats1", "norm1", "q0", "k0", "v0")
FIRST = [name for names in SIDE.values() for name in names if name.startswith(OF_J)]


def beside(n, i, j):
    for name in SIDE.get(n, ()):
        if name == "copy_x" or name.startswith(OF_B) or (i is not None and not name.startswith(OF_J)) \
                or (j is not None and name.startswith(OF_J)):
            yield name


START = 1


class Signal:

    def __init__(self, sem, per_image, size=1):
        self.sem, self.per_image, self.size = sem, per_image, size

    def __call__(self, image, k):
        image, away = image if isinstance(image, tuple) else (image, 0)
        return image * (self.per_image * self.size) + ((away * self.per_image + k) * self.size + START)


def number(image):
    return image[0] + image[1] if isinstance(image, tuple) else image


def chain_kernel(nc, x, weights, vectors, rows, filters, consts, out):
    with ExitStack() as ctx:
        def sb(name, shape, dt=F32, over=None):
            return (over or ctx).enter_context(nc.sbuf_tensor(name, shape, dt))

        looped = []

        def signal(name, per_image, size=1):
            made = Signal(ctx.enter_context(nc.semaphore(name)), per_image, size)
            if per_image:
                looped.append(made)
            return made

        ps = ctx.enter_context(nc.psum_tensor("ps", [P, 8, HALF], F32))

        wq0 = sb("wq0", [P, CT, 3 * CR])
        wr0 = sb("wr0", [P, C])
        wqk1 = sb("wqk1", [P, CT, 4 * P])
        wv1 = sb("wv1", [P, CT, C])
        wp1 = sb("wp1", [P, CT, C])
        wkv2 = sb("wkv2", [P, CT, 2 * C])
        wo2 = sb("wo2", [P, CT, C])
        vec = sb("vec", [P, NVEC])
        rowc = sb("rowc", [P, 5 * C])
        ident = sb("ident", [P, P])
        avg8 = sb("avg8", [P, P])
        avg16 = sb("avg16", [P, P])
        up_m = sb("up_m", [P, 4 * 3, P])
        dn_m = sb("dn_m", [P, WIN * W])
        inv0 = sb("inv0", [P, CT])
        add0 = sb("add0", [P, CT])
        minus_half = sb("minus_half", [P, CT])
        b_z = sb("b_z", [P, C])

        xb = sb("xb", [P, CT, N])
        xa = sb("xa", [P, CT, N])
        st6 = sb("st6", [P, 3, CT, 2, 6])
        mv = sb("mv", [P, 3, CT, 2])
        sq = sb("sq", [P, 3, CT])
        gm = sb("gm", [P, 3, CT, 2])
        gsq = sb("gsq", [P, 3, CT])
        gve = sb("gve", [P, 3, CT])
        rstd = sb("rstd", [P, 3, CT])
        ga = sb("ga", [P, 3, CT])
        gma = sb("gma", [P, 3, CT])
        gb = sb("gb", [P, 3, CT])
        pick = sb("pick", [8 * Q4, 4, P])
        spare = sb("spare", [P, 1])
        xn1 = sb("xn1", [P, CT, N])
        ks = sb("ks", [P, HEADS, N], F32R)
        qs = sb("qs", [P, UNITS, Q4, HALF], F32R)
        vo = sb("vo", [P, NT, HEADS, DH])
        mxh = sb("mxh", [P, 4 * Q4, 2])
        sumh = sb("sumh", [P, 2, 4 * Q4, 2])
        apart = sb("apart", [P, 4 * Q4, 2])
        rsum = sb("rsum", [P, 4 * Q4])
        stat = sb("stat", [P, 2, 4 * Q4])
        mrow = sb("mrow", [4 * Q4, P], F32R)
        srow = sb("srow", [8 * Q4, P])
        prob = sb("prob", [P, 2, Q4, HALF])
        recs = sb("recs", [P, HALF])
        att1 = sb("att1", [P, GROUPS4, N])
        with ExitStack() as own:
            hi1 = sb("hi1", [P, 2, N], F32R, over=own)
            lo1 = sb("lo1", [P, 2, N], F32R, over=own)
        qT0 = sb("qT0", [P, H, 32])
        kT0 = sb("kT0", [P, H, 32])
        vT0 = sb("vT0", [P, W, 32])
        mx0 = sb("mx0", [P, 32])
        sum0 = sb("sum0", [P, 32])
        cmx = sb("cmx", [P, C])
        ctx2 = sb("ctx2", [P, CT, C])
        up_h = sb("up_h", [P, 4 * 3 * 2])
        up_w = sb("up_w", [P, UPH])
        dn_h = sb("dn_h", [P, WIN + 1])
        dn_w = sb("dn_w", [P, W])
        sb("region_end", [P, 64])
        slots0 = xn1
        e0, pT0 = (slots0[:, m, :].rearrange("p (c n) -> p c n", n=32) for m in range(2))
        y0 = e0
        yc0 = qT0
        xn2 = sb("xn2", [P, CT, N])
        o3 = xn2
        rmx = sb("rmx", [P, NT])
        qsum = sb("qsum", [P, NT])
        qrec = sb("qrec", [P, NT])
        cmc = sb("cmc", [P, CT])
        crec = sb("crec", [P, CT])
        with ExitStack() as own:
            up3 = sb("up3", [P, UPT, P], over=own)
        k2 = sb("k2", [P, NT, C])
        qe = sb("qe", [P, NT, C])
        v2 = sb("v2", [P, NT, C + 1])
        qc = k2[:, :, :].rearrange("p t c -> p (t c)").rearrange("p (a n) -> p a n", a=CT)
        o2 = qe[:, :, :].rearrange("p t c -> p (t c)").rearrange("p (a n) -> p a n", a=CT)
        z3 = v2[:, :, 0:C]

        def v(name, i=0):
            at = VEC[name][0]
            return vec[:, at + i:at + i + 1]

        def vv(name):
            at, n = VEC[name]
            return vec[:, at:at + n]

        def both(at=6):
            return ps[:, at:at + 2, :].rearrange("p a n -> p (a n)")

        def gn_ps(n):
            return ps[:, 7 if n == 2 else 6, 0:2 * CT].rearrange("p (c s) -> p c s", s=2)

        consts_in = signal("consts_in", 0)
        prep_v = signal("prep_v", 0)
        prep_p = signal("prep_p", 0)
        x_in = signal("x_in", 2, 16)
        xa_in = signal("xa_in", 1, 16)
        l0_mm = signal("l0_mm", 3)
        l0_sb = signal("l0_sb", 3)
        tr0 = signal("tr0", 3)
        corr0 = signal("corr0", 1)
        mx0_ok = signal("mx0_ok", 1)
        sub0 = signal("sub0", 1)
        exp0 = signal("exp0", 1)
        pT0_ok = signal("pT0_ok", 1)
        sum0_ok = signal("sum0_ok", 2)
        av0 = signal("av0", 1)
        y0_ok = signal("y0_ok", 1)
        yc0_ok = signal("yc0_ok", 1)
        wr_mm = signal("wr_mm", 2)
        res0 = signal("res0", 2)
        x1_ok = signal("x1_ok", 2)
        gn_v = [signal(f"gn_v{n}", 12) for n in range(3)]
        gn_mm = [signal(f"gn_mm{n}", 1) for n in range(3)]
        gn_p = [signal(f"gn_p{n}", 1) for n in range(3)]
        xn1_ok = signal("xn1_ok", 2)
        qk1_mm = signal("qk1_mm", 8)
        hi1_ok = signal("hi1_ok", 8)
        lo1_ok = signal("lo1_ok", 8)
        stack_ok = [signal(f"stack_ok{g}", 6 * Q4, 16) for g in range(GROUPS4)]
        v1_mm = signal("v1_mm", 2)
        v1_ok = signal("v1_ok", 4)
        max_mm = signal("max_mm", STEPS * Q4)
        max_ok = signal("max_ok", STEPS * Q4)
        sum_ok = signal("sum_ok", STEPS * Q4)
        join_v = signal("join_v", UNITS * 2)
        apart_ok = signal("apart_ok", UNITS)
        rec_ok = signal("rec_ok", UNITS * 3)
        row_mm = signal("row_mm", UNITS)
        row_ok = signal("row_ok", UNITS * 2)
        row_in = signal("row_in", UNITS, 16)
        s_mm = signal("s_mm", STEPS * Q4)
        p_ok = signal("p_ok", STEPS * Q4)
        av_mm = signal("av_mm", STEPS)
        spread_mm = signal("spread_mm", UNITS)
        spread_ok = signal("spread_ok", UNITS)
        att_ok = signal("att_ok", UNITS)
        proj_mm = signal("proj_mm", 2)
        x2_ok = signal("x2_ok", 2)
        xn2_ok = signal("xn2_ok", 2)
        ones2 = signal("ones2", 1)
        kv_mm = signal("kv_mm", NT)
        kv_ok = signal("kv_ok", NT * 2)
        rmx_ok = signal("rmx_ok", 2)
        qe_ok = signal("qe_ok", NT)
        qrec_ok = signal("qrec_ok", 1)
        qn_ok = signal("qn_ok", NT)
        cmx_ok = signal("cmx_ok", 2)
        cmt_mm = signal("cmt_mm", 1)
        cmc_ok = signal("cmc_ok", 1)
        cmb_mm = signal("cmb_mm", 1)
        cmb_ok = signal("cmb_ok", 1)
        ksub = signal("ksub", 2)
        ke_ok = signal("ke_ok", 2)
        qt_mm = signal("qt_mm", 4)
        qc_ok = signal("qc_ok", 4)
        ctx_mm = signal("ctx_mm", CT)
        crec_ok = signal("crec_ok", CT)
        ctx_ok = signal("ctx_ok", CT)
        o2_mm = signal("o2_mm", 2)
        o2_ok = signal("o2_ok", 2)
        g2_ok = signal("g2_ok", 2)
        z_mm = signal("z_mm", 4)
        z_ok = signal("z_ok", 4)
        up_mm = signal("up_mm", UPT // 2)
        relu_ok = signal("relu_ok", UPT // 2)
        up_ok = signal("up_ok", UPT // 2)
        dn_mm = signal("dn_mm", 2)
        o3_ok = signal("o3_ok", 2)
        stored = signal("stored", 2, 16)

        loads = [(wq0, weights["wq0"]), (wr0, weights["wr0"]), (wqk1, weights["wqk1"]), (wv1, weights["wv1"]),
                 (wp1, weights["wp1"]), (wkv2, weights["wkv2"]), (wo2, weights["wo2"]), (vec, vectors),
                 (rowc, rows), (ident, consts["ident"]), (avg8, consts["avg8"]), (avg16, consts["avg16"]),
                 (pick, consts["pick"]),
                 (up_h, filters["up_h"]), (up_w, filters["up_w"]), (dn_h, filters["dn_h"]), (dn_w, filters["dn_w"])]
        PREP_V = 27
        PREP_P = 5
        MAX_BANKS = (2, 3, 5)

        def periods(eng, first, period, last):
            first()
            period(0, None, 1)
            with eng.Fori(1, B - 1) as b:
                period((b, 0), (b, -1), (b, 1))
            period(B - 1, B - 2, None)
            last(B - 1)

        def copied(eng, n, *images):
            if n % 4 or not isinstance(images[0], tuple):
                return images
            register = eng.alloc_register(f"image_at_step{n}")
            eng.reg_mov(register, images[0][0])
            copy = eng.snap(register, min_val=1, max_val=B - 2)
            return [(copy, away) for _, away in images]

        def spread_bank(t):
            return MAX_BANKS[(Q4 * NT * ((t + 1) % UNITS) + 2) % 3]

        def turn_at(n):
            return (n - 1) // NT + 1 if n % NT == NT - LEAD else None

        block = ctx.enter_context(nc.Block())

        @block.sync
        def _(sp):
            for made in looped:
                sp.sem_inc(made.sem, START)
            for dst, src in loads:
                sp.dma_start(dst[:, 0:WIN] if dst is dn_h else dst[tuple(slice(None) for _ in dst.shape)], src).then_inc(consts_in.sem, 16)

            def load(j):
                for ct in range(CT):
                    sp.dma_start(xb[:, ct, :], x[number(j), ct * P:(ct + 1) * P, :]).then_inc(x_in.sem, 16)

            def copy_x(b, i, j):
                if i is not None:
                    sp.wait_ge(xn2_ok.sem, xn2_ok(i, 2))
                sp.dma_start(xa[:, :, :], xb[:, :, :]).then_inc(xa_in.sem, 16)
                if j is not None:
                    sp.wait_ge(xa_in.sem, xa_in(b, 1))
                    load(j)

            def stack(b, before, g, part):
                sp.wait_ge(hi1_ok.sem, hi1_ok(b, 2 * (2 * g + part + 1)))
                sp.wait_ge(lo1_ok.sem, lo1_ok(b, 2 * (2 * g + part + 1)))
                if before is not None:
                    sp.wait_ge(s_mm.sem, s_mm(before, STEPS * Q4 // 2 * (g + 1)))
                for h in range(Q4):
                    for r, of in enumerate(((hi1, lo1, hi1), (hi1, hi1, lo1))[part]):
                        at = slice(DH * r, DH * r + DH)
                        src = of[DH * h:DH * h + DH, part, :]
                        if part:
                            sp.dma_start(ks[at, g * Q4 + h, :].bitcast(F32), src.bitcast(F32))\
                              .then_inc(stack_ok[g].sem, 16)
                        else:
                            sp.dma_start(qs[at, 2 * g:2 * g + 2, h, :].bitcast(F32),
                                         src.bitcast(F32).rearrange("p (a n) -> p a n", a=2))\
                              .then_inc(stack_ok[g].sem, 16)

            def rows_in(b, u):
                sp.wait_ge(row_ok.sem, row_ok(b, 2 * u + 1))
                sp.dma_start(qs[STACK:STACK + 1, u % UNITS, :, :].bitcast(F32), mrow[:, :].bitcast(F32))\
                    .then_inc(row_in.sem, 16)

            def store(i, ct):
                sp.wait_ge(o3_ok.sem, o3_ok(i, ct + 1))
                sp.dma_start(out[number(i), ct * P:(ct + 1) * P, :], o3[:, ct, :]).then_inc(stored.sem, 16)

            def side(name, b, i, j):
                if name == "copy_x":
                    copy_x(b, i, j)
                elif name in ("q1", "k1"):
                    stack(b, i, 1, int(name == "k1"))
                elif name in ("q0", "k0"):
                    stack(j, b, 0, int(name == "k0"))
                elif name in ("dn03", "dn13"):
                    store(i, int(name[2]))

            def first():
                load(0)
                for name in FIRST:
                    side(name, None, None, 0)
                rows_in(0, 0)

            def period(b, i, j):
                for n in range(STEPS):
                    b, i, j = copied(sp, n, b, i, j)
                    t = turn_at(n)
                    if t is not None and (t < UNITS or j is not None):
                        rows_in(b, t)
                    for name in [*beside(2 * n, i, j), *beside(2 * n + 1, i, j)]:
                        side(name, b, i, j)

            def last(i):
                for names in SIDE.values():
                    for name in names:
                        if not name.startswith(OF_B + OF_J) and name != "copy_x":
                            side(name, None, i, None)

            periods(sp, first, period, last)
            sp.wait_ge(stored.sem, stored(B, 0))

        @block.gpsimd
        def _(pool):
            pool.memset(minus_half[:, :], -0.5).then_inc(prep_p.sem, 1)
            pool.wait_ge(prep_p.sem, 1)
            pool.memset(ks[STACK:STACK + 1, :, :].bitcast(F32), 1.0).then_inc(prep_p.sem, 1)
            pool.wait_ge(prep_p.sem, 2)
            pool.memset(stat[:, :, :], 1.0).then_inc(prep_p.sem, 1)
            pool.wait_ge(prep_p.sem, 3)
            pool.wait_ge(consts_in.sem, 16 * len(loads))
            pool.tensor_scalar(inv0[:, :], vv("var"), EPS, None, ALU.add).then_inc(prep_p.sem, 1)
            pool.wait_ge(prep_p.sem, 4)
            pool.tensor_tensor(inv0[:, :], inv0[:, :], minus_half[:, :], ALU.pow).then_inc(prep_p.sem, 1)

            def side(name, b, i, j):
                if name in ("norm1a", "norm2a", "norm3a"):
                    n = int(name[4]) - 1
                    pool.wait_ge(gn_v[n].sem, gn_v[n](j if n == 0 else i, 9))
                    pool.tensor_tensor(rstd[:, n, :], gve[:, n, :], minus_half[:, :], ALU.pow).then_inc(gn_p[n].sem, 1)

            def first():
                for name in FIRST:
                    side(name, None, None, 0)

            def period(b, i, j):
                for n in range(STEPS):
                    b, i, j = copied(pool, n, b, i, j)
                    for name in [*beside(2 * n, i, j), *beside(2 * n + 1, i, j)]:
                        side(name, b, i, j)

            def last(i):
                for names in SIDE.values():
                    for name in names:
                        if not name.startswith(OF_B + OF_J):
                            side(name, None, i, None)

            periods(pool, first, period, last)

        @block.vector
        def _(dve):
            dve.wait_ge(consts_in.sem, 16 * len(loads))
            dve.wait_ge(prep_p.sem, PREP_P)
            done = 0

            def prepared(ins):
                nonlocal done
                done += 1
                ins.then_inc(prep_v.sem, 1)

            for m in range(4 * 3):
                for e in range(2):
                    prepared(dve.tensor_scalar(up_m[:, m, e * UPH:(e + 1) * UPH], up_w[:, :],
                                               up_h[:, 2 * m + e:2 * m + e + 1], 4.0, ALU.mult, ALU.mult))
            for r in range(WIN):
                ins = dve.tensor_scalar(dn_m[:, r * W:(r + 1) * W], dn_w[:, :], dn_h[:, r:r + 1], None, ALU.mult)
            prepared(ins)
            dve.tensor_tensor(b_z[:, :], rowc[:, 3 * C:4 * C], rowc[:, 4 * C:5 * C], ALU.add)
            dve.tensor_scalar(wqk1[:, :, :], wqk1[:, :, :], float(DH) ** -0.25, None, ALU.mult)
            dve.tensor_scalar(vv("b_qk"), vv("b_qk"), float(DH) ** -0.25, None, ALU.mult)
            dve.tensor_tensor(inv0[:, :], inv0[:, :], vv("gamma"), ALU.mult)
            prepared(dve.tensor_tensor(add0[:, :], vv("br"), vv("mean"), ALU.subtract))
            dve.wait_ge(prep_v.sem, done)
            prepared(dve.tensor_tensor(add0[:, :], add0[:, :], inv0[:, :], ALU.mult))
            dve.wait_ge(prep_v.sem, done)
            dve.tensor_tensor(add0[:, :], add0[:, :], vv("beta"), ALU.add).then_inc(prep_v.sem, 1)
            assert done + 1 == PREP_V + 1, done
            dve.wait_ge(prep_v.sem, done + 1)

            def stepper(n, i, k):
                def step(ins):
                    nonlocal k
                    k += 1
                    ins.then_inc(gn_v[n].sem, 1)

                def last():
                    dve.wait_ge(gn_v[n].sem, gn_v[n](i, k))
                return step, last

            def stats(n, i, src, ct):
                step, last = stepper(n, i, ct)
                for half in range(2):
                    ins = dve.bn_stats(st6[:, n, ct, half, :], src[:, ct, half * HALF:(half + 1) * HALF])
                step(ins)
                if ct < CT - 1:
                    return
                last()
                dve.memset(spare[:, :], 0.0)
                for ct in range(CT):
                    ins = dve.bn_aggr(mv[:, n, ct, :], st6[:, n, ct, :, :])
                step(ins)
                last()
                step(dve.tensor_tensor(sq[:, n, :], mv[:, n, :, 0], mv[:, n, :, 0], ALU.mult))
                last()
                step(dve.tensor_tensor(mv[:, n, :, 1], mv[:, n, :, 1], sq[:, n, :], ALU.add))

            def variances(n, i):
                step, last = stepper(n, i, 5)
                dve.wait_ge(gn_mm[n].sem, gn_mm[n](i, 1))
                step(dve.tensor_copy(gm[:, n, :, :], gn_ps(n)))
                last()
                step(dve.tensor_tensor(gsq[:, n, :], gm[:, n, :, 0], gm[:, n, :, 0], ALU.mult))
                step(dve.tensor_scalar(gve[:, n, :], gm[:, n, :, 1], EPS, None, ALU.add))
                last()
                step(dve.tensor_tensor(gve[:, n, :], gve[:, n, :], gsq[:, n, :], ALU.subtract))

            def factors(n, i, scale, bias):
                step, last = stepper(n, i, 9)
                dve.wait_ge(gn_p[n].sem, gn_p[n](i, 1))
                step(dve.tensor_tensor(ga[:, n, :], rstd[:, n, :], vv(scale), ALU.mult))
                last()
                step(dve.tensor_tensor(gma[:, n, :], gm[:, n, :, 0], ga[:, n, :], ALU.mult))
                last()
                step(dve.tensor_tensor(gb[:, n, :], vv(bias), gma[:, n, :], ALU.subtract))
                last()

            def apply_norm(n, dst, src, ok):
                for ct in range(CT):
                    dve.tensor_scalar(dst[:, ct, :], src[:, ct, :], ga[:, n, ct:ct + 1], gb[:, n, ct:ct + 1],
                                      ALU.mult, ALU.add).then_inc(ok.sem, 1)

            def turn(j, m):
                dst, pattern = ((qT0, "p (h w) -> p h w"), (kT0, "p (h w) -> p h w"), (vT0, "p (h w) -> p w h"))[m]
                dve.wait_ge(l0_sb.sem, l0_sb(j, m + 1))
                dve.transpose(dst[:, :, :], slots0[:, m % 2, :].rearrange(pattern, h=H)).then_inc(tr0.sem, 1)

            def less_max(j):
                scores = ps[:, 6:8, :].rearrange("p a (c j) -> p (a c) j", j=32)
                dve.wait_ge(corr0.sem, corr0(j, 1))
                dve.tensor_reduce(mx0[:, :], scores, AX_X, ALU.max).then_inc(mx0_ok.sem, 1)
                dve.wait_ge(mx0_ok.sem, mx0_ok(j, 1))
                dve.wait_ge(tr0.sem, tr0(j, 3))
                dve.tensor_tensor(e0, scores, mx0[:, :].unsqueeze(2).to_broadcast([P, 32, 32]),
                                  ALU.subtract).then_inc(sub0.sem, 1)

            def weights0(j):
                dve.wait_ge(exp0.sem, exp0(j, 1))
                dve.transpose(pT0, e0).then_inc(pT0_ok.sem, 1)
                dve.tensor_reduce(sum0[:, :], e0, AX_X, ALU.add).then_inc(sum0_ok.sem, 1)
                dve.wait_ge(sum0_ok.sem, sum0_ok(j, 1))
                dve.reciprocal(sum0[:, :], sum0[:, :]).then_inc(sum0_ok.sem, 1)

            def result0(j):
                dve.wait_ge(sum0_ok.sem, sum0_ok(j, 2))
                dve.wait_ge(av0.sem, av0(j, 1))
                dve.tensor_tensor(y0, ps[:, 6:8, :].rearrange("p a (c n) -> p (a c) n", n=32),
                                  sum0[:, :].unsqueeze(2).to_broadcast([P, 32, 32]), ALU.mult).then_inc(y0_ok.sem, 1)
                dve.wait_ge(y0_ok.sem, y0_ok(j, 1))
                dve.transpose(yc0[:, :, :].rearrange("p h w -> p w h"),
                              y0.rearrange("p c w -> p w c")).then_inc(yc0_ok.sem, 1)

            def residual0(j, ct):
                dve.wait_ge(wr_mm.sem, wr_mm(j, ct + 1))
                dve.scalar_tensor_tensor(out=xb[:, ct, :], in0=both(), scalar=inv0[:, ct:ct + 1], in1=xb[:, ct, :],
                                         op0=ALU.mult, op1=ALU.add).then_inc(res0.sem, 1)
                dve.wait_ge(res0.sem, res0(j, ct + 1))
                dve.tensor_scalar(xb[:, ct, :], xb[:, ct, :], add0[:, ct:ct + 1], None, ALU.add).then_inc(x1_ok.sem, 1)

            def low(b, g, part):
                k = 2 * g + part
                for hf in range(2):
                    at = slice(hf * HALF, (hf + 1) * HALF)
                    dve.wait_ge(hi1_ok.sem, hi1_ok(b, 2 * k + hf + 1))
                    dve.scalar_tensor_tensor(out=lo1[:, part, at], in0=ps[:, 6 + hf, :], scalar=v("b_qk", k),
                                             in1=hi1[:, part, at].bitcast(F32), op0=ALU.add, op1=ALU.subtract)\
                        .then_inc(lo1_ok.sem, 1)

            def values_in(b, g):
                dve.wait_ge(v1_mm.sem, v1_mm(b, g + 1))
                for m in range(2):
                    dve.tensor_tensor(vo[:, 4 * m:4 * m + 4, g * Q4:(g + 1) * Q4, 0:DH],
                                      ps[:, 6 + m, :].rearrange("p (s h d) -> p s h d", s=4, d=DH),
                                      rowc[:, g * P:(g + 1) * P].rearrange("p (s h d) -> p s h d", s=1, d=DH)
                                      .to_broadcast([P, 4, Q4, DH]), ALU.add).then_inc(v1_ok.sem, 1)

            def max_steps(b, m, pair):
                k = 4 * (2 * (m % 2) + pair) + m % NT // 2
                for e in range(2):
                    at = Q4 * m + 2 * pair + e
                    dve.wait_ge(max_mm.sem, max_mm(b, at + 1))
                    dve.tensor_reduce(mxh[:, k, e:e + 1], ps[:, MAX_BANKS[at % 3], :], AX_X, ALU.max,
                                      negate=True).then_inc(max_ok.sem, 1)

            def maxima_joined(b, t):
                dve.wait_ge(max_ok.sem, max_ok(b, Q4 * NT * (t + 1)))
                dve.wait_ge(row_mm.sem, row_mm(b, t))
                dve.tensor_tensor(stat[:, 0, :].bitcast(F32R), mxh[:, :, 0], mxh[:, :, 1], ALU.min).then_inc(join_v.sem, 1)
                dve.wait_ge(join_v.sem, join_v(b, 2 * t + 1))
                dve.tensor_tensor(apart[:, :, :], stat[:, 0, :].unsqueeze(2).to_broadcast([P, 4 * Q4, 2]), mxh[:, :, :],
                                  ALU.subtract).then_inc(join_v.sem, 1)
                dve.wait_ge(join_v.sem, join_v(b, 2 * t + 2))

            def sums_joined(b, t):
                dve.wait_ge(row_mm.sem, row_mm(b, t + 1))
                dve.wait_ge(apart_ok.sem, apart_ok(b, t + 1))
                dve.tensor_tensor(apart[:, :, :], apart[:, :, :], sumh[:, t % 2, :, :], ALU.mult).then_inc(rec_ok.sem, 1)
                dve.wait_ge(rec_ok.sem, rec_ok(b, 3 * t + 1))
                dve.tensor_tensor(rsum[:, :], apart[:, :, 0], apart[:, :, 1], ALU.add).then_inc(rec_ok.sem, 1)
                dve.wait_ge(rec_ok.sem, rec_ok(b, 3 * t + 2))
                dve.reciprocal(stat[:, 1, :], rsum[:, :]).then_inc(rec_ok.sem, 1)

            def rows_turned(b, t):
                dve.wait_ge(row_mm.sem, row_mm(b, t + 1))
                dve.wait_ge(row_in.sem, row_in(b, t))
                dve.tensor_copy(mrow[:, :], ps[0:4 * Q4, spread_bank(t), 0:P]).then_inc(row_ok.sem, 1)
                dve.tensor_copy(srow[:, :], ps[0:8 * Q4, spread_bank(t), 0:P]).then_inc(row_ok.sem, 1)

            def reciprocals_in(b, u):
                dve.wait_ge(spread_mm.sem, spread_mm(b, u + 1))
                dve.wait_ge(att_ok.sem, att_ok(b, u))
                dve.tensor_copy(recs[:, :], ps[:, spread_bank(u + 1), :]).then_inc(spread_ok.sem, 1)

            def normalise(b, u):
                g, th = u // 2, u % 2
                dve.wait_ge(av_mm.sem, av_mm(b, (u + 1) * NT))
                dve.wait_ge(spread_ok.sem, spread_ok(b, u + 1))
                dve.tensor_tensor(att1[:, g, th * HALF:(th + 1) * HALF], ps[:, 4, :], recs[:, :],
                                  ALU.mult).then_inc(att_ok.sem, 1)

            def residual1(i, ct):
                dve.wait_ge(proj_mm.sem, proj_mm(i, ct + 1))
                dve.wait_ge(xa_in.sem, xa_in(i, 1))
                dve.scalar_tensor_tensor(out=xa[:, ct, :], in0=both(), scalar=v("b_proj", ct), in1=xa[:, ct, :],
                                         op0=ALU.add, op1=ALU.add).then_inc(x2_ok.sem, 1)

            def kv_in(i, m):
                if m == 0:
                    dve.memset(v2[:, :, C:C + 1], 1.0).then_inc(ones2.sem, 1)
                for t in (2 * m, 2 * m + 1):
                    dve.wait_ge(kv_mm.sem, kv_mm(i, t + 1))
                    dve.tensor_tensor(k2[:, t, :], ps[:, 6 + t % 2, 0:C], rowc[:, C:2 * C], ALU.add).then_inc(kv_ok.sem, 1)
                    dve.tensor_tensor(v2[:, t, 0:C], ps[:, 6 + t % 2, C:2 * C], rowc[:, 2 * C:3 * C],
                                      ALU.add).then_inc(kv_ok.sem, 1)

            def k_maxima(i, b, m):
                if m == 0:
                    dve.wait_ge(kv_ok.sem, kv_ok(i, 2 * NT))
                    if b is not None:
                        dve.wait_ge(stack_ok[1].sem, stack_ok[1](b, 6 * Q4))
                dve.tensor_reduce(cmx[:, m * P:(m + 1) * P], k2[:, :, m * P:(m + 1) * P].rearrange("p t d -> p d t"),
                                  AX_X, ALU.max).then_inc(cmx_ok.sem, 1)

            def q_maxima(m):
                at = slice(4 * m, 4 * m + 4)
                dve.tensor_reduce(rmx[:, at], k2[:, at, :], AX_X, ALU.max, negate=True).then_inc(rmx_ok.sem, 1)

            def k_maxima_joined(i):
                dve.wait_ge(cmt_mm.sem, cmt_mm(i, 1))
                dve.tensor_reduce(cmc[:, :], ps[:, 6, 0:C].rearrange("p (a n) -> p a n", a=CT), AX_X, ALU.max)\
                    .then_inc(cmc_ok.sem, 1)

            def spread_in(i):
                dve.wait_ge(cmb_mm.sem, cmb_mm(i, 1))
                dve.tensor_copy(cmx[:, :], ps[:, 7, 0:C]).then_inc(cmb_ok.sem, 1)

            def k_less_max(i, m):
                at = slice(4 * m, 4 * m + 4)
                dve.wait_ge(cmb_ok.sem, cmb_ok(i, 1))
                dve.wait_ge(qe_ok.sem, qe_ok(i, 4 * m + 4))
                dve.tensor_tensor(k2[:, at, :], k2[:, at, :], cmx[:, :].unsqueeze(1).to_broadcast([P, 4, C]),
                                  ALU.subtract).then_inc(ksub.sem, 1)

            def q_normalise(i):
                dve.wait_ge(qe_ok.sem, qe_ok(i, NT))
                dve.reciprocal(qrec[:, :], qsum[:, :]).then_inc(qrec_ok.sem, 1)
                dve.wait_ge(qrec_ok.sem, qrec_ok(i, 1))
                for t in range(NT):
                    dve.tensor_scalar(qe[:, t, :], qe[:, t, :], qrec[:, t:t + 1], float(C) ** -0.5,
                                      ALU.mult, ALU.mult).then_inc(qn_ok.sem, 1)

            def context_in(i, ct):
                dve.wait_ge(ctx_mm.sem, ctx_mm(i, ct + 1))
                dve.reciprocal(crec[:, ct:ct + 1], ps[:, 6 + ct, C:C + 1]).then_inc(crec_ok.sem, 1)
                dve.wait_ge(crec_ok.sem, crec_ok(i, ct + 1))
                dve.tensor_scalar(ctx2[:, ct, :], ps[:, 6 + ct, 0:C], crec[:, ct:ct + 1], None,
                                  ALU.mult).then_inc(ctx_ok.sem, 1)

            def q_turned(i, m):
                for hf in range(2):
                    dve.wait_ge(qt_mm.sem, qt_mm(i, 2 * m + hf + 1))
                    dve.tensor_copy(qc[:, m, hf * HALF:(hf + 1) * HALF], ps[:, 6 + hf, :]).then_inc(qc_ok.sem, 1)

            def z_in(i, m):
                dve.wait_ge(z_mm.sem, z_mm(i, m + 1))
                dve.tensor_tensor(z3[:, 2 * m:2 * m + 2, :], ps[:, 6 + m % 2, :].rearrange("p (s c) -> p s c", s=2),
                                  b_z[:, :].unsqueeze(1).to_broadcast([P, 2, C]), ALU.add).then_inc(z_ok.sem, 1)

            def leaky(i, f):
                dve.wait_ge(relu_ok.sem, relu_ok(i, f + 1))
                tile = up3[:, 4 * (f % 8):4 * (f % 8) + 4, :].rearrange("p s c -> p (s c)")
                dve.scalar_tensor_tensor(out=tile, in0=ps[:, 6 + f % 2, :], scalar=SLOPE * ROOT2, in1=tile,
                                         op0=ALU.mult, op1=ALU.add).then_inc(up_ok.sem, 1)

            def side(name, b, i, j):
                digit = int(name[-1]) if name[-1].isdigit() else None
                if name in ("l0q", "l0k", "l0v"):
                    turn(j, "qkv".index(name[2]))
                elif name == "soft0":
                    less_max(j)
                elif name == "soft2":
                    weights0(j)
                elif name == "av3":
                    result0(j)
                elif name in ("wr0", "wr1"):
                    residual0(j, digit)
                elif name in ("stats1a", "stats1b"):
                    ct = "ab".index(name[-1])
                    dve.wait_ge(x1_ok.sem, x1_ok(j, ct + 1))
                    stats(0, j, xb, ct)
                elif name == "norm1a":
                    variances(0, j)
                elif name == "norm1b":
                    factors(0, j, "gn1_scale", "gn1_bias")
                    if b is not None:
                        dve.wait_ge(v1_mm.sem, v1_mm(b, 2))
                    apply_norm(0, xn1, xb, xn1_ok)
                elif name in ("q0", "k0"):
                    low(j, 0, int(name == "k0"))
                elif name in ("q1", "k1"):
                    low(b, 1, int(name == "k1"))
                elif name == "v0":
                    values_in(j, 0)
                elif name == "v1":
                    values_in(b, 1)
                elif name in ("proj0", "proj1"):
                    residual1(i, digit)
                elif name in ("stats2a", "stats2b"):
                    ct = "ab".index(name[-1])
                    dve.wait_ge(x2_ok.sem, x2_ok(i, ct + 1))
                    stats(1, i, xa, ct)
                elif name == "norm2a":
                    variances(1, i)
                elif name == "norm2b":
                    factors(1, i, "gn2_scale", "gn2_bias")
                    dve.wait_ge(stored.sem, stored(i, 0))
                    apply_norm(1, xn2, xa, xn2_ok)
                elif name.startswith("kv"):
                    kv_in(i, digit)
                elif name in ("kmax0", "kmax1"):
                    k_maxima(i, b, digit)
                elif name in ("rmax0", "rmax1"):
                    q_maxima(digit)
                elif name == "kmaxT":
                    k_maxima_joined(i)
                elif name == "spread":
                    spread_in(i)
                elif name in ("ksub0", "ksub1"):
                    k_less_max(i, digit)
                elif name == "qn":
                    q_normalise(i)
                elif name in ("context0", "context1"):
                    context_in(i, digit)
                elif name in ("qT0", "qT1"):
                    q_turned(i, digit)
                elif name in ("stats3a", "stats3b"):
                    ct = "ab".index(name[-1])
                    dve.wait_ge(o2_ok.sem, o2_ok(i, ct + 1))
                    stats(2, i, o2, ct)
                elif name == "norm3a":
                    variances(2, i)
                elif name == "norm3b":
                    factors(2, i, "gn3_scale", "gn3_bias")
                elif name.startswith("z"):
                    z_in(i, digit)
                elif name.startswith("up"):
                    leaky(i, int(name[2:]))

            def first():
                for name in FIRST:
                    side(name, None, None, 0)
                for m in range(NT):
                    max_steps(0, m, 0)
                    max_steps(0, m, 1)
                maxima_joined(0, 0)
                rows_turned(0, 0)
                sums_joined(0, 0)
                for m in range(NT, NT + LEAD):
                    max_steps(0, m, 0)
                    max_steps(0, m, 1)

            def period(b, i, j):
                for n in range(STEPS):
                    b, i, j = copied(dve, n, b, i, j)
                    t = turn_at(n)
                    if t is not None:
                        if t < UNITS or j is not None:
                            maxima_joined(b, t)
                        rows_turned(b, t)
                    for pair in range(2):
                        m = n + NT + LEAD
                        if m < STEPS:
                            max_steps(b, m, pair)
                        elif j is not None:
                            max_steps(j, m - STEPS, pair)
                        if pair == 1 and t is not None and (t < UNITS or j is not None):
                            sums_joined(b, t)
                        of, u = (b, n // NT - 1) if n else (i, UNITS - 1)
                        if n % NT == 0 and pair == 0 and of is not None:
                            normalise(of, u)
                        for name in beside(2 * n + pair, i, j):
                            side(name, b, i, j)
                        if pair == 0 and t is not None:
                            reciprocals_in(b, t - 1)

            def last(i):
                normalise(i, UNITS - 1)
                for names in SIDE.values():
                    for name in names:
                        if not name.startswith(OF_B + OF_J):
                            side(name, None, i, None)

            periods(dve, first, period, last)

        @block.scalar
        def _(act):
            act.wait_ge(consts_in.sem, 16 * len(loads))
            act.wait_ge(prep_v.sem, PREP_V + 1)

            def exponentials(b, i, n, pair):
                for h in (2 * pair, 2 * pair + 1):
                    k = Q4 * n + h
                    if h == 0:
                        if n > 0:
                            act.wait_ge(av_mm.sem, av_mm(b, n - 1))
                        elif i is not None:
                            act.wait_ge(av_mm.sem, av_mm(i, STEPS - 1))
                    act.wait_ge(s_mm.sem, s_mm(b, k + 1))
                    act.activation(prob[:, n % 2, h, :], ps[:, k % 2, :], ACT.Exp).then_inc(p_ok.sem, 1)

            def sums(b, m, pair):
                k = 4 * (2 * (m % 2) + pair) + m % NT // 2
                for e in range(2):
                    at = Q4 * m + 2 * pair + e
                    bank = MAX_BANKS[at % 3]
                    act.wait_ge(max_ok.sem, max_ok(b, at + 1))
                    act.activation(ps[:, bank, :], ps[:, bank, :], ACT.Exp, bias=mxh[:, k, e:e + 1],
                                   accum_out=sumh[:, m // NT % 2, k, e:e + 1]).then_inc(sum_ok.sem, 1)

            def halves(b, t):
                act.wait_ge(join_v.sem, join_v(b, 2 * t + 2))
                act.activation(apart[:, :, :], apart[:, :, :], ACT.Exp).then_inc(apart_ok.sem, 1)

            def qkv0(j, b, m):
                act.wait_ge(l0_mm.sem, l0_mm(j, m + 1))
                if m == 0 and b is not None:
                    act.wait_ge(stack_ok[1].sem, stack_ok[1](b, 6 * Q4))
                if m == 2:
                    act.wait_ge(tr0.sem, tr0(j, 1))
                act.activation(slots0[:, m % 2, :], both(), ACT.Identity, bias=v(("bq", "bk", "bv")[m]))\
                    .then_inc(l0_sb.sem, 1)

            def high(b, g, part):
                k = 2 * g + part
                for hf in range(2):
                    act.wait_ge(qk1_mm.sem, qk1_mm(b, 2 * k + hf + 1))
                    if g == 1 and hf == 0:
                        act.wait_ge(stack_ok[0].sem, stack_ok[0](b, 6 * Q4))
                    act.activation(hi1[:, part, hf * HALF:(hf + 1) * HALF], ps[:, 6 + hf, :], ACT.Identity,
                                   bias=v("b_qk", k)).then_inc(hi1_ok.sem, 1)

            def side(name, b, i, j):
                digit = int(name[-1]) if name[-1].isdigit() else None
                if name in ("l0q", "l0k", "l0v"):
                    qkv0(j, b, "qkv".index(name[2]))
                elif name == "soft1":
                    act.wait_ge(sub0.sem, sub0(j, 1))
                    act.activation(e0, e0, ACT.Exp).then_inc(exp0.sem, 1)
                elif name in ("q0", "k0"):
                    high(j, 0, int(name == "k0"))
                elif name in ("q1", "k1"):
                    high(b, 1, int(name == "k1"))
                elif name in ("qe0", "qe1"):
                    act.wait_ge(rmx_ok.sem, rmx_ok(i, digit + 1))
                    for t in range(4 * digit, 4 * digit + 4):
                        act.activation(qe[:, t, :], k2[:, t, :], ACT.Exp, bias=rmx[:, t:t + 1],
                                       accum_out=qsum[:, t:t + 1]).then_inc(qe_ok.sem, 1)
                elif name in ("kexp0", "kexp1"):
                    at = slice(4 * digit, 4 * digit + 4)
                    act.wait_ge(ksub.sem, ksub(i, digit + 1))
                    act.activation(k2[:, at, :], k2[:, at, :], ACT.Exp).then_inc(ke_ok.sem, 1)
                elif name in ("o20", "o21"):
                    act.wait_ge(o2_mm.sem, o2_mm(i, digit + 1))
                    act.activation(o2[:, digit, :], both(), ACT.Copy).then_inc(o2_ok.sem, 1)
                elif name == "gelu":
                    act.wait_ge(gn_v[2].sem, gn_v[2](i, 12))
                    for ct in range(CT):
                        act.activation(o2[:, ct, :], o2[:, ct, :], ACT.Gelu, bias=gb[:, 2, ct:ct + 1],
                                       scale=ga[:, 2, ct:ct + 1]).then_inc(g2_ok.sem, 1)
                elif name.startswith("up"):
                    f = int(name[2:])
                    act.wait_ge(up_mm.sem, up_mm(i, f + 1))
                    act.activation(up3[:, 4 * (f % 8):4 * (f % 8) + 4, :].rearrange("p s c -> p (s c)"),
                                   ps[:, 6 + f % 2, :], ACT.Relu, scale=(1.0 - SLOPE) * ROOT2).then_inc(relu_ok.sem, 1)
                elif name in ("dn03", "dn13"):
                    ct = int(name[2])
                    act.wait_ge(dn_mm.sem, dn_mm(i, ct + 1))
                    act.activation(o3[:, ct, :], both(), ACT.Copy).then_inc(o3_ok.sem, 1)

            def first():
                for name in FIRST:
                    side(name, None, None, 0)
                for m in range(NT + LEAD):
                    sums(0, m, 0)
                    sums(0, m, 1)
                    if m == NT - 1:
                        halves(0, 0)

            def period(b, i, j):
                for n in range(STEPS):
                    b, i, j = copied(act, n, b, i, j)
                    for pair in range(2):
                        exponentials(b, i, n, pair)
                        t = turn_at(n)
                        if t is not None and pair == 0 and (t < UNITS or j is not None):
                            halves(b, t)
                        m = n + NT + LEAD
                        if m < STEPS:
                            sums(b, m, pair)
                        elif j is not None:
                            sums(j, m - STEPS, pair)
                        for name in beside(2 * n + pair, i, j):
                            side(name, b, i, j)

            def last(i):
                for names in SIDE.values():
                    for name in names:
                        if not name.startswith(OF_B + OF_J):
                            side(name, None, i, None)

            periods(act, first, period, last)

        @block.tensor
        def _(pe):
            pe.wait_ge(consts_in.sem, 16 * len(loads))
            pe.wait_ge(prep_p.sem, PREP_P)
            pe.wait_ge(prep_v.sem, PREP_V + 1)

            def product(dst, pairs):
                for n, (lhsT, rhs) in enumerate(pairs):
                    ins = pe.matmul(dst, lhsT, rhs, start=(n == 0), stop=(n == len(pairs) - 1))
                return ins

            def both_halves(weights, src, signal):
                for hf in range(2):
                    ins = product(ps[:, 6 + hf, :], [(w, s[:, hf * HALF:(hf + 1) * HALF]) for w, s in zip(weights, src)])
                ins.then_inc(signal.sem, 1)

            def channel_tiles(t):
                return [t[:, ct, :] for ct in range(CT)]

            def average(n, i, matrix):
                pe.wait_ge(gn_v[n].sem, gn_v[n](i, 5))
                pe.matmul(gn_ps(n), matrix[:, :], mv[:, n, :, :], start=True, stop=True).then_inc(gn_mm[n].sem, 1)

            def logits(b, n, pair, i):
                u, s = n // NT, n % NT
                for h in (2 * pair, 2 * pair + 1):
                    k = Q4 * n + h
                    if k >= 2:
                        pe.wait_ge(p_ok.sem, p_ok(b, k - 1))
                    elif i is not None:
                        pe.wait_ge(p_ok.sem, p_ok(i, STEPS * Q4 + k - 1))
                    if s == 0 and h == 0:
                        pe.wait_ge(row_in.sem, row_in(b, u + 1))
                    pe.matmul(ps[:, k % 2, :], ks[0:STACK + 1, (u // 2) * Q4 + h, s * P:(s + 1) * P],
                              qs[0:STACK + 1, u, h, :], start=True, stop=True).then_inc(s_mm.sem, 1)

            def max_products(b, m, pair, i=None):
                u, s = m // NT, m % NT
                if m in (0, STEPS // 2) and pair == 0:
                    pe.wait_ge(stack_ok[u // 2].sem, stack_ok[u // 2](b, 6 * Q4))
                head = 2 * (s % 2) + pair
                for e in range(2):
                    k = Q4 * m + 2 * pair + e
                    if k >= 3:
                        pe.wait_ge(sum_ok.sem, sum_ok(b, k - 2))
                    elif i is not None:
                        pe.wait_ge(sum_ok.sem, sum_ok(i, STEPS * Q4 - (1, 0, 2)[k]))
                    if k % (Q4 * NT) == 2 and (u > 0 or i is not None):
                        pe.wait_ge(spread_ok.sem, spread_ok(b, u - 1))
                    pe.matmul(ps[:, MAX_BANKS[k % 3], :], qs[0:STACK, u, head, (s // 2) * P:(s // 2 + 1) * P],
                              ks[0:STACK, (u // 2) * Q4 + head, e * HALF:(e + 1) * HALF],
                              start=True, stop=True).then_inc(max_mm.sem, 1)

            def turn(b, t, joined=True):
                if joined:
                    pe.wait_ge(sum_ok.sem, sum_ok(b, Q4 * NT * (t + 1)))
                    pe.wait_ge(join_v.sem, join_v(b, 2 * t + 1))
                else:
                    pe.wait_ge(sum_ok.sem, sum_ok(b, Q4 * STEPS))
                pe.wait_ge(rec_ok.sem, rec_ok(b, 3 * t))
                pe.transpose(ps[0:8 * Q4, spread_bank(t), 0:P], stat[:, :, :].rearrange("p a k -> p (a k)"),
                             ident[:, :]).then_inc(row_mm.sem, 1)

            def spread(b, t):
                pe.wait_ge(row_ok.sem, row_ok(b, 2 * t + 2))
                for a in range(4):
                    ins = pe.matmul(ps[:, spread_bank(t), a * P:(a + 1) * P], pick[:, a, :], srow[:, :],
                                    start=True, stop=True)
                ins.then_inc(spread_mm.sem, 1)

            def values(b, n, i=None):
                u, s = n // NT, n % NT
                pe.wait_ge(p_ok.sem, p_ok(b, Q4 * n + Q4))
                if s == 0 and n > 0:
                    pe.wait_ge(att_ok.sem, att_ok(b, u))
                elif n == 0 and i is not None:
                    pe.wait_ge(att_ok.sem, att_ok(i, UNITS))
                for h in range(Q4):
                    ins = pe.matmul(ps[DH * h:DH * h + DH, 4, :], vo[:, s, (u // 2) * Q4 + h, :],
                                    prob[:, n % 2, h, :], start=(s == 0), stop=(s == NT - 1))
                ins.then_inc(av_mm.sem, 1)

            def qkv0(b, i, j, m):
                if m == 0:
                    pe.wait_ge(x_in.sem, x_in(j, 2))
                    if i is not None:
                        pe.wait_ge(cmb_ok.sem, cmb_ok(i, 1))
                    elif b is not None:
                        pe.wait_ge(v1_ok.sem, v1_ok(b, 4))
                else:
                    pe.wait_ge(l0_sb.sem, l0_sb(j, m))
                both_halves([wq0[:, kt, m * CR:(m + 1) * CR] for kt in range(CT)], channel_tiles(xb), l0_mm)

            def one_column(bank):
                pe.matmul(ps[:, bank, 0:1], ident[:, :], ident[:, 0:1], start=True, stop=True)

            def scores0(i, j, q):
                if q == 0:
                    pe.wait_ge(l0_sb.sem, l0_sb(j, 3))
                    pe.wait_ge(tr0.sem, tr0(j, 2))
                    one_column(6)
                at = slice(32 * q, 32 * q + 32)
                for c in range(32):
                    ins = pe.matmul(ps[at, 6 + c // 16, 32 * (c % 16):32 * (c % 16) + 32],
                                    qT0[at, :, c], kT0[at, :, c], start=True, stop=True)
                if q == Q4 - 1:
                    ins.then_inc(corr0.sem, 1)

            def values0(i, j, q):
                if q == 0:
                    pe.wait_ge(tr0.sem, tr0(j, 3))
                    if i is not None:
                        pe.wait_ge(ctx_ok.sem, ctx_ok(i, CT))
                    pe.wait_ge(pT0_ok.sem, pT0_ok(j, 1))
                    one_column(6)
                at = slice(32 * q, 32 * q + 32)
                for c in range(32):
                    ins = pe.matmul(ps[at, 6 + c // 16, 32 * (c % 16):32 * (c % 16) + 32],
                                    pT0[at, c, :], vT0[at, :, c], start=True, stop=True)
                if q == Q4 - 1:
                    ins.then_inc(av0.sem, 1)

            def wr(i, j, ct):
                if ct == 0:
                    pe.wait_ge(yc0_ok.sem, yc0_ok(j, 1))
                    if i is not None:
                        pe.wait_ge(qc_ok.sem, qc_ok(i, 4))
                else:
                    pe.wait_ge(res0.sem, res0(j, 1))
                both_halves([wr0[:, ct * P:(ct + 1) * P]], [yc0[:, :, :].rearrange("p h w -> p (h w)")], wr_mm)

            def qk1(b, i, g, part):
                k = 2 * g + part
                if part == 0 and g == 0:
                    pe.wait_ge(xn1_ok.sem, xn1_ok(b, 2))
                    if i is not None:
                        pe.wait_ge(o2_ok.sem, o2_ok(i, 2))
                elif part == 0:
                    pe.wait_ge(v1_ok.sem, v1_ok(b, 2))
                    if i is not None:
                        pe.wait_ge(o3_ok.sem, o3_ok(i, 0))
                for hf in range(2):
                    if part == 1:
                        pe.wait_ge(lo1_ok.sem, lo1_ok(b, 2 * (k - 1) + hf + 1))
                    if part == 1 and hf == 1 and g == 0 and i is not None:
                        pe.wait_ge(gn_v[2].sem, gn_v[2](i, 6))
                    product(ps[:, 6 + hf, :], [(wqk1[:, kt, k * P:(k + 1) * P], xn1[:, kt, hf * HALF:(hf + 1) * HALF])
                                               for kt in range(CT)]).then_inc(qk1_mm.sem, 1)

            def v1(b, i, g):
                if g == 1 and i is not None:
                    pe.wait_ge(x2_ok.sem, x2_ok(i, 2))
                for t in range(NT):
                    if t % 4 == 0:
                        pe.wait_ge(lo1_ok.sem, lo1_ok(b, 2 * (2 * g + 1) + t // 4 + 1))
                    ins = product(ps[:, 6 + t // 4, (t % 4) * P:(t % 4 + 1) * P],
                                  [(xn1[:, kt, t * P:(t + 1) * P], wv1[:, kt, g * P:(g + 1) * P]) for kt in range(CT)])
                ins.then_inc(v1_mm.sem, 1)

            def proj(b, i, ct):
                if ct == 0:
                    if b is not None:
                        pe.wait_ge(lo1_ok.sem, lo1_ok(b, 8))
                    else:
                        pe.wait_ge(o3_ok.sem, o3_ok(i, 0))
                    pe.wait_ge(att_ok.sem, att_ok(i, UNITS))
                else:
                    pe.wait_ge(x2_ok.sem, x2_ok(i, 1))
                both_halves([wp1[:, kt, ct * P:(ct + 1) * P] for kt in range(CT)], channel_tiles(att1), proj_mm)

            def kv(i, m):
                if m == 0:
                    pe.wait_ge(xn2_ok.sem, xn2_ok(i, 2))
                for t in (2 * m, 2 * m + 1):
                    if t >= 2:
                        pe.wait_ge(kv_ok.sem, kv_ok(i, 2 * (t - 1)))
                    product(ps[:, 6 + t % 2, :],
                            [(xn2[:, kt, t * P:(t + 1) * P], wkv2[:, kt, :]) for kt in range(CT)]).then_inc(kv_mm.sem, 1)

            def maxima_turned(i):
                pe.wait_ge(cmx_ok.sem, cmx_ok(i, CT))
                for ct in range(CT):
                    ins = pe.transpose(ps[:, 6, ct * P:(ct + 1) * P], cmx[:, ct * P:(ct + 1) * P], ident[:, :])
                ins.then_inc(cmt_mm.sem, 1)

            def maxima_spread(i):
                pe.wait_ge(cmc_ok.sem, cmc_ok(i, 1))
                for ct in range(CT):
                    ins = pe.matmul(ps[:, 7, ct * P:(ct + 1) * P], cmc[:, ct:ct + 1].to_broadcast([P, P]),
                                    ident[:, :], start=True, stop=True)
                ins.then_inc(cmb_mm.sem, 1)

            def context(i, j, ct):
                if ct == 0:
                    pe.wait_ge(ke_ok.sem, ke_ok(i, 2))
                    if j is not None:
                        pe.wait_ge(sub0.sem, sub0(j, 1))
                product(ps[:, 6 + ct, 0:C + 1],
                        [(k2[:, t, ct * P:(ct + 1) * P], v2[:, t, :]) for t in range(NT)]).then_inc(ctx_mm.sem, 1)

            def q_turned(i, j, m):
                if m == 0:
                    pe.wait_ge(qn_ok.sem, qn_ok(i, NT))
                    if j is not None:
                        pe.wait_ge(y0_ok.sem, y0_ok(j, 1))
                    else:
                        pe.wait_ge(ctx_ok.sem, ctx_ok(i, CT))
                for hf in range(2):
                    if m == 1:
                        pe.wait_ge(qc_ok.sem, qc_ok(i, 1 + hf))
                    for t in range(4):
                        ins = pe.transpose(ps[:, 6 + hf, t * P:(t + 1) * P], qe[:, 4 * hf + t, m * P:(m + 1) * P],
                                           ident[:, :])
                    ins.then_inc(qt_mm.sem, 1)

            def o2_product(i, j, ct):
                if ct == 0:
                    pe.wait_ge(qc_ok.sem, qc_ok(i, 4))
                    if j is not None:
                        pe.wait_ge(res0.sem, res0(j, 2))
                else:
                    pe.wait_ge(o2_ok.sem, o2_ok(i, 1))
                both_halves([ctx2[:, kt, ct * P:(ct + 1) * P] for kt in range(CT)], channel_tiles(qc), o2_mm)

            def z_product(i, j, m):
                if m == 0:
                    pe.wait_ge(g2_ok.sem, g2_ok(i, 2))
                    if j is not None:
                        pe.wait_ge(v1_ok.sem, v1_ok(j, 2))
                if m >= 2:
                    pe.wait_ge(z_ok.sem, z_ok(i, m - 1))
                for s in range(2):
                    at = slice((2 * m + s) * P, (2 * m + s + 1) * P)
                    for kt in range(CT):
                        pe.matmul(ps[:, 6 + m % 2, s * C:(s + 1) * C], o2[:, kt, at], wo2[:, kt, :],
                                  start=(kt == 0 and s == 0), stop=False, skip_group_check=True)
                    for kt in range(CT):
                        ins = pe.matmul(ps[:, 6 + m % 2, s * C + kt * P:s * C + (kt + 1) * P], xn2[:, kt, at],
                                        ident[:, :], start=False, stop=True, skip_group_check=True)
                ins.then_inc(z_mm.sem, 1)

            def up(i, f):
                ct = f // 8
                if f == 0:
                    pe.wait_ge(z_ok.sem, z_ok(i, 4))
                elif f == 8:
                    pe.wait_ge(o3_ok.sem, o3_ok(i, 1))
                elif f != 1 and f != 9:
                    pe.wait_ge(up_ok.sem, up_ok(i, f - 1))
                for m in range(4):
                    t = 4 * (f % 8) + m
                    tiles = [(t // 4 + d, 3 * (t % 4) + d + 1) for d in (-1, 0, 1)
                             if 0 <= t // 4 + d < NT and t - REACH < 4 * (t // 4 + d) + 4 and t + REACH >= 4 * (t // 4 + d)]
                    ins = product(ps[:, 6 + f % 2, m * P:(m + 1) * P],
                                  [(up_m[:, k, :], z3[:, s, ct * P:(ct + 1) * P]) for s, k in tiles])
                ins.then_inc(up_mm.sem, 1)

            def down(i, ct, part):
                if part == 0:
                    pe.wait_ge(up_ok.sem, up_ok(i, 8 * ct + 8))
                for t in range(8 * part, 8 * part + 8):
                    lo, hi = max(t - REACH, 0), min(t + REACH + 1, H)
                    for bank in range(2):
                        r, e = max(lo, 16 * bank), min(hi, 16 * bank + 16)
                        if r >= e:
                            continue
                        at = (r - (t - REACH)) * W
                        ins = pe.matmul(ps[:, 6 + bank, (r - 16 * bank) * W:(e - 16 * bank) * W],
                                        up3[:, t, :], dn_m[:, at:at + (e - r) * W],
                                        start=(t == (0, 16 - REACH)[bank]), stop=(t == (15 + REACH, UPT - 1)[bank]),
                                        skip_group_check=True)
                if part == 3:
                    ins.then_inc(dn_mm.sem, 1)

            def side(name, b, i, j):
                digit = int(name[-1]) if name[-1].isdigit() else None
                if name in ("l0q", "l0k", "l0v"):
                    qkv0(b, i, j, "qkv".index(name[2]))
                elif name.startswith("corr"):
                    scores0(i, j, digit)
                elif name.startswith("av"):
                    values0(i, j, digit)
                elif name in ("wr0", "wr1"):
                    wr(i, j, digit)
                elif name == "norm1a":
                    if i is not None:
                        pe.wait_ge(o2_ok.sem, o2_ok(i, 2))
                    average(0, j, avg8)
                elif name in ("q0", "k0"):
                    qk1(j, i, 0, int(name == "k0"))
                elif name in ("q1", "k1"):
                    qk1(b, i, 1, int(name == "k1"))
                elif name == "v0":
                    v1(j, i, 0)
                elif name == "v1":
                    v1(b, i, 1)
                elif name in ("proj0", "proj1"):
                    proj(b, i, digit)
                elif name == "norm2a":
                    if b is not None:
                        pe.wait_ge(v1_ok.sem, v1_ok(b, 4))
                    average(1, i, avg16)
                elif name == "norm3a":
                    if j is not None:
                        pe.wait_ge(lo1_ok.sem, lo1_ok(j, 2))
                    average(2, i, avg16)
                elif name.startswith("kv"):
                    kv(i, digit)
                elif name == "kmaxT":
                    maxima_turned(i)
                elif name == "spread":
                    maxima_spread(i)
                elif name in ("context0", "context1"):
                    context(i, j, digit)
                elif name in ("qT0", "qT1"):
                    q_turned(i, j, digit)
                elif name in ("o20", "o21"):
                    o2_product(i, j, digit)
                elif name.startswith("z"):
                    z_product(i, j, digit)
                elif name.startswith("up"):
                    up(i, int(name[2:]))
                elif name.startswith("dn"):
                    down(i, int(name[2]), digit)

            def first():
                for name in FIRST:
                    side(name, None, None, 0)
                for m in range(NT):
                    max_products(0, m, 0)
                    max_products(0, m, 1)
                turn(0, 0)
                pe.wait_ge(row_ok.sem, row_ok(0, 2))
                for m in range(NT, NT + LEAD):
                    max_products(0, m, 0)
                    max_products(0, m, 1)

            def period(b, i, j):
                for n in range(STEPS):
                    b, i, j = copied(pe, n, b, i, j)
                    for pair in range(2):
                        logits(b, n, pair, i)
                        t = turn_at(n)
                        if pair == 0 and t is not None:
                            turn(b, t, t < UNITS or j is not None)
                        m = n + NT + LEAD
                        if m < STEPS:
                            max_products(b, m, pair)
                        elif j is not None:
                            max_products(j, m - STEPS, pair, b)
                        if pair == 0 and (n or i is not None):
                            of, before = (b, n - 1) if n else (i, STEPS - 1)
                            values(of, before, i)
                        for name in beside(2 * n + pair, i, j):
                            side(name, b, i, j)
                        if pair == 0 and t is not None:
                            spread(b, t)

            def last(i):
                values(i, STEPS - 1)
                for names in SIDE.values():
                    for name in names:
                        if not name.startswith(OF_B + OF_J):
                            side(name, None, i, None)

            periods(pe, first, period, last)


def kernel(x, **w):
    import numpy as np
    import concourse.bacc as bacc
    from concourse.bass_utils import run_bass_kernel_spmd

    def tiles(a):
        a = np.asarray(a)
        return np.ascontiguousarray(a.reshape(-1, P, a.shape[-1]).transpose(1, 0, 2))

    def toeplitz(taps, index):
        padded = np.concatenate([np.asarray(taps)[::-1], np.zeros(1, np.float32)])
        return padded[np.where((index >= 0) & (index < TAPS), index, TAPS)]

    a = {k: np.asarray(v) for k, v in w.items()}
    x = np.asarray(x)
    L0, L1, L2, L3 = "L0_conv_", "L1_conv_", "L2_conv_", "L3_conv_"
    arrays = {"x": np.ascontiguousarray(x.reshape(B, C, N))}
    arrays["wq0"] = tiles(np.concatenate([a[L0 + "Wq"], a[L0 + "Wk"], a[L0 + "Wv"]]).T)
    arrays["wr0"] = np.ascontiguousarray(a[L0 + "Wr"].T)
    qkv = a[L1 + "w_qkv"].reshape(GROUPS4, Q4, 3, DH, C)
    arrays["wqk1"] = tiles(qkv[:, :, 0:2].transpose(0, 2, 1, 3, 4).reshape(4 * P, C).T)
    arrays["wv1"] = tiles(qkv[:, :, 2].reshape(C, C).T)
    arrays["wp1"] = tiles(a[L1 + "w_proj"].T)
    arrays["wkv2"] = tiles(a[L2 + "kv_w"].T)
    arrays["wo2"] = tiles(a[L2 + "out_w"].T)
    b_qkv = a[L1 + "b_qkv"].reshape(GROUPS4, Q4, 3, DH)
    vectors = {"bq": a[L0 + "bq"], "bk": a[L0 + "bk"], "bv": a[L0 + "bv"], "br": a[L0 + "br"],
               "gamma": a[L0 + "gamma"], "beta": a[L0 + "beta"], "mean": a[L0 + "running_mean"],
               "var": a[L0 + "running_var"], "gn1_scale": a[L1 + "gn_scale"], "gn1_bias": a[L1 + "gn_bias"],
               "b_qk": b_qkv[:, :, 0:2].transpose(0, 2, 1, 3).reshape(-1), "b_proj": a[L1 + "b_proj"],
               "gn2_scale": a[L2 + "norm1_w"], "gn2_bias": a[L2 + "norm1_b"],
               "gn3_scale": a[L2 + "norm2_w"], "gn3_bias": a[L2 + "norm2_b"]}
    arrays["vectors"] = np.ascontiguousarray(np.concatenate([vectors[k].reshape(-1, P) for k in VEC]).T)
    row = np.concatenate([b_qkv[:, :, 2].reshape(-1), a[L2 + "kv_b"], a[L2 + "out_b"], a[L3 + "bias"]])
    arrays["rows"] = np.ascontiguousarray(np.broadcast_to(row, (P, row.size)))

    lane = np.arange(P)
    h4, w4 = lane // W, lane % W
    r, d, e = (i.reshape(-1) for i in np.meshgrid(np.arange(4), np.arange(-1, 2), np.arange(2), indexing="ij"))
    up = a[L3 + "up_filter"]
    arrays["up_h"] = toeplitz(up, 2 * (4 * d[None] + h4[:, None]) - (2 * r + e)[None] + 6)
    arrays["up_w"] = toeplitz(up, 2 * w4[:, None] - np.arange(UPH)[None] + 6)
    down = a[L3 + "down_filter"]
    e2, w2 = lane // UPH, lane % UPH
    arrays["dn_h"] = toeplitz(down, e2[:, None] - 2 * np.arange(WIN)[None] + 11)
    arrays["dn_w"] = toeplitz(down, w2[:, None] - 2 * np.arange(W)[None] + 5)

    arrays["ident"] = np.eye(P, dtype=np.float32)
    arrays["pick"] = np.zeros((2, Q4, 4, 4, Q4, DH), np.float32)
    for h in range(Q4):
        for t in range(4):
            arrays["pick"][1, h, t, t, h] = 1.0
    arrays["pick"] = arrays["pick"].reshape(8 * Q4, 4, P)
    for name, size in (("avg8", 8), ("avg16", 16)):
        arrays[name] = np.kron(np.eye(P // size), np.full((size, size), 1.0 / size)).astype(np.float32)

    nc = bacc.Bacc("TRN2", target_bir_lowering=False, num_devices=1)
    ap = {k: nc.dram_tensor("in_" + k, t.shape, mybir.dt.from_np(t.dtype), kind="ExternalInput").ap()
          for k, t in arrays.items()}
    out = nc.dram_tensor("out", (B, C, N), F32, kind="ExternalOutput").ap()
    chain_kernel(nc, ap["x"], ap, ap["vectors"], ap["rows"], ap, ap, out)
    got = run_bass_kernel_spmd(nc, [{"in_" + k: t for k, t in arrays.items()}], core_ids=[0])
    return got.results[0]["out"].reshape(B, C, H, W)
```
